# Optimizing a Trainium2 kernel written in Bass

```python
import numpy as np
import jax
import jax.numpy as jnp

def _softmax(x, axis=-1):
    return jax.nn.softmax(x, axis=axis)

def _gelu(x):
    return jax.nn.gelu(x, approximate=True)

def _silu(x):
    return jax.nn.silu(x)

def _sigmoid(x):
    return jax.nn.sigmoid(x)

def _layernorm(x, axis=-1, eps=1e-05):
    m = jnp.mean(x, axis=axis, keepdims=True)
    v = jnp.var(x, axis=axis, keepdims=True)
    return (x - m) / jnp.sqrt(v + eps)

def _scatter_add(tgt, idx, src, axis=0):
    return tgt.at[idx].add(src)

def _segment_sum(src, seg, n):
    return jax.ops.segment_sum(src, seg, n)
kernel_name = 'mk_sandwich_d1_jaxref_r4_2e3101'

def setup_inputs(seed: int=0):
    np.random.seed(seed)
    _w = jnp.asarray

    def _L0_attn_setup():
        import math
        import jax, jax.numpy as jnp
        import numpy as np
        B, T, E = (2, 512, 1024)
        H, HKV = (32, 8)
        DH = E // H
        G = H // HKV
        ROPE_THETA = 500000.0
        ROPE_FACTOR = 32.0
        HI_FREQ_FACTOR = 4.0
        LO_FREQ_FACTOR = 1.0
        ORIG_CTX = 2048

        def _rope_cos_sin(t_len):
            inv_freq = 1.0 / ROPE_THETA ** (jnp.arange(0, DH, 2, dtype=jnp.float32) / DH)
            wavelen = 2.0 * math.pi / inv_freq
            cut_lo = ORIG_CTX / HI_FREQ_FACTOR
            cut_hi = ORIG_CTX / LO_FREQ_FACTOR
            inv_freq = jnp.where(wavelen > cut_hi, inv_freq / ROPE_FACTOR, inv_freq)
            smooth = (ORIG_CTX / wavelen - LO_FREQ_FACTOR) / (HI_FREQ_FACTOR - LO_FREQ_FACTOR)
            smoothed = (1.0 - smooth) * inv_freq / ROPE_FACTOR + smooth * inv_freq
            is_medium = ~(wavelen < cut_hi) & ~(wavelen > cut_lo)
            inv_freq = jnp.where(is_medium, smoothed, inv_freq)
            pos = jnp.arange(t_len, dtype=jnp.float32)
            freqs = pos[:, None] * inv_freq[None, :]
            emb = jnp.concatenate([freqs, freqs], axis=-1)
            return (jnp.cos(emb), jnp.sin(emb))

        def _rotate_half(x):
            x1, x2 = jnp.split(x, 2, axis=-1)
            return jnp.concatenate([-x2, x1], axis=-1)
        key = jax.random.key(seed)
        kx, kq, kk, kv, ko = jax.random.split(key, 5)
        w = lambda k, shape: jax.random.normal(k, shape, jnp.float32) * 0.02
        return {'x': jax.random.normal(kx, (B, T, E), jnp.float32), 'Wq': w(kq, (E, E)), 'Wk': w(kk, (HKV * DH, E)), 'Wv': w(kv, (HKV * DH, E)), 'Wo': w(ko, (E, E))}
    _L0_attn_in = _L0_attn_setup()

    def _L0_ffn_setup():
        import jax, jax.numpy as jnp
        import numpy as np
        GROUP = 64

        def dequantize(W_q, scale, zero):
            out, half = W_q.shape
            hi = W_q >> 4 & 15
            lo = W_q & 15
            w = jnp.stack([hi, lo], axis=-1).reshape(out, half * 2).astype(scale.dtype)
            w = w.reshape(out, -1, GROUP)
            w = (w - zero[:, :, None]) * scale[:, :, None]
            return w.reshape(out, half * 2)
        key = jax.random.key(seed)
        ks = jax.random.split(key, 10)
        hidden, inter = (1024, 2752)
        B, S = (4, 256)
        x = jax.random.normal(ks[0], (B, S, hidden), dtype=jnp.float32)
        gate_Wq = jax.random.randint(ks[1], (inter, hidden // 2), 0, 64, dtype=jnp.int32)
        up_Wq = jax.random.randint(ks[2], (inter, hidden // 2), 0, 64, dtype=jnp.int32)
        down_Wq = jax.random.randint(ks[3], (hidden, inter // 2), 0, 64, dtype=jnp.int32)
        gate_scale = jax.random.uniform(ks[4], (inter, hidden // GROUP)) * 0.01 + 0.0001
        gate_zero = jax.random.uniform(ks[5], (inter, hidden // GROUP)) * 15.0
        up_scale = jax.random.uniform(ks[6], (inter, hidden // GROUP)) * 0.01 + 0.0001
        up_zero = jax.random.uniform(ks[7], (inter, hidden // GROUP)) * 15.0
        down_scale = jax.random.uniform(ks[8], (hidden, inter // GROUP)) * 0.01 + 0.0001
        down_zero = jax.random.uniform(ks[9], (hidden, inter // GROUP)) * 15.0
        return {'x': x, 'gate_Wq': gate_Wq, 'up_Wq': up_Wq, 'down_Wq': down_Wq, 'gate_scale': gate_scale, 'gate_zero': gate_zero, 'up_scale': up_scale, 'up_zero': up_zero, 'down_scale': down_scale, 'down_zero': down_zero}
    _L0_ffn_in = _L0_ffn_setup()
    _d = {'L0_attn_x': _L0_attn_in['x'], 'L0_attn_Wq': _L0_attn_in['Wq'], 'L0_attn_Wk': _L0_attn_in['Wk'], 'L0_attn_Wv': _L0_attn_in['Wv'], 'L0_attn_Wo': _L0_attn_in['Wo'], 'L0_ffn_gate_Wq': _L0_ffn_in['gate_Wq'], 'L0_ffn_up_Wq': _L0_ffn_in['up_Wq'], 'L0_ffn_down_Wq': _L0_ffn_in['down_Wq'], 'L0_ffn_gate_scale': _L0_ffn_in['gate_scale'], 'L0_ffn_gate_zero': _L0_ffn_in['gate_zero'], 'L0_ffn_up_scale': _L0_ffn_in['up_scale'], 'L0_ffn_up_zero': _L0_ffn_in['up_zero'], 'L0_ffn_down_scale': _L0_ffn_in['down_scale'], 'L0_ffn_down_zero': _L0_ffn_in['down_zero']}
    _x0 = _d['L0_attn_x']
    _d['L0_attn_x'] = jax.random.normal(jax.random.fold_in(jax.random.key(seed), 1), (2, 1024, 1024), dtype=_x0.dtype)
    del _x0
    return _d

def reference(L0_attn_x, L0_attn_Wq, L0_attn_Wk, L0_attn_Wv, L0_attn_Wo, L0_ffn_gate_Wq, L0_ffn_up_Wq, L0_ffn_down_Wq, L0_ffn_gate_scale, L0_ffn_gate_zero, L0_ffn_up_scale, L0_ffn_up_zero, L0_ffn_down_scale, L0_ffn_down_zero):

    def _L0_attn_ref(x, Wq, Wk, Wv, Wo):
        import math
        import jax, jax.numpy as jnp
        import numpy as np
        B, T, E = (2, 512, 1024)
        H, HKV = (32, 8)
        DH = E // H
        G = H // HKV
        ROPE_THETA = 500000.0
        ROPE_FACTOR = 32.0
        HI_FREQ_FACTOR = 4.0
        LO_FREQ_FACTOR = 1.0
        ORIG_CTX = 2048

        def _rope_cos_sin(t_len):
            inv_freq = 1.0 / ROPE_THETA ** (jnp.arange(0, DH, 2, dtype=jnp.float32) / DH)
            wavelen = 2.0 * math.pi / inv_freq
            cut_lo = ORIG_CTX / HI_FREQ_FACTOR
            cut_hi = ORIG_CTX / LO_FREQ_FACTOR
            inv_freq = jnp.where(wavelen > cut_hi, inv_freq / ROPE_FACTOR, inv_freq)
            smooth = (ORIG_CTX / wavelen - LO_FREQ_FACTOR) / (HI_FREQ_FACTOR - LO_FREQ_FACTOR)
            smoothed = (1.0 - smooth) * inv_freq / ROPE_FACTOR + smooth * inv_freq
            is_medium = ~(wavelen < cut_hi) & ~(wavelen > cut_lo)
            inv_freq = jnp.where(is_medium, smoothed, inv_freq)
            pos = jnp.arange(t_len, dtype=jnp.float32)
            freqs = pos[:, None] * inv_freq[None, :]
            emb = jnp.concatenate([freqs, freqs], axis=-1)
            return (jnp.cos(emb), jnp.sin(emb))

        def _rotate_half(x):
            x1, x2 = jnp.split(x, 2, axis=-1)
            return jnp.concatenate([-x2, x1], axis=-1)
        b, t, _ = x.shape
        q = (x @ Wq.T).reshape(b, t, H, DH).transpose(0, 2, 1, 3)
        k = (x @ Wk.T).reshape(b, t, HKV, DH).transpose(0, 2, 1, 3)
        v = (x @ Wv.T).reshape(b, t, HKV, DH).transpose(0, 2, 1, 3)
        cos, sin = _rope_cos_sin(t)
        cos = cos.astype(x.dtype)[None, None]
        sin = sin.astype(x.dtype)[None, None]
        q = q * cos + _rotate_half(q) * sin
        k = k * cos + _rotate_half(k) * sin
        qg = q.reshape(b, HKV, G, t, DH)
        scores = jnp.einsum('bhgtd,bhkd->bhgtk', qg.astype(jnp.float32), k.astype(jnp.float32)) / math.sqrt(DH)
        causal = jnp.tril(jnp.ones((t, t), dtype=bool))
        scores = jnp.where(causal[None, None, None], scores, jnp.finfo(jnp.float32).min)
        attn = jax.nn.softmax(scores, axis=-1).astype(x.dtype)
        ctx = jnp.einsum('bhgtk,bhkd->bhgtd', attn, v)
        out = ctx.reshape(b, H, t, DH).transpose(0, 2, 1, 3).reshape(b, t, E)
        return out @ Wo.T

    def _L0_ffn_ref(x, gate_Wq, up_Wq, down_Wq, gate_scale, gate_zero, up_scale, up_zero, down_scale, down_zero):
        import jax, jax.numpy as jnp
        import numpy as np
        GROUP = 64

        def dequantize(W_q, scale, zero):
            out, half = W_q.shape
            hi = W_q >> 4 & 15
            lo = W_q & 15
            w = jnp.stack([hi, lo], axis=-1).reshape(out, half * 2).astype(scale.dtype)
            w = w.reshape(out, -1, GROUP)
            w = (w - zero[:, :, None]) * scale[:, :, None]
            return w.reshape(out, half * 2)
        Wg = dequantize(gate_Wq, gate_scale, gate_zero)
        Wu = dequantize(up_Wq, up_scale, up_zero)
        Wd = dequantize(down_Wq, down_scale, down_zero)
        g = jnp.einsum('bsh,ih->bsi', x, Wg)
        u = jnp.einsum('bsh,ih->bsi', x, Wu)
        h = jax.nn.silu(g) * u
        return jnp.einsum('bsi,hi->bsh', h, Wd)
    x = L0_attn_x
    x = x + _layernorm(_L0_attn_ref(_layernorm(x, axis=-1), L0_attn_Wq, L0_attn_Wk, L0_attn_Wv, L0_attn_Wo), axis=-1)
    x = x + _layernorm(_L0_ffn_ref(_layernorm(x, axis=-1), L0_ffn_gate_Wq, L0_ffn_up_Wq, L0_ffn_down_Wq, L0_ffn_gate_scale, L0_ffn_gate_zero, L0_ffn_up_scale, L0_ffn_up_zero, L0_ffn_down_scale, L0_ffn_down_zero), axis=-1)
    return x

_drawn_inputs = setup_inputs


def setup_inputs(seed=0):
    import zlib

    import numpy as np

    out = dict(_drawn_inputs(seed))
    spreads = {}
    factors = {}
    for name, (base, spread) in spreads.items():
        noise = np.random.default_rng([zlib.crc32(name.encode()), seed]).standard_normal(out[name].shape)
        drawn = base * np.exp(spread * noise) if base else spread * noise
        out[name] = jnp.asarray(drawn.astype(out[name].dtype))
    for name, factor in factors.items():
        out[name] = (out[name] * factor).astype(out[name].dtype)
    return out
```

```python
import numpy as np
import concourse.bass as bass
from concourse import mybir
from contextlib import ExitStack

F32 = mybir.dt.float32
F16 = mybir.dt.float16
BF16 = mybir.dt.bfloat16
I32 = mybir.dt.int32
ACT = mybir.ActivationFunctionType
ALU = mybir.AluOpType
AX = mybir.AxisListType

P = 128
BATCH, T, E = 2, 1024, 1024
TOK = BATCH * T
NT = TOK // P
NC = E // P
HEADS, KVH, DH = 32, 8, 32
GQ = HEADS // KVH
UT = T // P
QW = GQ * P
WCOL = (GQ + 2) * DH
INTER = 2752
GROUPS, GROUP_I = INTER // 256, 256
LASTW = (INTER - GROUPS * GROUP_I) // 2
EPS = 1e-5
XS = 1024.0
QS = 2.0 ** -24
MS = 2.0 ** 15
PS_LOG = 14 * float(np.log(2.0))
HS = 2.0 ** -45
SQ, SK, SV, SO, SG, SU, SD = range(7)
MASKED = -3.0e38


def wait(eng, sem, value):
    if isinstance(value, int) and value <= 0:
        return
    eng.wait_ge(sem, value)


def apart(eng, sem):
    eng.sem_inc(sem, 1)


def loop(eng, first, last, body):
    body(first)
    if last - first > 1:
        with eng.Fori(first + 1, last) as r:
            body(r)
    body(last)


def phase_scales_and_norm(nc, K, x, wqkv, wo, szs):
    with ExitStack() as ctx:
        sb = lambda n, s, d: ctx.enter_context(nc.sbuf_tensor(n, s, d))
        sem = lambda n: ctx.enter_context(nc.semaphore(n))
        wtmp = sb("a_wtmp", [P, 2, 2048], F32)
        ztmp = sb("a_ztmp", [P, 6, 344], F32)
        zab = sb("a_zab", [P, 344], F32)
        part = sb("a_part", [P, 4, 8], F32)
        own = sb("a_own", [P, 8], F32)
        allm = sb("a_allm", [P, 8], F32)
        ebits = sb("a_ebits", [P, 8], I32)
        tmp1 = sb("a_tmp1", [P, 1], F32)
        tmp2 = sb("a_tmp2", [P, 1], F32)
        xin = sb("a_xin", [P, 2, E], F32)
        xn = sb("a_xn", [P, 2, E], F32)
        xhl = sb("a_xhl", [P, 2, 2, E], F16)
        st6 = sb("a_st6", [P, 2, 2, 6], F32)
        mv = sb("a_mv", [P, 2, 2], F32)
        ve = sb("a_ve", [P, 2], F32)
        sd = sb("a_sd", [P, 2], F32)
        rs = sb("a_rs", [P, 2], F32)
        pt = [[ctx.enter_context(nc.psum_tensor(f"a_pt{s}{h}", [P, NC, P], F16)) for h in range(2)]
              for s in range(2)]
        w_in = [sem("a_w_in0"), sem("a_w_in1")]
        w_used = sem("a_w_used")
        z_in = sem("a_z_in")
        x_in = [sem("a_x_in0"), sem("a_x_in1")]
        s_const = sem("a_const")
        s_bound = sem("a_bound")
        s_allmax = sem("a_allmax")
        s_chain = sem("a_chain")
        s_stats = sem("a_stats")
        s_apart = sem("a_apart")
        s_var = sem("a_var")
        s_std = sem("a_std")
        s_rstd = sem("a_rstd")
        s_xn = sem("a_xn_done")
        s_hi = sem("a_hi")
        s_lo = sem("a_lo")
        s_tr = sem("a_tr")
        s_ev_hi = sem("a_ev_hi")
        s_ev_lo = sem("a_ev_lo")
        xv = x.rearrange("(n p) e -> n p e", p=P)
        block = ctx.enter_context(nc.Block())

        @block.sync
        def _(sp):
            def load_x(n, k):
                wait(sp, s_xn, n - 1)
                sp.dma_start(xin[:, k, :], xv[bass.ds(n, 1)].rearrange("a p e -> p (a e)")).then_inc(x_in[k], 16)

            load_x(0, 0)
            load_x(1, 1)
            for i, sz in enumerate(szs):
                sp.dma_start(ztmp[:, i, :], sz).then_inc(z_in, 16)
            for i in range(12):
                wait(sp, w_used, i - 1)
                src = wqkv[i].rearrange("p c n -> p (c n)") if i < 8 else wo[:, bass.ts(i - 8, 2048)]
                dst = wtmp[:, i % 2, 0:NC * WCOL] if i < 8 else wtmp[:, i % 2, :]
                sp.dma_start(dst, src).then_inc(w_in[i % 2], 16)
            with sp.Fori(1, NT // 2) as r:
                load_x(r * 2, 0)
                load_x(r * 2 + 1, 1)

        @block.gpsimd
        def _(pool):
            nc.gpsimd.memset(K.ident[:], 0.0).then_inc(s_const, 1)
            nc.gpsimd.memset(K.identb[:], 0.0).then_inc(s_const, 1)
            nc.gpsimd.memset(K.maskb[:], 0.0).then_inc(s_const, 1)
            nc.gpsimd.memset(K.ln_ps[:], PS_LOG)
            pool.wait_ge(s_const, 3)
            for m in (K.ident, K.identb):
                nc.gpsimd.affine_select(out=m[:], in_=m[:], compare_op=ALU.not_equal, fill=1.0, base=0,
                                        pattern=[[-1, P]], channel_multiplier=1).then_inc(s_const, 1)
            nc.gpsimd.affine_select(out=K.maskb[:], in_=K.maskb[:], compare_op=ALU.is_ge, fill=MASKED, base=0,
                                    pattern=[[-1, P]], channel_multiplier=1).then_inc(s_const, 1)
            pool.wait_ge(s_bound, 1)
            nc.gpsimd.partition_all_reduce(allm[:, 0:7], own[:, 0:7], P, bass.bass_isa.ReduceOp.max)\
                .then_inc(s_allmax, 1)

        @block.vector
        def _(dve):
            links = [0]

            def link(ins):
                links[0] += 1
                ins.then_inc(s_chain, 1)
                dve.wait_ge(s_chain, links[0])

            def norm(n, k, half):
                wait(dve, x_in[k], (half + 1) * 16)
                wait(dve, s_rstd, n)
                for h in range(2):
                    nc.vector.bn_stats(st6[:, k, h, :], xin[:, k, h * 512:(h + 1) * 512]).then_inc(s_stats, 1)
                dve.wait_ge(s_stats, n * 3 + 2)
                apart(dve, s_apart)
                nc.vector.bn_aggr(mv[:, k, :], st6[:, k, :, :]).then_inc(s_stats, 1)
                dve.wait_ge(s_stats, n * 3 + 3)
                nc.vector.tensor_scalar(ve[:, k:k + 1], mv[:, k, 1:2], EPS, None, ALU.add).then_inc(s_var, 1)
                dve.wait_ge(s_std, n + 1)
                nc.vector.reciprocal(rs[:, k:k + 1], sd[:, k:k + 1]).then_inc(s_rstd, 1)
                dve.wait_ge(s_rstd, n + 1)
                wait(dve, s_hi, n - 1)
                wait(dve, s_lo, n - 1)
                nc.vector.tensor_scalar(xn[:, k, :], xin[:, k, :], mv[:, k, 0:1], rs[:, k:k + 1],
                                        ALU.subtract, ALU.mult).then_inc(s_xn, 1)
                dve.wait_ge(s_hi, n + 1)
                nc.vector.tensor_tensor(xhl[:, k, 1, :], xn[:, k, :], xhl[:, k, 0, :], ALU.subtract)\
                    .then_inc(s_lo, 1)
                dve.wait_ge(s_tr, n * 2 + 2)
                nc.vector.tensor_copy(K.xT[:, 1, :, bass.ds(n * P, P)], pt[k][1][:]).then_inc(s_ev_lo, 1)

            for i in range(12):
                dve.wait_ge(w_in[i % 2], 16 * (i // 2 + 1))
                if i < 8:
                    w = wtmp[:, i % 2, 0:NC * WCOL].rearrange("p (c n) -> p c n", c=NC)
                    for m, (a, b) in enumerate(((0, P), (P, P + DH), (P + DH, WCOL))):
                        last = nc.vector.tensor_reduce(part[:, m, i:i + 1], w[:, :, a:b], AX.XY, ALU.max,
                                                       apply_absolute_value=True)
                else:
                    last = nc.vector.tensor_reduce(part[:, 3, i - 8:i - 7], wtmp[:, i % 2, :], AX.X, ALU.max,
                                                   apply_absolute_value=True)
                last.then_inc(w_used, 1)
            dve.wait_ge(w_used, 12)
            for m, n in ((0, 8), (1, 8), (2, 8), (3, 4)):
                nc.vector.tensor_reduce(own[:, m:m + 1], part[:, m, 0:n], AX.X, ALU.max)
            dve.wait_ge(z_in, 96)
            for m in range(3):
                zero = ztmp[:, 2 * m + 1, :]
                link(nc.vector.scalar_tensor_tensor(zab[:], zero, -1.0, zero, ALU.mult, ALU.max))
                link(nc.vector.scalar_tensor_tensor(zab[:], zab[:], 15.0, ztmp[:, 2 * m, :], ALU.add, ALU.mult))
                link(nc.vector.tensor_reduce(own[:, 4 + m:5 + m], zab[:], AX.X, ALU.max,
                                             apply_absolute_value=True))
            nc.vector.tensor_scalar(tmp1[:], zab[:, 0:1], 0.0, None, ALU.mult).then_inc(s_bound, 1)
            dve.wait_ge(s_allmax, 1)
            link(nc.vector.tensor_scalar(ebits[:, 0:7], allm[:, 0:7].bitcast(I32), 0x7F800000, None,
                                         ALU.bitwise_and))
            link(nc.vector.tensor_scalar(ebits[:, 0:7], ebits[:, 0:7], float(27 << 23), None, ALU.max))
            link(nc.vector.tensor_scalar(K.sc[:, 0:7].bitcast(I32), ebits[:, 0:7], -1.0, float(268 << 23),
                                         ALU.mult, ALU.add))
            link(nc.vector.tensor_scalar(K.inv[:, 0:7].bitcast(I32), ebits[:, 0:7], float(14 << 23), None,
                                         ALU.subtract))

            def product(out, a, ca, b, cb):
                link(nc.vector.tensor_scalar(tmp1[:], a, ca, None, ALU.mult))
                link(nc.vector.tensor_scalar(tmp2[:], b, cb, None, ALU.mult))
                link(nc.vector.tensor_tensor(out, tmp1[:], tmp2[:], ALU.mult))

            col = lambda t, i: t[:, i:i + 1]
            product(K.k_score[:], col(K.inv, SQ), 2.0 ** 14 / float(np.sqrt(np.float32(DH))), col(K.inv, SK), 2.0 ** 14)
            product(K.k_att[:], col(K.inv, SV), 2.0 ** 14, col(K.inv, SO), 1.0)
            product(K.k_y[:], col(K.inv, SG), 2.0 ** 17, col(K.inv, SU), 2.0 ** 18)
            link(nc.vector.tensor_tensor(K.k_y[:], K.k_y[:], col(K.inv, SD), ALU.mult))
            link(nc.vector.tensor_scalar(K.k_gate[:], col(K.inv, SG), 1.0 / XS, None, ALU.mult))
            link(nc.vector.tensor_scalar(K.k_h[:], col(K.sc, SG), HS, None, ALU.mult))
            norm(0, 0, 0)
            norm(1, 1, 0)
            with dve.Fori(1, NT // 2) as r:
                norm(r * 2, 0, r)
                norm(r * 2 + 1, 1, r)

        @block.scalar
        def _(act):
            def tile(n, k):
                act.wait_ge(s_var, n + 1)
                nc.scalar.activation(sd[:, k:k + 1], ve[:, k:k + 1], ACT.Sqrt, scale=XS ** -2).then_inc(s_std, 1)
                act.wait_ge(s_xn, n + 1)
                wait(act, s_tr, n * 2 - 2)
                nc.scalar.activation(xhl[:, k, 0, :], xn[:, k, :], ACT.Copy).then_inc(s_hi, 1)
                act.wait_ge(s_tr, n * 2 + 1)
                nc.scalar.activation(K.xT[:, 0, :, bass.ds(n * P, P)], pt[k][0][:], ACT.Copy)\
                    .then_inc(s_ev_hi, 1)

            tile(0, 0)
            tile(1, 1)
            with act.Fori(1, NT // 2) as r:
                tile(r * 2, 0)
                tile(r * 2 + 1, 1)

        @block.tensor
        def _(pe):
            pe.wait_ge(s_const, 6)

            def tile(n, k):
                pe.wait_ge(s_hi, n + 1)
                wait(pe, s_ev_hi, n - 1)
                for c in range(NC):
                    last = nc.tensor.transpose(pt[k][0][:, c, :], xhl[:, k, 0, c * P:(c + 1) * P], K.ident[:])
                last.then_inc(s_tr, 1)
                pe.wait_ge(s_lo, n + 1)
                wait(pe, s_ev_lo, n - 1)
                for c in range(NC):
                    last = nc.tensor.transpose(pt[k][1][:, c, :], xhl[:, k, 1, c * P:(c + 1) * P], K.ident[:])
                last.then_inc(s_tr, 1)

            tile(0, 0)
            tile(1, 1)
            with pe.Fori(1, NT // 2) as r:
                tile(r * 2, 0)
                tile(r * 2 + 1, 1)


BT, BB, BPC = 2 * UT, 72, 44
RING = 6
PIECES = (1, 1, 2, 2, 4, 4, 4, 4)
AHEAD = 4
AV_LAG, NORM_LAG, SPLIT_LAG, CTX_LAG = 4, 5, 7, 9


def base(l):
    return 36 * (l // UT) + (l % UT) * (l % UT + 1) // 2


def pbase(l):
    return 22 * (l // UT) + sum(PIECES[:l % UT])


def tile_of(s):
    l = 8 * (s // 36)
    while base(l + 1) <= s:
        l += 1
    return l


def last_of(s, lag):
    l = tile_of(s - lag)
    return l if base(l + 1) - 1 == s - lag else None


def issued(s):
    l = tile_of(s - CTX_LAG)
    return l + 1 if base(l + 1) - 1 <= s - CTX_LAG else l


def has_tile(r, l):
    return not isinstance(r, int) or 0 <= BT * r + l < BT * KVH


def has_block(r, s):
    return not isinstance(r, int) or 0 <= BB * r + s < BB * KVH


def due(k, parts, n):
    return min(n - 1, (2 * k + 1) * n // (2 * parts))


def key_tile(s):
    l = tile_of(s)
    return l % UT if s == base(l) else s - base(l) - 1


def phase_attention(nc, K, wqkv, ropes):
    with ExitStack() as ctx:
        sb = lambda n, s, d: ctx.enter_context(nc.sbuf_tensor(n, s, d))
        ps = lambda n, s, d: ctx.enter_context(nc.psum_tensor(n, s, d))
        sem = lambda n: ctx.enter_context(nc.semaphore("b_" + n))
        rope = sb("b_rope", [P, 2, UT, DH], F32)
        wraw = sb("b_wraw", [P, NC, WCOL], F32)
        wcur = sb("b_wcur", [P, 2, NC, WCOL], F16)
        qkv = sb("b_qkv", [P, 2, WCOL], F32)
        t1 = sb("b_t1", [P, GQ + 1, DH], F32)
        t2 = sb("b_t2", [P, GQ + 1, DH], F32)
        rot = sb("b_rot", [P, 2, GQ + 1, DH], F32)
        nat = sb("b_nat", [P, 2, GQ + 1, 3 * DH], F16)
        qst = sb("b_qst", [P, 4, QW], F16)
        kst = sb("b_kst", [P, 2, T], F16)
        vaug = sb("b_vaug", [P, 2, UT, 66], F16)
        negm = sb("b_negm", [P, 2, GQ], F32)
        maug = sb("b_maug", [P, 2, GQ, 2], F16)
        p32 = sb("b_p32", [P, RING, QW], F32)
        phi = sb("b_phi", [P, RING, QW], F16)
        plo = sb("b_plo", [P, RING, QW], F16)
        num = sb("b_num", [P, GQ, DH], F32)
        rden = sb("b_rden", [P, GQ, 1], F32)
        c32 = sb("b_c32", [P, 2, P], F32)
        chl = sb("b_chl", [P, 2, 2, P], F16)
        ST = [ps(f"b_st{i}", [P, QW], F32) for i in range(3)]
        M = ps("b_m", [P, T], F32)
        AV = ps("b_av", [P, 512], F32)
        PR = ps("b_pr", [P, 512], F32)
        TB = ps("b_tb", [P, 1024], F16)
        apart_pool = sem("apart")
        rope_in, const_ok = sem("rope_in"), sem("const_ok")
        w_in, w_hi, w_ready = sem("w_in"), sem("w_hi"), sem("w_ready")
        p_done, p_evac = sem("p_done"), sem("p_evac")
        rope_st, rope_done = sem("rope_st"), sem("rope_done")
        v_hi, v_ready = sem("v_hi"), sem("v_ready")
        nat_hi, nat_ready = sem("nat_hi"), sem("nat_ready")
        t_done, t_evac = sem("t_done"), sem("t_evac")
        m_mm, m_red, mq_hi, mq_ready = sem("m_mm"), sem("m_red"), sem("mq_hi"), sem("mq_ready")
        maug_t, maug_evac = sem("maug_t"), sem("maug_evac")
        st_done, exp_done, mask_done = sem("st_done"), sem("exp_done"), sem("mask_done")
        hi_act, hi_dve, lo_dve, lo_pool = sem("hi_act"), sem("hi_dve"), sem("lo_dve"), sem("lo_pool")
        av_done, norm_in, norm_done = sem("av_done"), sem("norm_in"), sem("norm_done")
        ctx_hi, ctx_lo, ctx_t, ctxt_evac = sem("ctx_hi"), sem("ctx_lo"), sem("ctx_t"), sem("ctxt_evac")
        block = ctx.enter_context(nc.Block())

        def steps(eng, step, tail):
            for l in range(-AHEAD, 0):
                step(0, l)

            def body(r):
                for l in range(BT):
                    step(r, l)
            loop(eng, 0, KVH - 1, body)
            for s in range(BB, BB + CTX_LAG):
                tail(KVH - 1, s)

        @block.sync
        def _(sp):
            sp.dma_start(rope[:], ropes).then_inc(rope_in, 16)

            def load(r):
                wait(sp, w_ready, r)
                sp.dma_start(wraw[:], wqkv[bass.ds(r, 1)].rearrange("a p c n -> p (a c) n")).then_inc(w_in, 16)
            load(0)
            with sp.Fori(1, KVH) as r:
                load(r)

        @block.tensor
        def _(pe):
            pe.wait_ge(const_ok, 2)

            def project(r, l, cs):
                if not has_tile(r, l) or not cs:
                    return
                if cs[0] == 0:
                    pe.wait_ge(w_ready, r + l // BT + 1)
                    wait(pe, p_evac, r * BT + l)
                t0 = (l // UT) % 2 * T + l % UT * P
                for c in cs:
                    for x, w in ((0, 0), (0, 1), (1, 0)):
                        last = nc.tensor.matmul(PR[:, 0:WCOL], K.xT[:, x, c, t0:t0 + P], wcur[:, w, c, :],
                                                start=(c == 0 and x == 0 and w == 0),
                                                stop=(c == NC - 1 and x == 1))
                if cs[-1] == NC - 1:
                    last.then_inc(p_done, 1)

            def scores_for_max(r, l, k):
                j, h0, hn = l % UT, k * GQ // PIECES[l % UT], GQ // PIECES[l % UT]
                w = (j + 1) * P
                if k == 0:
                    pe.wait_ge(t_evac, r * BT + l + 1)
                wait(pe, m_red, r * BPC + pbase(l) + k)
                for a in range(hn):
                    o = a * (1 << (w - 1).bit_length())
                    q = qst[0:96, l % 4, (h0 + a) * P:(h0 + a + 1) * P]
                    for k0 in range(0, w, 512):
                        k1 = min(w, k0 + 512)
                        nc.tensor.matmul(M[:, o + k0:o + k1], q, kst[0:96, (l // UT) % 2, k0:k1],
                                         start=True, stop=(k1 < w))
                    last = nc.tensor.matmul(M[:, o + w - P:o + w], K.identb[:], K.maskb[:],
                                            start=False, stop=True)
                last.then_inc(m_mm, 1)

            def max_rows(r, l):
                pe.wait_ge(mq_ready, r * BT + l + 1)
                pe.wait_ge(t_evac, r * BT + l + (2 if has_tile(r, l + 1) else 1))
                wait(pe, ctxt_evac, r * BT + issued(base(l - 1) - 1))
                for h in range(GQ):
                    last = nc.tensor.transpose(TB[96:98, h * P:(h + 1) * P], maug[:, l % 2, h, :], K.ident[:])
                last.then_inc(maug_t, 1)

            def stack(r, l):
                pe.wait_ge(nat_ready, r * BT + l + 1)
                wait(pe, t_evac, r * BT + l)
                wait(pe, ctxt_evac, r * BT + issued(base(l - 2) - 1))
                wait(pe, maug_evac, r * BT + l - 2)
                for h in range(GQ + 1):
                    last = nc.tensor.transpose(TB[0:96, h * P:(h + 1) * P], nat[:, l % 2, h, :], K.ident[:])
                last.then_inc(t_done, 1)

            def scores(r, s):
                l = tile_of(s)
                if s == base(l):
                    pe.wait_ge(maug_evac, r * BT + l + 1)
                wait(pe, exp_done, r * BB + s - 2)
                kt = key_tile(s)
                nc.tensor.matmul(ST[s % 3][:], kst[0:98, (l // UT) % 2, kt * P:(kt + 1) * P], qst[0:98, l % 4, :],
                                 start=True, stop=True).then_inc(st_done, 1)

            def weigh(r, s):
                l = tile_of(s)
                first, final = s == base(l), s == base(l + 1) - 1
                if first:
                    pe.wait_ge(v_ready, r * BT + l + 1)
                    wait(pe, norm_in, (r * BT + l) * 2)
                pe.wait_ge(lo_dve if s % 2 == 0 else lo_pool, r * (BB // 2) + s // 2 + 1)
                v = vaug[:, (l // UT) % 2, key_tile(s), :]
                for h in range(GQ):
                    a = h * 65
                    nc.tensor.matmul(AV[:, a:a + 65], phi[:, s % RING, h * P:(h + 1) * P], v[:, 0:65],
                                     start=(first and h == 0), stop=False, skip_group_check=True)
                    last = nc.tensor.matmul(AV[:, a + 32:a + 65], plo[:, s % RING, h * P:(h + 1) * P], v[:, 32:65],
                                            start=False, stop=(final and h == GQ - 1), skip_group_check=True)
                last.then_inc(av_done, 1)

            def after(r, s, l):
                if has_block(r, s - AV_LAG):
                    weigh(r, s - AV_LAG)
                q = last_of(s, CTX_LAG)
                if q is not None and has_tile(r, q):
                    pe.wait_ge(ctx_lo, r * BT + q + 1)
                    wait(pe, maug_evac, r * BT + l + 2 if has_tile(r, l + 1) else KVH * BT)
                    wait(pe, ctxt_evac, r * BT + q)
                    for x in range(2):
                        last = nc.tensor.transpose(TB[:, x * P:(x + 1) * P], chl[:, q % 2, x, :], K.ident[:])
                    last.then_inc(ctx_t, 1)

            def step(r, l):
                if has_tile(r, l + 2):
                    stack(r, l + 2)
                here = has_tile(r, l)
                n = l % UT + 1 if here else 1
                for i in range(n):
                    s = base(l) + i
                    if here:
                        scores(r, s)
                    late = l % BT == BT - AHEAD
                    project(r, l + AHEAD, [c for c in range(NC) if (n - 1 if late else due(c, NC, n)) == i])
                    if i == 0 and has_tile(r, l + 1):
                        max_rows(r, l + 1)
                    for k in range(PIECES[(l + 2) % UT] if has_tile(r, l + 2) else 0):
                        if due(k, PIECES[(l + 2) % UT], n) == i:
                            scores_for_max(r, l + 2, k)
                    if here:
                        after(r, s, l)

            steps(pe, step, lambda r, s: after(r, s, BT))

        @block.scalar
        def _(act):
            def split_w(r):
                act.wait_ge(w_in, (r + 1) * 16)
                wait(act, p_done, r * BT)
                for (a, b), m in zip(((0, P), (P, P + DH), (P + DH, WCOL)), (SQ, SK, SV)):
                    last = nc.scalar.activation(wcur[:, 0, :, a:b], wraw[:, :, a:b], ACT.Copy, scale=K.sc[:, m:m + 1])
                last.then_inc(w_hi, 1)

            def exps(r, s):
                act.wait_ge(st_done, r * BB + s + 1)
                wait(act, lo_dve if s % 2 == 0 else lo_pool, r * (BB // 2) + (s - RING) // 2 + 1)
                nc.scalar.activation(p32[:, s % RING, :], ST[s % 3][:], ACT.Exp, bias=PS_LOG,
                                     scale=K.k_score[:]).then_inc(exp_done, 1)

            def after(r, s):
                if has_block(r, s - 1) and (s - 1) % 2 == 0:
                    l = tile_of(s - 1)
                    if s - 1 == base(l):
                        act.wait_ge(mask_done, r * BT + l + 1)
                    act.wait_ge(exp_done, r * BB + s)
                    wait(act, av_done, r * BB + s - RING)
                    nc.scalar.activation(phi[:, (s - 1) % RING, :], p32[:, (s - 1) % RING, :], ACT.Copy)\
                        .then_inc(hi_act, 1)
                q = last_of(s, SPLIT_LAG)
                if q is not None and has_tile(r, q):
                    act.wait_ge(norm_done, r * BT + q + 1)
                    wait(act, ctx_t, r * BT + q - 1)
                    nc.scalar.activation(chl[:, q % 2, 0, :], c32[:, q % 2, :], ACT.Copy).then_inc(ctx_hi, 1)
                q = last_of(s, CTX_LAG)
                if q is not None and has_tile(r, q):
                    act.wait_ge(ctx_t, r * BT + q + 1)
                    t0 = (q // UT) % 2 * T + q % UT * P
                    g = r + q // BT
                    dst = K.ctxT[:, :, bass.ds(g, 1), t0:t0 + P].rearrange("p x a t -> p x (a t)")
                    nc.scalar.activation(dst, TB[:, 0:2 * P].rearrange("p (x t) -> p x t", x=2), ACT.Copy)\
                        .then_inc(ctxt_evac, 1)

            def step(r, l):
                n = r * BT + l
                if has_tile(r, l + AHEAD) and (l + AHEAD) % BT == 0:
                    split_w(r + (l + AHEAD) // BT)
                if has_tile(r, l + 2):
                    act.wait_ge(t_done, n + 3)
                    wait(act, st_done, r * BB + base(l - 1))
                    nc.scalar.activation(qst[0:96, (l + 2) % 4, :], TB[0:96, 0:QW], ACT.Copy)
                    nc.scalar.activation(kst[0:96, ((l + 2) // UT) % 2, (l + 2) % UT * P:(l + 2) % UT * P + P],
                                         TB[0:96, QW:QW + P], ACT.Copy).then_inc(t_evac, 1)
                here = has_tile(r, l)
                for i in range(l % UT + 1 if here else 1):
                    s = base(l) + i
                    if here:
                        exps(r, s)
                    if i == 0 and has_tile(r, l + 1):
                        act.wait_ge(maug_t, n + 2)
                        nc.scalar.activation(qst[96:98, (l + 1) % 4, :], TB[96:98, 0:QW], ACT.Copy)\
                            .then_inc(maug_evac, 1)
                    if here:
                        after(r, s)
                if has_tile(r, l + 3):
                    act.wait_ge(rope_done, n + 4)
                    wait(act, t_done, n + 2)
                    src = rot[:, (l + 3) % 2, :, :]
                    dst = nat[:, (l + 3) % 2, :, :]
                    hi2 = dst[:, 0:GQ, :].rearrange("p h (x d) -> p h x d", x=3)[:, :, 0:3:2, :]
                    nc.scalar.activation(hi2, src[:, 0:GQ, None, :].broadcast_to([P, GQ, 2, DH]), ACT.Copy)
                    nc.scalar.activation(dst[:, GQ, 0:2 * DH].rearrange("p (x d) -> p x d", x=2),
                                         src[:, GQ, None, :].broadcast_to([P, 2, DH]), ACT.Copy).then_inc(nat_hi, 1)
                if has_tile(r, l + AHEAD):
                    act.wait_ge(p_done, n + AHEAD + 1)
                    wait(act, rope_done, n + AHEAD - 1)
                    wait(act, v_ready, n + AHEAD - 1)
                    nc.scalar.activation(qkv[:, (l + AHEAD) % 2, :], PR[:, 0:WCOL], ACT.Copy, scale=QS)\
                        .then_inc(p_evac, 1)

            steps(act, step, lambda r, s: after(r, s))

        @block.vector
        def _(dve):
            def split_w(r):
                dve.wait_ge(w_hi, r + 1)
                for (a, b), m in zip(((0, P), (P, P + DH), (P + DH, WCOL)), (SQ, SK, SV)):
                    last = nc.vector.scalar_tensor_tensor(wcur[:, 1, :, a:b], wraw[:, :, a:b], K.sc[:, m:m + 1],
                                                          wcur[:, 0, :, a:b], ALU.mult, ALU.subtract)
                last.then_inc(w_ready, 1)

            def after(r, s):
                if has_block(r, s - 1) and (s - 1) % 2 == 1:
                    l = tile_of(s - 1)
                    if s - 1 == base(l):
                        dve.wait_ge(mask_done, r * BT + l + 1)
                    dve.wait_ge(exp_done, r * BB + s)
                    wait(dve, av_done, r * BB + s - RING)
                    nc.vector.tensor_copy(phi[:, (s - 1) % RING, :], p32[:, (s - 1) % RING, :]).then_inc(hi_dve, 1)
                if has_block(r, s - 2) and (s - 2) % 2 == 0:
                    dve.wait_ge(hi_act, r * (BB // 2) + (s - 2) // 2 + 1)
                    wait(dve, av_done, r * BB + s - 1 - RING)
                    nc.vector.tensor_tensor(plo[:, (s - 2) % RING, :], p32[:, (s - 2) % RING, :],
                                            phi[:, (s - 2) % RING, :], ALU.subtract).then_inc(lo_dve, 1)
                q = last_of(s, NORM_LAG)
                if q is not None and has_tile(r, q):
                    n = r * BT + q
                    dve.wait_ge(av_done, r * BB + base(q + 1))
                    wait(dve, norm_done, n)
                    av = AV[:, 0:4 * 65].rearrange("p (h c) -> p h c", h=GQ)
                    nc.vector.tensor_reduce(num[:], av[:, :, 0:64].rearrange("p h (x d) -> p h d x", x=2),
                                            AX.X, ALU.add).then_inc(norm_in, 1)
                    nc.vector.reciprocal(rden[:], av[:, :, 64:65]).then_inc(norm_in, 1)
                    dve.wait_ge(norm_in, (n + 1) * 2)
                    wait(dve, ctx_hi, n - 1)
                    wait(dve, ctx_lo, n - 1)
                    nc.vector.tensor_tensor(c32[:, q % 2, :].rearrange("p (h d) -> p h d", h=GQ), num[:],
                                            rden[:].broadcast_to([P, GQ, DH]), ALU.mult).then_inc(norm_done, 1)
                q = last_of(s, SPLIT_LAG)
                if q is not None and has_tile(r, q):
                    dve.wait_ge(ctx_hi, r * BT + q + 1)
                    nc.vector.tensor_tensor(chl[:, q % 2, 1, :], c32[:, q % 2, :], chl[:, q % 2, 0, :],
                                            ALU.subtract).then_inc(ctx_lo, 1)

            def row_max(r, l, k):
                j, h0, hn = l % UT, k * GQ // PIECES[l % UT], GQ // PIECES[l % UT]
                w = (j + 1) * P
                o = 1 << (w - 1).bit_length()
                dve.wait_ge(m_mm, r * BPC + pbase(l) + k + 1)
                wait(dve, mq_ready, r * BT + l)
                nc.vector.tensor_reduce(negm[:, l % 2, h0:h0 + hn],
                                        M[:, 0:hn * o].rearrange("p (h c) -> p h c", h=hn)[:, :, 0:w],
                                        AX.X, ALU.max, negate=True).then_inc(m_red, 1)
                if k == PIECES[j] - 1:
                    dve.wait_ge(m_red, r * BPC + pbase(l + 1))
                    wait(dve, maug_t, r * BT + l - 1)
                    nc.vector.tensor_scalar(maug[:, l % 2, :, 0], negm[:, l % 2, :], 1.0 / MS, None, ALU.mult)\
                        .then_inc(mq_hi, 1)
                    dve.wait_ge(mq_hi, r * BT + l + 1)
                    nc.vector.scalar_tensor_tensor(maug[:, l % 2, :, 1], negm[:, l % 2, :], 1.0 / MS,
                                                   maug[:, l % 2, :, 0], ALU.mult, ALU.subtract)\
                        .then_inc(mq_ready, 1)

            def step(r, l):
                n = r * BT + l
                if has_tile(r, l + AHEAD) and (l + AHEAD) % BT == 0:
                    split_w(r + (l + AHEAD) // BT)
                here = has_tile(r, l)
                nb = l % UT + 1 if here else 1
                for i in range(nb):
                    if here:
                        after(r, base(l) + i)
                    for k in range(PIECES[(l + 2) % UT] if has_tile(r, l + 2) else 0):
                        if due(k, PIECES[(l + 2) % UT], nb) == i:
                            row_max(r, l + 2, k)
                if has_tile(r, l + 3):
                    dve.wait_ge(p_evac, n + 4)
                    b, j, k = ((l + 3) // UT) % 2, (l + 3) % UT, (l + 3) % 2
                    wait(dve, av_done, r * BB + 36 * ((l + 3) // UT - 1))
                    v32 = qkv[:, k, WCOL - DH:WCOL]
                    nc.vector.tensor_copy(vaug[:, b, j, 32:64], v32).then_inc(v_hi, 1)
                    dve.wait_ge(v_hi, n + 4)
                    nc.vector.tensor_tensor(vaug[:, b, j, 0:32], v32, vaug[:, b, j, 32:64], ALU.subtract)\
                        .then_inc(v_ready, 1)
                    dve.wait_ge(nat_hi, n + 4)
                    nc.vector.tensor_tensor(nat[:, k, 0:GQ, DH:2 * DH], rot[:, k, 0:GQ, :], nat[:, k, 0:GQ, 0:DH],
                                            ALU.subtract)
                    nc.vector.tensor_tensor(nat[:, k, GQ, 2 * DH:3 * DH], rot[:, k, GQ, :], nat[:, k, GQ, 0:DH],
                                            ALU.subtract).then_inc(nat_ready, 1)

            steps(dve, step, lambda r, s: after(r, s))

        @block.gpsimd
        def _(pool):
            nc.gpsimd.memset(kst[96:98, :, :], MS).then_inc(const_ok, 1)
            pool.wait_ge(const_ok, 1)
            nc.gpsimd.memset(vaug[:, :, :, 64:65], 1.0).then_inc(const_ok, 1)
            pool.wait_ge(rope_in, 16)

            def rotate(r, l):
                n = r * BT + l
                k, j = l % 2, l % UT
                pool.wait_ge(p_evac, n + 1)
                wait(pool, rope_done, n)
                wait(pool, nat_ready, n - 1)
                x = qkv[:, k, 0:(GQ + 1) * DH].rearrange("p (h d) -> p h d", d=DH)
                bc = lambda t, w: t[:, None, :].broadcast_to([P, GQ + 1, w])
                H = DH // 2
                nc.gpsimd.tensor_tensor(t1[:], x, bc(rope[:, 0, j, :], DH), ALU.mult)
                nc.gpsimd.tensor_tensor(t2[:, :, 0:H], x[:, :, H:DH], bc(rope[:, 1, j, 0:H], H), ALU.mult)
                nc.gpsimd.tensor_tensor(t2[:, :, H:DH], x[:, :, 0:H], bc(rope[:, 1, j, H:DH], H), ALU.mult)\
                    .then_inc(rope_st, 1)
                pool.wait_ge(rope_st, n + 1)
                nc.gpsimd.tensor_tensor(rot[:, k, :, :], t1[:], t2[:], ALU.add).then_inc(rope_done, 1)

            def after(r, s):
                if has_block(r, s - 2) and (s - 2) % 2 == 1:
                    pool.wait_ge(hi_dve, r * (BB // 2) + (s - 2) // 2 + 1)
                    wait(pool, av_done, r * BB + s - 1 - RING)
                    nc.gpsimd.tensor_tensor(plo[:, (s - 2) % RING, :], p32[:, (s - 2) % RING, :],
                                            phi[:, (s - 2) % RING, :], ALU.subtract).then_inc(lo_pool, 1)

            def step(r, l):
                here = has_tile(r, l)
                for i in range(l % UT + 1 if here else 1):
                    s = base(l) + i
                    if i == 0 and here:
                        pool.wait_ge(exp_done, r * BB + s + 1)
                        apart(pool, apart_pool)
                        d = p32[:, s % RING, :].rearrange("p (h q) -> p h q", h=GQ)
                        nc.gpsimd.affine_select(out=d, in_=d, compare_op=ALU.is_ge, fill=0.0, base=0,
                                                pattern=[[0, GQ], [1, P]], channel_multiplier=-1)\
                            .then_inc(mask_done, 1)
                    if here:
                        after(r, s)
                    if i == 0 and has_tile(r, l + 3):
                        rotate(r, l + 3)

            steps(pool, step, lambda r, s: after(r, s))


def phase_output(nc, K, x, wo, x1_dram):
    with ExitStack() as ctx:
        sb = lambda n, s, d: ctx.enter_context(nc.sbuf_tensor("c_" + n, s, d))
        ps = lambda n, s, d: ctx.enter_context(nc.psum_tensor("c_" + n, s, d))
        sem = lambda n: ctx.enter_context(nc.semaphore("c_" + n))
        wraw = sb("wraw", [P, 2, 2 * E], F32)
        wohl = sb("wohl", [P, 2, NC, E], F16)
        xin = sb("xin", [P, 2, E], F32)
        z = sb("z", [P, E], F32)
        x1 = sb("x1", [P, 2, E], F32)
        xhl = sb("xhl", [P, 2, 2, E], F16)
        st6 = sb("st6", [P, 2, 6], F32)
        mv = sb("mv", [P, 2], F32)
        ve = sb("ve", [P, 1], F32)
        sd = sb("sd", [P, 1], F32)
        rs = sb("rs", [P, 1], F32)
        Y = [ps(f"y{i}", [P, E], F32) for i in range(2)]
        PT = [[ps(f"pt{s}{h}", [P, NC, P], F16) for h in range(2)] for s in range(2)]
        w_in = [sem("w_in0"), sem("w_in1")]
        w_hi, w_lo = sem("w_hi"), sem("w_lo")
        x_in = [sem("x_in0"), sem("x_in1")]
        x1_out = [sem("x1_out0"), sem("x1_out1")]
        y_mm, chain = sem("y_mm"), sem("chain")
        var_ok, std_ok = sem("var"), sem("std")
        x1_ok, xn_ok, hi_ok, lo_ok = sem("x1_ok"), sem("xn"), sem("hi"), sem("lo")
        apart_dve = sem("apart")
        tr, ev_hi, ev_lo = sem("tr"), sem("ev_hi"), sem("ev_lo")
        xv = x.rearrange("(n p) e -> n p e", p=P)
        x1v = x1_dram.rearrange("(n p) e -> n p e", p=P)
        LINKS = 14
        block = ctx.enter_context(nc.Block())

        def pair(eng, tile):
            def body(r):
                tile(r * 2, 0, r)
                tile(r * 2 + 1, 1, r)
            loop(eng, 0, NT // 2 - 1, body)

        @block.sync
        def _(sp):
            for i in range(4):
                wait(sp, w_lo, i - 1)
                sp.dma_start(wraw[:, i % 2, :], wo[:, bass.ts(i, 2 * E)]).then_inc(w_in[i % 2], 16)

            def tile(n, k, r):
                wait(sp, x1_ok, n - 1)
                sp.dma_start(xin[:, k, :], xv[bass.ds(n, 1)].rearrange("a p e -> p (a e)")).then_inc(x_in[k], 16)
                if isinstance(n, int) and n == 0:
                    return
                store(n - 1, 1 - k)

            def store(n, k):
                sp.wait_ge(x1_ok, n + 1)
                sp.dma_start(x1v[bass.ds(n, 1)].rearrange("a p e -> p (a e)"), x1[:, k, :]).then_inc(x1_out[k], 16)

            pair(sp, tile)
            store(NT - 1, 1)
            for k in range(2):
                sp.wait_ge(x1_out[k], 16 * NT // 2)

        @block.scalar
        def _(act):
            for i in range(4):
                act.wait_ge(w_in[i % 2], 16 * (i // 2 + 1))
                nc.scalar.activation(wohl[:, 0, 2 * i:2 * i + 2, :].rearrange("p c n -> p (c n)"), wraw[:, i % 2, :],
                                     ACT.Copy, scale=K.sc[:, SO:SO + 1]).then_inc(w_hi, 1)

            def copy_out(n, k):
                act.wait_ge(tr, n * 2 + 1)
                nc.scalar.activation(K.xT[:, 0, :, bass.ds(n * P, P)], PT[k][0][:], ACT.Copy).then_inc(ev_hi, 1)

            def tile(n, k, r):
                act.wait_ge(var_ok, n * 2 + 1)
                nc.scalar.activation(sd[:], ve[:], ACT.Sqrt).then_inc(std_ok, 1)
                act.wait_ge(var_ok, n * 2 + 2)
                nc.scalar.activation(sd[:], ve[:], ACT.Sqrt, scale=XS ** -2).then_inc(std_ok, 1)
                act.wait_ge(xn_ok, n + 1)
                wait(act, tr, n * 2 - 2)
                nc.scalar.activation(xhl[:, k, 0, :], z[:], ACT.Copy).then_inc(hi_ok, 1)
                if not (isinstance(n, int) and n == 0):
                    copy_out(n - 1, 1 - k)

            pair(act, tile)
            copy_out(NT - 1, 1)

        @block.tensor
        def _(pe):
            pe.wait_ge(w_lo, 4)

            def transposes(n, k):
                for h, ready, out in ((0, hi_ok, ev_hi), (1, lo_ok, ev_lo)):
                    pe.wait_ge(ready, n + 1)
                    wait(pe, out, n - 1)
                    for c in range(NC):
                        j0 = c % 4 * 2 * P + c // 4
                        last = nc.tensor.transpose(PT[k][h][:, c, :], xhl[:, k, h, j0:j0 + 2 * P - 1:2], K.ident[:])
                    last.then_inc(tr, 1)

            def tile(n, k, r):
                wait(pe, chain, (n - 1) * LINKS - 7)
                for c in range(NC):
                    for a, b in ((0, 0), (0, 1), (1, 0)):
                        for h in range(2):
                            last = nc.tensor.matmul(Y[k][:, h * 512:(h + 1) * 512],
                                                    K.ctxT[:, a, c, bass.ds(n * P, P)],
                                                    wohl[:, b, c, h * 512:(h + 1) * 512],
                                                    start=(c == 0 and a == b), stop=(c == NC - 1 and a == 1))
                last.then_inc(y_mm, 1)
                if not (isinstance(n, int) and n == 0):
                    transposes(n - 1, 1 - k)

            pair(pe, tile)
            transposes(NT - 1, 1)

        @block.vector
        def _(dve):
            for i in range(4):
                dve.wait_ge(w_hi, i + 1)
                hi, lo = (wohl[:, h, 2 * i:2 * i + 2, :].rearrange("p c n -> p (c n)") for h in range(2))
                nc.vector.scalar_tensor_tensor(lo, wraw[:, i % 2, :], K.sc[:, SO:SO + 1], hi,
                                               ALU.mult, ALU.subtract).then_inc(w_lo, 1)

            def copy_out(n, k):
                dve.wait_ge(tr, n * 2 + 2)
                nc.vector.tensor_copy(K.xT[:, 1, :, bass.ds(n * P, P)], PT[k][1][:]).then_inc(ev_lo, 1)

            def tile(n, k, r):
                links = [0]

                def link(ins):
                    links[0] += 1
                    ins.then_inc(chain, 1)
                    dve.wait_ge(chain, n * LINKS + links[0])

                def stats(src):
                    for h in range(2):
                        last = nc.vector.bn_stats(st6[:, h, :], src[:, h * 512:(h + 1) * 512])
                    link(last)
                    apart(dve, apart_dve)
                    link(nc.vector.bn_aggr(mv[:], st6[:]))

                dve.wait_ge(y_mm, n + 1)
                stats(Y[k])
                link(nc.vector.tensor_scalar(ve[:], mv[:, 1:2], K.k_att[:], K.k_att[:], ALU.mult, ALU.mult))
                link(nc.vector.tensor_scalar(ve[:], ve[:], EPS, None, ALU.add))
                dve.sem_inc(var_ok, 1)
                dve.wait_ge(std_ok, n * 2 + 1)
                link(nc.vector.reciprocal(rs[:], sd[:]))
                link(nc.vector.tensor_scalar(rs[:], rs[:], K.k_att[:], None, ALU.mult))
                wait(dve, hi_ok, n)
                link(nc.vector.tensor_scalar(z[:], Y[k][:], mv[:, 0:1], rs[:], ALU.subtract, ALU.mult))
                dve.wait_ge(x_in[k], r * 16 + 16)
                wait(dve, x1_out[k], r * 16)
                link(nc.vector.tensor_tensor(x1[:, k, :], z[:], xin[:, k, :], ALU.add))
                dve.sem_inc(x1_ok, 1)
                stats(x1[:, k, :])
                link(nc.vector.tensor_scalar(ve[:], mv[:, 1:2], EPS, None, ALU.add))
                dve.sem_inc(var_ok, 1)
                dve.wait_ge(std_ok, n * 2 + 2)
                link(nc.vector.reciprocal(rs[:], sd[:]))
                link(nc.vector.tensor_scalar(z[:], x1[:, k, :], mv[:, 0:1], rs[:], ALU.subtract, ALU.mult))
                dve.sem_inc(xn_ok, 1)
                dve.wait_ge(hi_ok, n + 1)
                link(nc.vector.tensor_tensor(xhl[:, k, 1, :], z[:], xhl[:, k, 0, :], ALU.subtract))
                dve.sem_inc(lo_ok, 1)
                assert links[0] == LINKS
                if not (isinstance(n, int) and n == 0):
                    copy_out(n - 1, 1 - k)

            pair(dve, tile)
            copy_out(NT - 1, 1)


def phase_ffn(nc, K, gu_q, gu_sz, down_q, down_sz, x1_dram, out):
    with ExitStack() as ctx:
        sb = lambda n, s, d: ctx.enter_context(nc.sbuf_tensor("d_" + n, s, d))
        ps = lambda n, s, d: ctx.enter_context(nc.psum_tensor("d_" + n, s, d))
        sem = lambda n: ctx.enter_context(nc.semaphore("d_" + n))
        y = sb("y", [P, NT, E], F32)
        wgu = [sb(f"wgu{c}", [P, 2, NC, 2, P], F16) for c in range(2)]
        wd = sb("wd", [P, 2, 2, E], F16)
        gq = sb("gq", [P, 4, 2 * P], I32)
        gsz = sb("gsz", [P, 4, 4 * P], F32)
        dq = sb("dq", [P, E], I32)
        dsz = sb("dsz", [P, 2, E], F32)
        nib = sb("nib", [P, 512], I32)
        wf = sb("wf", [P, 512], F32)
        hT = sb("hT", [P, 2, 2, TOK], F16)
        sil = sb("sil", [P, 2, 512], F32)
        h32 = sb("h32", [P, 2, 512], F32)
        st6 = sb("st6", [P, 2, 2, 6], F32)
        mv = sb("mv", [P, 2, 2], F32)
        ve = sb("ve", [P, 2], F32)
        sd = sb("sd", [P, 2], F32)
        rs = sb("rs", [P, 2], F32)
        x1 = gsz[:].rearrange("p a b -> p (a b)").rearrange("p (k e) -> p k e", k=2)
        z = dsz
        GP = [ps(f"g{i}", [P, 512], F32) for i in range(2)]
        UP = [ps(f"u{i}", [P, 512], F32) for i in range(2)]
        D = [ps(f"d{i}", [P, E], F32) for i in range(2)]
        gq_in, gsz_in, dq_in, dsz_in = sem("gq_in"), sem("gsz_in"), sem("dq_in"), sem("dsz_in")
        g_unpacked, g_scaled, d_unpacked, d_scaled = sem("g_unp"), sem("g_scl"), sem("d_unp"), sem("d_scl")
        w_sub, w_step, w_hi, w_lo = sem("w_sub"), sem("w_step"), sem("w_hi"), sem("w_lo")
        gu_mm, silu_ok, h_ok, h_hi, h_lo = sem("gu_mm"), sem("silu"), sem("h_ok"), sem("h_hi"), sem("h_lo")
        d_mm, y_ok = sem("d_mm"), sem("y_ok")
        x1_in = [sem("x1_in0"), sem("x1_in1")]
        chain, var_ok, std_ok, z_ok, o_ok = sem("chain"), sem("var"), sem("std"), sem("z_ok"), sem("o_ok")
        o_out = [sem("o_out0"), sem("o_out1")]
        x1v = x1_dram.rearrange("(n p) e -> n p e", p=P)
        outv = out.rearrange("(n p) e -> n p e", p=P)
        LAST = GROUPS
        width = lambda g: LASTW if isinstance(g, int) and g == LAST else P
        block = ctx.enter_context(nc.Block())

        def groups(eng, body):
            body(0)
            with eng.Fori(1, LAST - 1) as g:
                body(g)
            body(LAST - 1)
            body(LAST)


        @block.sync
        def _(sp):
            def load_chunk(g, c):
                w = width(g)
                i = g * 2 + c
                o = g * (4 * P) + c * 2 * w
                wait(sp, g_unpacked, i * 4)
                sp.dma_start(gq[:, :, 0:2 * w], gu_q.rearrange("(j p) n -> p j n", p=P)[:, :, bass.ds(o, 2 * w)])\
                    .then_inc(gq_in, 16)
                wait(sp, g_scaled, i * 4)
                for q in range(4):
                    src = gu_sz.rearrange("(j q) n -> q j n", q=4)[q, :, bass.ds(g * (8 * P) + c * 4 * w, 4 * w)]
                    sp.dma_start(gsz[q * 32:(q + 1) * 32, :, 0:4 * w], src.partition_broadcast(32))\
                        .then_inc(gsz_in, 16)

            def load_down(g):
                w = width(g)
                wait(sp, d_unpacked, g * 4)
                sp.dma_start(dq[0:w, :], down_q[bass.ds(g * P, w), :]).then_inc(dq_in, 16)
                wait(sp, d_scaled, g * 4)
                for q in range(w // 32):
                    src = down_sz[bass.ds(g * 4 + q, 1)].rearrange("a x n -> (a x) n")
                    sp.dma_start(dsz[q * 32:(q + 1) * 32, :, :], src.partition_broadcast(32)).then_inc(dsz_in, 16)

            def body(g):
                load_chunk(g, 0)
                load_chunk(g, 1)
                load_down(g)
            groups(sp, body)
            sp.wait_ge(w_lo, 12 * (LAST + 1))
            for t in range(NT):
                wait(sp, o_ok, t - 1)
                sp.dma_start(x1[:, t % 2, :], x1v[t]).then_inc(x1_in[t % 2], 16)
                if t:
                    sp.wait_ge(o_ok, t)
                    sp.dma_start(outv[t - 1], z[:, (t - 1) % 2, :]).then_inc(o_out[(t - 1) % 2], 16)
            sp.wait_ge(o_ok, NT)
            sp.dma_start(outv[NT - 1], z[:, 1, :]).then_inc(o_out[1], 16)
            for k in range(2):
                sp.wait_ge(o_out[k], 16 * NT // 2)

        def split_target(g, kind, k):
            w = width(g)
            if kind == 2:
                dst = [wd[0:w, x, k // 2, k % 2 * 512:(k % 2 + 1) * 512] for x in range(2)]
                return dst, wf[0:w, :], K.sc[0:w, SD:SD + 1]
            n = k // 2 * 4
            m = SG + k % 2
            dst = [wgu[kind][:, x, n:n + 4, k % 2, 0:w] for x in range(2)]
            return dst, wf[:, 0:4 * w].rearrange("p (j i) -> p j i", j=4), K.sc[:, m:m + 1]

        @block.scalar
        def _(act):
            def item(g, kind, k):
                n = g * 12 + kind * 4 + k
                act.wait_ge(w_step, n + 1)
                (hi, _), src, scale = split_target(g, kind, k)
                nc.scalar.activation(hi, src, ACT.Copy, scale=scale).then_inc(w_hi, 1)

            def gate(g, c, b):
                w, e = width(g), g * 8 + c * 4 + b
                act.wait_ge(gu_mm, e + 1)
                wait(act, h_ok, e - 1)
                nc.scalar.activation(sil[0:w, b % 2, :], GP[b % 2][0:w, :], ACT.Silu, scale=K.k_gate[0:w, :])\
                    .then_inc(silu_ok, 1)
                act.wait_ge(h_ok, e + 1)
                wait(act, d_mm, g * NT)
                nc.scalar.activation(hT[0:w, 0, c, b * 512:(b + 1) * 512], h32[0:w, b % 2, :], ACT.Copy)\
                    .then_inc(h_hi, 1)

            for k in range(8):
                item(0, k // 4, k % 4)

            def body(g):
                last = isinstance(g, int) and g == LAST
                for b in range(4):
                    gate(g, 0, b)
                    item(g, 2, b)
                for b in range(4):
                    gate(g, 1, b)
                    if not last:
                        item(g + 1, 0, b)
                if not last:
                    for k in range(4):
                        item(g + 1, 1, k)
            groups(act, body)
            for t in range(NT):
                act.wait_ge(var_ok, t + 1)
                nc.scalar.activation(sd[:, t % 2:t % 2 + 1], ve[:, t % 2:t % 2 + 1], ACT.Sqrt).then_inc(std_ok, 1)

        @block.tensor
        def _(pe):
            def body(g):
                w = width(g)
                for c in range(2):
                    pe.wait_ge(w_lo, g * 12 + c * 4 + 4)
                    for b in range(4):
                        e = g * 8 + c * 4 + b
                        wait(pe, silu_ok, e - 1)
                        wait(pe, h_ok, e - 1)
                        for m, out_bank in enumerate((GP[b % 2], UP[b % 2])):
                            for kc in range(NC):
                                for a, x in ((0, 0), (0, 1), (1, 0)):
                                    last = nc.tensor.matmul(out_bank[0:w, :], wgu[c][:, a, kc, m, 0:w],
                                                            K.xT[:, x, kc, b * 512:(b + 1) * 512],
                                                            start=(kc == 0 and a == x), stop=(kc == NC - 1 and a == 1))
                        last.then_inc(gu_mm, 1)
                pe.wait_ge(w_lo, g * 12 + 12)
                for t in range(NT):
                    pe.wait_ge(h_lo, g * 8 + 4 + t // 4 + 1)
                    wait(pe, y_ok, g * NT + t - 1)
                    for c in range(2):
                        for a, b in ((0, 0), (0, 1), (1, 0)):
                            for h in range(2):
                                last = nc.tensor.matmul(D[t % 2][:, h * 512:(h + 1) * 512],
                                                        hT[0:w, a, c, t * P:(t + 1) * P],
                                                        wd[0:w, b, c, h * 512:(h + 1) * 512],
                                                        start=(c == 0 and a == b), stop=(c == 1 and a == 1))
                    last.then_inc(d_mm, 1)
            groups(pe, body)

        @block.vector
        def _(dve):
            links = [0]

            def link(ins):
                links[0] += 1
                ins.then_inc(chain, 1)
                dve.wait_ge(chain, links[0])

            def item(g, kind, k):
                w, n = width(g), g * 12 + kind * 4 + k
                (hi, lo), src, scale = split_target(g, kind, k)
                wait(dve, w_lo, n)
                if kind == 2:
                    dve.wait_ge(dq_in, g * 16 + 16)
                    raw, nb = dq[0:w, k % 2 * 512:(k % 2 + 1) * 512], nib[0:w, :]
                    s, zero = (dsz[0:w, x, k % 2 * 512:(k % 2 + 1) * 512] for x in range(2))
                    unpacked, scaled = d_unpacked, d_scaled
                else:
                    dve.wait_ge(gq_in, (g * 2 + kind + 1) * 16)
                    raw = gq[:, :, k % 2 * w:(k % 2 + 1) * w]
                    nb = nib[:, 0:4 * w].rearrange("p (j i) -> p j i", j=4)
                    s, zero = (gsz[:, :, (k % 2 * 2 + x) * w:(k % 2 * 2 + x + 1) * w] for x in range(2))
                    unpacked, scaled = g_unpacked, g_scaled
                if k // 2 == 0:
                    ins = nc.vector.tensor_scalar(nb, raw, 4, 15, ALU.logical_shift_right, ALU.bitwise_and)
                else:
                    ins = nc.vector.tensor_scalar(nb, raw, 15, None, ALU.bitwise_and)
                ins.then_inc(unpacked, 1)
                if kind == 2:
                    dve.wait_ge(d_unpacked, g * 4 + k + 1)
                    if width(g) == P:
                        dve.wait_ge(dsz_in, g * 64 + 64)
                    else:
                        dve.wait_ge(dsz_in, LAST * 64 + LASTW // 32 * 16)
                else:
                    dve.wait_ge(g_unpacked, (g * 2 + kind) * 4 + k + 1)
                    dve.wait_ge(gsz_in, (g * 2 + kind + 1) * 64)
                nc.vector.tensor_tensor(src, nb, zero, ALU.subtract).then_inc(w_sub, 1)
                dve.wait_ge(w_sub, n + 1)
                nc.vector.tensor_tensor(src, src, s, ALU.mult).then_inc(scaled, 1)
                if kind == 2:
                    dve.wait_ge(d_scaled, g * 4 + k + 1)
                    wait(dve, d_mm, g * NT)
                else:
                    dve.wait_ge(g_scaled, (g * 2 + kind) * 4 + k + 1)
                    wait(dve, gu_mm, g * 8 + kind * 4 - 4)
                dve.sem_inc(w_step, 1)
                dve.wait_ge(w_hi, n + 1)
                nc.vector.scalar_tensor_tensor(lo, src, scale, hi, ALU.mult, ALU.subtract).then_inc(w_lo, 1)

            def gated(g, c, b):
                w, e = width(g), g * 8 + c * 4 + b
                dve.wait_ge(silu_ok, e + 1)
                wait(dve, h_hi, e - 1)
                wait(dve, h_lo, e - 1)
                nc.vector.scalar_tensor_tensor(h32[0:w, b % 2, :], sil[0:w, b % 2, :], K.k_h[0:w, :],
                                               UP[b % 2][0:w, :], ALU.mult, ALU.mult).then_inc(h_ok, 1)

            def gated_low(g, c, b):
                w, e = width(g), g * 8 + c * 4 + b
                dve.wait_ge(h_hi, e + 1)
                cols = slice(b * 512, (b + 1) * 512)
                nc.vector.tensor_tensor(hT[0:w, 1, c, cols], h32[0:w, b % 2, :], hT[0:w, 0, c, cols],
                                        ALU.subtract).then_inc(h_lo, 1)

            def gather(g, t):
                dve.wait_ge(d_mm, g * NT + t + 1)
                if isinstance(g, int) and g == 0:
                    nc.vector.tensor_copy(y[:, t, :], D[t % 2][:]).then_inc(y_ok, 1)
                else:
                    wait(dve, y_ok, g * NT + t - (NT - 1))
                    nc.vector.tensor_tensor(y[:, t, :], y[:, t, :], D[t % 2][:], ALU.add).then_inc(y_ok, 1)

            for k in range(8):
                item(0, k // 4, k % 4)

            def body(g):
                last = isinstance(g, int) and g == LAST
                for b in range(4):
                    gated(g, 0, b)
                    item(g, 2, b)
                    gated_low(g, 0, b)
                for b in range(4):
                    gated(g, 1, b)
                    if not last:
                        item(g + 1, 0, b)
                    gated_low(g, 1, b)
                for t in range(NT):
                    gather(g, t)
                    if not last and t % 4 == 3:
                        item(g + 1, 1, t // 4)
                    if last:
                        last_norm(t)
                        if t:
                            last_norm_end(t - 1)

            def last_norm(t):
                k = t % 2
                dve.wait_ge(y_ok, LAST * NT + t + 1)
                for h in range(2):
                    last = nc.vector.bn_stats(st6[:, k, h, :], y[:, t, h * 512:(h + 1) * 512])
                link(last)
                link(nc.vector.bn_aggr(mv[:, k, :], st6[:, k, :, :]))
                wait(dve, std_ok, t - 1)
                link(nc.vector.tensor_scalar(ve[:, k:k + 1], mv[:, k, 1:2], K.k_y[:], K.k_y[:], ALU.mult, ALU.mult))
                nc.vector.tensor_scalar(ve[:, k:k + 1], ve[:, k:k + 1], EPS, None, ALU.add).then_inc(var_ok, 1)

            def last_norm_end(t):
                k = t % 2
                dve.wait_ge(std_ok, t + 1)
                link(nc.vector.reciprocal(rs[:, k:k + 1], sd[:, k:k + 1]))
                link(nc.vector.tensor_scalar(rs[:, k:k + 1], rs[:, k:k + 1], K.k_y[:], None, ALU.mult))
                wait(dve, o_out[k], t // 2 * 16)
                nc.vector.tensor_scalar(z[:, k, :], y[:, t, :], mv[:, k, 0:1], rs[:, k:k + 1],
                                        ALU.subtract, ALU.mult).then_inc(z_ok, 1)

            groups(dve, body)
            last_norm_end(NT - 1)

        @block.gpsimd
        def _(pool):
            for t in range(NT):
                k = t % 2
                pool.wait_ge(z_ok, t + 1)
                pool.wait_ge(x1_in[k], t // 2 * 16 + 16)
                nc.gpsimd.tensor_tensor(z[:, k, :], z[:, k, :], x1[:, k, :], ALU.add).then_inc(o_ok, 1)


class Shared:
    pass


def build(nc, x, wqkv, wo, szs, gu_q, gu_sz, down_q, down_sz, ropes, x1_dram, out):
    K = Shared()
    with ExitStack() as ctx:
        sb = lambda n, s, d: ctx.enter_context(nc.sbuf_tensor(n, s, d))
        K.ident = sb("ident", [P, P], F16)
        K.identb = sb("identb", [P, P], BF16)
        K.maskb = sb("maskb", [P, P], BF16)
        K.ln_ps = sb("ln_ps", [P, 1], F32)
        K.sc = sb("sc", [P, 8], F32)
        K.inv = sb("inv", [P, 8], F32)
        K.k_score, K.k_att, K.k_y, K.k_gate, K.k_h = (sb(n, [P, 1], F32) for n in
                                                      ("k_score", "k_att", "k_y", "k_gate", "k_h"))
        K.xT = sb("xT", [P, 2, NC, TOK], F16)
        phase_scales_and_norm(nc, K, x, wqkv, wo, szs)
        with nc.sbuf_tensor("ctxT", [P, 2, NC, TOK], F16) as ctxT:
            K.ctxT = ctxT
            phase_attention(nc, K, wqkv, ropes)
            phase_output(nc, K, x, wo, x1_dram)
        phase_ffn(nc, K, gu_q, gu_sz, down_q, down_sz, x1_dram, out)


def rope_tables():
    f = np.float32
    inv = (f(1.0) / np.power(f(500000.0), np.arange(0, DH, 2, dtype=f) / f(DH))).astype(f)
    wavelen = (f(2.0 * np.pi) / inv).astype(f)
    scaled = np.where(wavelen > f(2048), inv / f(32.0), inv).astype(f)
    smooth = ((f(2048) / wavelen - f(1.0)) / f(3.0)).astype(f)
    smoothed = ((f(1.0) - smooth) * scaled / f(32.0) + smooth * scaled).astype(f)
    scaled = np.where(~(wavelen < 2048) & ~(wavelen > 512), smoothed, scaled).astype(f)
    ang = (np.arange(T, dtype=f)[:, None] * scaled[None]).astype(f)
    cos, sin = np.cos(ang), np.sin(ang)
    full = np.stack([np.concatenate([cos, cos], 1), np.concatenate([-sin, sin], 1)])
    return np.ascontiguousarray(full.reshape(2, UT, P, DH).transpose(2, 0, 1, 3)).astype(f)


def chunked():
    starts = range(0, INTER, GROUP_I)
    return [np.arange(s + c, min(s + GROUP_I, INTER), 2) for s in starts for c in range(2)]


def kernel(**inputs):
    import concourse.bacc as _bacc
    from concourse.bass_utils import run_bass_kernel_spmd as _run

    a = {k[3:]: np.asarray(v) for k, v in inputs.items()}
    kv = lambda w, n: w.reshape(KVH, n * DH, E)
    w = np.concatenate([kv(a["attn_Wq"], GQ), kv(a["attn_Wk"], 1), kv(a["attn_Wv"], 1)], 1)
    wqkv = w.reshape(KVH, WCOL, NC, P).transpose(0, 3, 2, 1)
    wo = a["attn_Wo"].T.reshape(NC, P, E).transpose(1, 0, 2).reshape(P, NC * E)
    order = chunked()
    gu_q = np.concatenate([a["ffn_" + m + "_Wq"][i].T for i in order for m in ("gate", "up")], 1)
    gu_sz = np.concatenate([a["ffn_" + m][i].T for i in order
                            for m in ("gate_scale", "gate_zero", "up_scale", "up_zero")], 1)
    down_sz = np.stack([a["ffn_down_scale"].T, a["ffn_down_zero"].T], 1)
    arrays = {
        "x": a["attn_x"].reshape(TOK, E), "wqkv": wqkv, "wo": wo, "gu_q": gu_q, "gu_sz": gu_sz,
        "down_q": a["ffn_down_Wq"].T, "down_sz": down_sz, "ropes": rope_tables(),
    }
    for m in ("gate", "up", "down"):
        for s in ("scale", "zero"):
            arrays[f"{m}_{s}"] = a[f"ffn_{m}_{s}"].reshape(P, -1)
    arrays = {"in_" + k: np.ascontiguousarray(v) for k, v in arrays.items()}

    nc = _bacc.Bacc("TRN2", target_bir_lowering=False, num_devices=1)
    d = {k[3:]: nc.dram_tensor(k, v.shape, mybir.dt.from_np(v.dtype), kind="ExternalInput").ap()
         for k, v in arrays.items()}
    x1 = nc.dram_tensor("x1_rows", (TOK, E), F32, kind="Internal").ap()
    out = nc.dram_tensor("out_rows", (TOK, E), F32, kind="ExternalOutput").ap()
    szs = [d[f"{m}_{s}"] for m in ("gate", "up", "down") for s in ("scale", "zero")]
    build(nc, d["x"], d["wqkv"], d["wo"], szs, d["gu_q"], d["gu_sz"], d["down_q"], d["down_sz"], d["ropes"], x1, out)
    r = _run(nc, [arrays], core_ids=[0])
    return r.results[0]["out_rows"].reshape(BATCH, T, E)
```

```python
import numpy as np
import concourse.bass as bass
from concourse import mybir
from contextlib import ExitStack

F32 = mybir.dt.float32
F16 = mybir.dt.float16
BF16 = mybir.dt.bfloat16
I32 = mybir.dt.int32
ACT = mybir.ActivationFunctionType
ALU = mybir.AluOpType
AX = mybir.AxisListType

P = 128
BATCH, T, E = 2, 1024, 1024
TOK = BATCH * T
NT = TOK // P
NC = E // P
HEADS, KVH, DH = 32, 8, 32
GQ = HEADS // KVH
UT = T // P
QW = GQ * P
WCOL = (GQ + 2) * DH
INTER = 2752
GROUPS, GROUP_I = INTER // 256, 256
LASTW = (INTER - GROUPS * GROUP_I) // 2
EPS = 1e-5
XS = 1024.0
QS = 2.0 ** -24
MS = 2.0 ** 15
PS_LOG = 14 * float(np.log(2.0))
HS = 2.0 ** -45
SQ, SK, SV, SO, SG, SU, SD = range(7)
MASKED = -3.0e38


def wait(eng, sem, value):
    if isinstance(value, int) and value <= 0:
        return
    eng.wait_ge(sem, value)


def apart(eng, sem):
    eng.sem_inc(sem, 1)


def loop(eng, first, last, body):
    body(first)
    if last - first > 1:
        with eng.Fori(first + 1, last) as r:
            body(r)
    body(last)


WO_PIECE = NC * E // KVH


def phase_scales_and_norm(nc, K, x, wqkv, wo, szs):
    with ExitStack() as ctx:
        sb = lambda n, s, d: ctx.enter_context(nc.sbuf_tensor(n, s, d))
        sem = lambda n: ctx.enter_context(nc.semaphore(n))
        wtmp = sb("a_wtmp", [P, 2, NC * WCOL], F32)
        otmp = sb("a_otmp", [P, 2, WO_PIECE], F32)
        ztmp = sb("a_ztmp", [P, 6, 344], F32)
        zab = sb("a_zab", [P, 344], F32)
        part = sb("a_part", [P, 4, 8], F32)
        own = sb("a_own", [P, 8], F32)
        allm = sb("a_allm", [P, 8], F32)
        ebits = sb("a_ebits", [P, 8], I32)
        tmp1 = sb("a_tmp1", [P, 1], F32)
        tmp2 = sb("a_tmp2", [P, 1], F32)
        xin = sb("a_xin", [P, 4, E], F32)
        xn = sb("a_xn", [P, 2, E], F32)
        xhl = sb("a_xhl", [P, 2, 2, E], F16)
        st6 = sb("a_st6", [P, 2, 2, 6], F32)
        mv = sb("a_mv", [P, 2, 2], F32)
        ve = sb("a_ve", [P, 2], F32)
        sd = sb("a_sd", [P, 2], F32)
        rs = sb("a_rs", [P, 2], F32)
        pt = [[ctx.enter_context(nc.psum_tensor(f"a_pt{s}{h}", [P, NC, P], F16)) for h in range(2)]
              for s in range(2)]
        w_in = [sem("a_w_in0"), sem("a_w_in1")]
        o_in = [sem("a_o_in0"), sem("a_o_in1")]
        w_used, o_used = sem("a_w_used"), sem("a_o_used")
        z_in = sem("a_z_in")
        x_in = [sem(f"a_x_in{k}") for k in range(4)]
        s_const = sem("a_const")
        s_bound = sem("a_bound")
        s_allmax = sem("a_allmax")
        s_chain = sem("a_chain")
        s_stats = sem("a_stats")
        s_apart = sem("a_apart")
        s_var = sem("a_var")
        s_std = sem("a_std")
        s_rstd = sem("a_rstd")
        s_xn = sem("a_xn_done")
        s_hi = sem("a_hi")
        s_lo = sem("a_lo")
        s_tr = sem("a_tr")
        s_ev_hi = sem("a_ev_hi")
        s_ev_lo = sem("a_ev_lo")
        xv = x.rearrange("(n p) e -> n p e", p=P)
        block = ctx.enter_context(nc.Block())


        @block.sync
        def _(sp):
            def body(r):
                for i in range(4):
                    n = r * 4 + i
                    wait(sp, s_xn, n - 3)
                    sp.dma_start(xin[:, i, :], xv[bass.ds(n, 1)].rearrange("a p e -> p (a e)"))\
                        .then_inc(x_in[i], 16)
                    g, k = r * 2 + i // 2, i // 2
                    if i % 2 == 0:
                        wait(sp, w_used, g - 1)
                        sp.dma_start(wtmp[:, k, :], wqkv[bass.ds(g, 1)].rearrange("a p c n -> p (a c n)"))\
                            .then_inc(w_in[k], 16)
                    else:
                        wait(sp, o_used, g - 1)
                        sp.dma_start(otmp[:, k, :], wo[:, bass.ds(g * WO_PIECE, WO_PIECE)]).then_inc(o_in[k], 16)
            body(0)
            for i, sz in enumerate(szs):
                sp.dma_start(ztmp[:, i, :], sz).then_inc(z_in, 16)
            with sp.Fori(1, NT // 4) as r:
                body(r)

        @block.gpsimd
        def _(pool):
            nc.gpsimd.memset(K.ident[:], 0.0).then_inc(s_const, 1)
            nc.gpsimd.memset(K.identb[:], 0.0).then_inc(s_const, 1)
            nc.gpsimd.memset(K.maskb[:], 0.0).then_inc(s_const, 1)
            nc.gpsimd.memset(K.ln_ps[:], PS_LOG)
            pool.wait_ge(s_const, 3)
            for m in (K.ident, K.identb):
                nc.gpsimd.affine_select(out=m[:], in_=m[:], compare_op=ALU.not_equal, fill=1.0, base=0,
                                        pattern=[[-1, P]], channel_multiplier=1).then_inc(s_const, 1)
            nc.gpsimd.affine_select(out=K.maskb[:], in_=K.maskb[:], compare_op=ALU.is_ge, fill=MASKED, base=0,
                                    pattern=[[-1, P]], channel_multiplier=1).then_inc(s_const, 1)
            pool.wait_ge(s_bound, 1)
            nc.gpsimd.partition_all_reduce(allm[:, 0:7], own[:, 0:7], P, bass.bass_isa.ReduceOp.max)\
                .then_inc(s_allmax, 1)

        @block.vector
        def _(dve):
            links = [0]

            def link(ins):
                links[0] += 1
                ins.then_inc(s_chain, 1)
                dve.wait_ge(s_chain, links[0])

            def stats(n, i, r):
                k = i % 2
                dve.wait_ge(x_in[i], (r + 1) * 16)
                wait(dve, s_xn, n - 1)
                for h in range(2):
                    nc.vector.bn_stats(st6[:, k, h, :], xin[:, i, h * 512:(h + 1) * 512]).then_inc(s_stats, 1)
                dve.wait_ge(s_stats, n * 3 + 2)
                apart(dve, s_apart)
                nc.vector.bn_aggr(mv[:, k, :], st6[:, k, :, :]).then_inc(s_stats, 1)
                dve.wait_ge(s_stats, n * 3 + 3)
                nc.vector.tensor_scalar(ve[:, k:k + 1], mv[:, k, 1:2], EPS, None, ALU.add).then_inc(s_var, 1)

            def scale_rows(n, i):
                k = i % 2
                dve.wait_ge(s_std, n + 1)
                nc.vector.reciprocal(rs[:, k:k + 1], sd[:, k:k + 1]).then_inc(s_rstd, 1)
                dve.wait_ge(s_rstd, n + 1)
                wait(dve, s_hi, n - 1)
                wait(dve, s_lo, n - 1)
                nc.vector.tensor_scalar(xn[:, k, :], xin[:, i, :], mv[:, k, 0:1], rs[:, k:k + 1],
                                        ALU.subtract, ALU.mult).then_inc(s_xn, 1)

            def low(n, k):
                dve.wait_ge(s_hi, n + 1)
                wait(dve, s_tr, n * 2 - 2)
                nc.vector.tensor_tensor(xhl[:, k, 1, :], xn[:, k, :], xhl[:, k, 0, :], ALU.subtract)\
                    .then_inc(s_lo, 1)

            def bounds(g, k, r):
                dve.wait_ge(w_in[k], 16 * (r + 1))
                w = wtmp[:, k, :].rearrange("p (c n) -> p c n", c=NC)
                for m, (a, b) in enumerate(((0, P), (P, P + DH), (P + DH, WCOL))):
                    last = nc.vector.tensor_reduce(part[:, m, bass.ds(g, 1)], w[:, :, a:b], AX.XY, ALU.max,
                                                   apply_absolute_value=True)
                last.then_inc(w_used, 1)
                dve.wait_ge(o_in[k], 16 * (r + 1))
                nc.vector.tensor_reduce(part[:, 3, bass.ds(g, 1)], otmp[:, k, :], AX.X, ALU.max,
                                        apply_absolute_value=True).then_inc(o_used, 1)

            def body(r):
                for i in range(4):
                    n = r * 4 + i
                    stats(n, i, r)
                    if not isinstance(n, int) or n > 0:
                        low(n - 1, (i + 1) % 2)
                    if i % 2:
                        bounds(r * 2 + i // 2, i // 2, r)
                    scale_rows(n, i)

            loop(dve, 0, NT // 4 - 1, body)
            low(NT - 1, 1)
            dve.wait_ge(w_used, KVH)
            dve.wait_ge(o_used, KVH)
            nc.vector.tensor_reduce(own[:, 0:4], part[:], AX.X, ALU.max)
            dve.wait_ge(z_in, 96)
            for m in range(3):
                zero = ztmp[:, 2 * m + 1, :]
                link(nc.vector.scalar_tensor_tensor(zab[:], zero, -1.0, zero, ALU.mult, ALU.max))
                link(nc.vector.scalar_tensor_tensor(zab[:], zab[:], 15.0, ztmp[:, 2 * m, :], ALU.add, ALU.mult))
                link(nc.vector.tensor_reduce(own[:, 4 + m:5 + m], zab[:], AX.X, ALU.max,
                                             apply_absolute_value=True))
            nc.vector.tensor_scalar(tmp1[:], zab[:, 0:1], 0.0, None, ALU.mult).then_inc(s_bound, 1)
            dve.wait_ge(s_allmax, 1)
            link(nc.vector.tensor_scalar(ebits[:, 0:7], allm[:, 0:7].bitcast(I32), 0x7F800000, None,
                                         ALU.bitwise_and))
            link(nc.vector.tensor_scalar(ebits[:, 0:7], ebits[:, 0:7], float(27 << 23), None, ALU.max))
            link(nc.vector.tensor_scalar(K.sc[:, 0:7].bitcast(I32), ebits[:, 0:7], -1.0, float(268 << 23),
                                         ALU.mult, ALU.add))
            link(nc.vector.tensor_scalar(K.inv[:, 0:7].bitcast(I32), ebits[:, 0:7], float(14 << 23), None,
                                         ALU.subtract))

            def product(out, a, ca, b, cb):
                link(nc.vector.tensor_scalar(tmp1[:], a, ca, None, ALU.mult))
                link(nc.vector.tensor_scalar(tmp2[:], b, cb, None, ALU.mult))
                link(nc.vector.tensor_tensor(out, tmp1[:], tmp2[:], ALU.mult))

            col = lambda t, i: t[:, i:i + 1]
            product(K.k_score[:], col(K.inv, SQ), 2.0 ** 14 / float(np.sqrt(np.float32(DH))), col(K.inv, SK), 2.0 ** 14)
            product(K.k_att[:], col(K.inv, SV), 2.0 ** 14, col(K.inv, SO), 1.0)
            product(K.k_y[:], col(K.inv, SG), 2.0 ** 17, col(K.inv, SU), 2.0 ** 18)
            link(nc.vector.tensor_tensor(K.k_y[:], K.k_y[:], col(K.inv, SD), ALU.mult))
            link(nc.vector.tensor_scalar(K.k_gate[:], col(K.inv, SG), 1.0 / XS, None, ALU.mult))
            link(nc.vector.tensor_scalar(K.k_h[:], col(K.sc, SG), HS, None, ALU.mult))

        @block.scalar
        def _(act):
            def copy_out(n, k, h):
                act.wait_ge(s_tr, n * 2 + h + 1)
                nc.scalar.activation(K.xT[:, h, :, bass.ds(n * P, P)], pt[k][h][:], ACT.Copy)\
                    .then_inc((s_ev_hi, s_ev_lo)[h], 1)

            def body(r):
                for i in range(4):
                    n, k = r * 4 + i, i % 2
                    act.wait_ge(s_var, n + 1)
                    wait(act, s_rstd, n - 1)
                    nc.scalar.activation(sd[:, k:k + 1], ve[:, k:k + 1], ACT.Sqrt, scale=XS ** -2).then_inc(s_std, 1)
                    before = not isinstance(n, int) or n > 0
                    if before:
                        copy_out(n - 1, 1 - k, 0)
                    act.wait_ge(s_xn, n + 1)
                    wait(act, s_tr, n * 2 - 3)
                    wait(act, s_lo, n - 1)
                    nc.scalar.activation(xhl[:, k, 0, :], xn[:, k, :], ACT.Copy).then_inc(s_hi, 1)
                    if before:
                        copy_out(n - 1, 1 - k, 1)

            loop(act, 0, NT // 4 - 1, body)
            copy_out(NT - 1, 1, 0)
            copy_out(NT - 1, 1, 1)

        @block.tensor
        def _(pe):
            pe.wait_ge(s_const, 6)

            def tile(n, k):
                for h in range(2):
                    pe.wait_ge((s_hi, s_lo)[h], n + 1)
                    wait(pe, (s_ev_hi, s_ev_lo)[h], n - 1)
                    for c in range(NC):
                        last = nc.tensor.transpose(pt[k][h][:, c, :], xhl[:, k, h, c * P:(c + 1) * P], K.ident[:])
                    last.then_inc(s_tr, 1)

            tile(0, 0)
            tile(1, 1)
            with pe.Fori(1, NT // 2) as r:
                tile(r * 2, 0)
                tile(r * 2 + 1, 1)


BT, BB = 2 * UT, 72
RING = 8
QSLOTS = 8
LEAD = 31
PROJ_SPAN = 69
NAT_HI, NAT_LO, STACK = 2, 2, 5
MAX_LEAD = 12
ROW_LAG = 3
AV_LAG, NORM_LAG, HI_LAG, LO_LAG, CTX_LAG = 5, 6, 7, 8, 10


def base(l):
    return 36 * (l // UT) + (l % UT) * (l % UT + 1) // 2


def tile_of(s):
    l = 8 * (s // 36)
    while base(l + 1) <= s:
        l += 1
    return l


def last_of(s, lag):
    l = tile_of(s - lag)
    return l if base(l + 1) - 1 == s - lag else None


def window(l):
    at = BB * (l // BT) - LEAD
    return at + l % BT * PROJ_SPAN // BT, at + (l % BT + 1) * PROJ_SPAN // BT


def tiles_with(s, after):
    return [l for l in range(-BT, 3 * BT) if window(l)[1] == s - after]


def chunks_at(s):
    for l in range(-BT, 3 * BT):
        a, b = window(l)
        if a <= s < b:
            return l, [c for c in range(NC) if a + c * (b - a) // NC == s]
    return None, []


def weights_change(s):
    q, j = divmod(s + LEAD - PROJ_SPAN, BB)
    return q + 1 if j == 0 else None


def has_tile(r, l):
    return not isinstance(r, int) or 0 <= BT * r + l < BT * KVH


def has_block(r, s):
    return not isinstance(r, int) or 0 <= BB * r + s < BB * KVH


def key_tile(s):
    l = tile_of(s)
    return l % UT if s == base(l) else s - base(l) - 1


def shared_bank(r, s):
    uses = [("stack", l) for l in tiles_with(s, STACK)]
    uses += [("rows", l) for l in [last_of(s + MAX_LEAD - ROW_LAG, 0)] if l is not None]
    uses += [("ctx", l) for l in [last_of(s, CTX_LAG)] if l is not None]
    return [(kind, l) for kind, l in uses if has_tile(r, l)]


def use_before(r, s, kind, l):
    uses = shared_bank(r, s)
    i = uses.index((kind, l))
    if i:
        return uses[i - 1]
    for p in range(s - 1, s - BB, -1):
        if shared_bank(r, p):
            return shared_bank(r, p)[-1]
    return None


def phase_attention(nc, K, wqkv, ropes):
    with ExitStack() as ctx:
        sb = lambda n, s, d: ctx.enter_context(nc.sbuf_tensor(n, s, d))
        ps = lambda n, s, d: ctx.enter_context(nc.psum_tensor(n, s, d))
        sem = lambda n: ctx.enter_context(nc.semaphore("b_" + n))
        rope = sb("b_rope", [P, 2, UT, DH], F32)
        wraw = sb("b_wraw", [P, NC, WCOL], F32)
        wcur = sb("b_wcur", [P, 2, NC, WCOL], F16)
        qkv = sb("b_qkv", [P, 2, WCOL], F32)
        t1 = sb("b_t1", [P, GQ + 1, DH], F32)
        t2 = sb("b_t2", [P, GQ + 1, DH], F32)
        rot = sb("b_rot", [P, 2, GQ + 1, DH], F32)
        nat = sb("b_nat", [P, 2, GQ + 1, 3 * DH], F16)
        qst = sb("b_qst", [P, QSLOTS, QW], F16)
        kst = sb("b_kst", [P, 2, T], F16)
        vaug = sb("b_vaug", [P, 2, UT, 66], F16)
        mpart = sb("b_mpart", [P, 2, GQ, UT], F32)
        negm = sb("b_negm", [P, 2, GQ], F32)
        maug = sb("b_maug", [P, 2, GQ, 2], F16)
        p32 = sb("b_p32", [P, RING, QW], F32)
        phi = sb("b_phi", [P, RING, QW], F16)
        plo = sb("b_plo", [P, RING, QW], F16)
        num = sb("b_num", [P, GQ, DH], F32)
        rden = sb("b_rden", [P, GQ, 1], F32)
        c32 = sb("b_c32", [P, 2, P], F32)
        chl = sb("b_chl", [P, 2, 2, P], F16)
        ST = [ps(f"b_st{i}", [P, QW], F32) for i in range(3)]
        M = [ps(f"b_m{i}", [P, QW], F32) for i in range(2)]
        AV = ps("b_av", [P, 512], F32)
        PR = ps("b_pr", [P, 512], F32)
        TB = ps("b_tb", [P, 1024], F16)
        apart_pool = sem("apart")
        rope_in, const_ok = sem("rope_in"), sem("const_ok")
        w_in, w_hi, w_ready = sem("w_in"), sem("w_hi"), sem("w_ready")
        p_done, p_evac = sem("p_done"), sem("p_evac")
        rope_st, rope_done = sem("rope_st"), sem("rope_done")
        v_hi, v_ready = sem("v_hi"), sem("v_ready")
        nat_hi, nat_ready = sem("nat_hi"), sem("nat_ready")
        stack_t, stack_evac = sem("stack_t"), sem("stack_evac")
        m_mm, m_red, m_all = sem("m_mm"), sem("m_red"), sem("m_all")
        maug_hi, maug_ready = sem("maug_hi"), sem("maug_ready")
        rows_t, rows_evac = sem("rows_t"), sem("rows_evac")
        st_done, exp_done, mask_done = sem("st_done"), sem("exp_done"), sem("mask_done")
        hi_act, hi_dve, lo_dve, lo_pool = sem("hi_act"), sem("hi_dve"), sem("lo_dve"), sem("lo_pool")
        av_done, norm_in, norm_done = sem("av_done"), sem("norm_in"), sem("norm_done")
        ctx_hi, ctx_lo, ctx_t, ctx_evac = sem("ctx_hi"), sem("ctx_lo"), sem("ctx_t"), sem("ctx_evac")
        block = ctx.enter_context(nc.Block())

        def lo_count(r, s):
            return lo_dve if s % 2 == 0 else lo_pool, r * (BB // 2) + s // 2 + 1

        def positions(eng, position):
            for s in range(PROJ_SPAN - LEAD - BB, 0):
                position(0, s)

            def body(r):
                for s in range(BB):
                    position(r, s)
            loop(eng, 0, KVH - 1, body)
            for s in range(BB, BB + CTX_LAG):
                position(KVH - 1, s)

        @block.sync
        def _(sp):
            sp.dma_start(rope[:], ropes).then_inc(rope_in, 16)

            def load(r):
                wait(sp, w_ready, r)
                sp.dma_start(wraw[:], wqkv[bass.ds(r, 1)].rearrange("a p c n -> p (a c) n")).then_inc(w_in, 16)
            load(0)
            with sp.Fori(1, KVH) as r:
                load(r)

        @block.tensor
        def _(pe):
            pe.wait_ge(const_ok, 2)

            def project(r, l, cs):
                if cs[0] == 0:
                    pe.wait_ge(w_ready, r + l // BT + 1)
                    wait(pe, p_evac, r * BT + l)
                t0 = (l // UT) % 2 * T + l % UT * P
                for c in cs:
                    for x, w in ((0, 0), (0, 1), (1, 0)):
                        last = nc.tensor.matmul(PR[:, 0:WCOL], K.xT[:, x, c, t0:t0 + P], wcur[:, w, c, :],
                                                start=(c == 0 and x == 0 and w == 0),
                                                stop=(c == NC - 1 and x == 1))
                if cs[-1] == NC - 1:
                    last.then_inc(p_done, 1)

            def scores_for_max(r, m):
                l, kt = tile_of(m), key_tile(m)
                diagonal = m == base(l)
                if diagonal:
                    pe.wait_ge(stack_evac, r * BT + l + 1)
                wait(pe, m_red, r * BB + m - 1)
                for h in range(GQ):
                    last = nc.tensor.matmul(M[m % 2][:, h * P:(h + 1) * P], qst[0:96, l % QSLOTS, h * P:(h + 1) * P],
                                            kst[0:96, (l // UT) % 2, kt * P:(kt + 1) * P],
                                            start=True, stop=not diagonal)
                    if diagonal:
                        last = nc.tensor.matmul(M[m % 2][:, h * P:(h + 1) * P], K.identb[:], K.maskb[:],
                                                start=False, stop=True)
                last.then_inc(m_mm, 1)

            def bank_free(r, s, kind, l):
                before = use_before(r, s, kind, l)
                if before is not None:
                    evac = {"stack": stack_evac, "rows": rows_evac, "ctx": ctx_evac}[before[0]]
                    pe.wait_ge(evac, r * BT + before[1] + 1)

            def max_rows(r, s, l):
                pe.wait_ge(maug_ready, r * BT + l + 1)
                bank_free(r, s, "rows", l)
                for h in range(GQ):
                    last = nc.tensor.transpose(TB[96:98, h * P:(h + 1) * P], maug[:, l % 2, h, :], K.ident[:])
                last.then_inc(rows_t, 1)

            def stack(r, s, l):
                pe.wait_ge(nat_ready, r * BT + l + 1)
                bank_free(r, s, "stack", l)
                for h in range(GQ + 1):
                    last = nc.tensor.transpose(TB[0:96, h * P:(h + 1) * P], nat[:, l % 2, h, :], K.ident[:])
                last.then_inc(stack_t, 1)

            def transpose_context(r, s, l):
                pe.wait_ge(ctx_lo, r * BT + l + 1)
                bank_free(r, s, "ctx", l)
                for x in range(2):
                    last = nc.tensor.transpose(TB[:, x * P:(x + 1) * P], chl[:, l % 2, x, :], K.ident[:])
                last.then_inc(ctx_t, 1)

            def scores(r, s):
                l = tile_of(s)
                if s == base(l):
                    pe.wait_ge(rows_evac, r * BT + l + 1)
                wait(pe, exp_done, r * BB + s - 2)
                kt = key_tile(s)
                nc.tensor.matmul(ST[s % 3][:], kst[0:98, (l // UT) % 2, kt * P:(kt + 1) * P],
                                 qst[0:98, l % QSLOTS, :], start=True, stop=True).then_inc(st_done, 1)

            def weigh(r, s):
                l = tile_of(s)
                first, final = s == base(l), s == base(l + 1) - 1
                if first:
                    pe.wait_ge(v_ready, r * BT + l + 1)
                    wait(pe, norm_in, (r * BT + l) * 2)
                pe.wait_ge(*lo_count(r, s))
                v = vaug[:, (l // UT) % 2, key_tile(s), :]
                for h in range(GQ):
                    a = h * 65
                    nc.tensor.matmul(AV[:, a:a + 65], phi[:, s % RING, h * P:(h + 1) * P], v[:, 0:65],
                                     start=(first and h == 0), stop=False, skip_group_check=True)
                    last = nc.tensor.matmul(AV[:, a + 32:a + 65], plo[:, s % RING, h * P:(h + 1) * P], v[:, 32:65],
                                            start=False, stop=(final and h == GQ - 1), skip_group_check=True)
                last.then_inc(av_done, 1)

            def position(r, s):
                if has_block(r, s):
                    scores(r, s)
                uses = shared_bank(r, s)
                for kind, l in uses:
                    if kind == "stack":
                        stack(r, s, l)
                if has_block(r, s + MAX_LEAD):
                    scores_for_max(r, s + MAX_LEAD)
                for kind, l in uses:
                    if kind == "rows":
                        max_rows(r, s, l)
                if has_block(r, s - AV_LAG):
                    weigh(r, s - AV_LAG)
                l, cs = chunks_at(s)
                if cs and has_tile(r, l):
                    project(r, l, cs)
                for kind, l in uses:
                    if kind == "ctx":
                        transpose_context(r, s, l)

            positions(pe, position)

        @block.scalar
        def _(act):
            def split_w(r):
                act.wait_ge(w_in, (r + 1) * 16)
                wait(act, p_done, r * BT)
                for (a, b), m in zip(((0, P), (P, P + DH), (P + DH, WCOL)), (SQ, SK, SV)):
                    last = nc.scalar.activation(wcur[:, 0, :, a:b], wraw[:, :, a:b], ACT.Copy, scale=K.sc[:, m:m + 1])
                last.then_inc(w_hi, 1)

            def copy_projection(r, l):
                act.wait_ge(p_done, r * BT + l + 1)
                wait(act, rope_done, r * BT + l - 1)
                wait(act, v_ready, r * BT + l - 1)
                nc.scalar.activation(qkv[:, l % 2, :], PR[:, 0:WCOL], ACT.Copy, scale=QS).then_inc(p_evac, 1)

            def exps(r, s):
                act.wait_ge(st_done, r * BB + s + 1)
                wait(act, *lo_count(r, s - RING))
                nc.scalar.activation(p32[:, s % RING, :], ST[s % 3][:], ACT.Exp, bias=PS_LOG,
                                     scale=K.k_score[:]).then_inc(exp_done, 1)

            def copy_shared(r, kind, l):
                if kind == "stack":
                    act.wait_ge(stack_t, r * BT + l + 1)
                    wait(act, st_done, r * BB + max(base(l - QSLOTS + 1), 36 * (l // UT - 1)))
                    nc.scalar.activation(qst[0:96, l % QSLOTS, :], TB[0:96, 0:QW], ACT.Copy)
                    nc.scalar.activation(kst[0:96, (l // UT) % 2, l % UT * P:l % UT * P + P],
                                         TB[0:96, QW:QW + P], ACT.Copy).then_inc(stack_evac, 1)
                elif kind == "rows":
                    act.wait_ge(rows_t, r * BT + l + 1)
                    nc.scalar.activation(qst[96:98, l % QSLOTS, :], TB[96:98, 0:QW], ACT.Copy).then_inc(rows_evac, 1)
                else:
                    act.wait_ge(ctx_t, r * BT + l + 1)
                    t0 = (l // UT) % 2 * T + l % UT * P
                    dst = K.ctxT[:, :, bass.ds(r + l // BT, 1), t0:t0 + P].rearrange("p x a t -> p x (a t)")
                    nc.scalar.activation(dst, TB[:, 0:2 * P].rearrange("p (x t) -> p x t", x=2), ACT.Copy)\
                        .then_inc(ctx_evac, 1)

            def high_half(r, s):
                l = tile_of(s)
                if s % 2 == 0:
                    act.wait_ge(exp_done, r * BB + s + 1)
                    if s == base(l):
                        act.wait_ge(mask_done, r * BT + l + 1)
                    wait(act, av_done, r * BB + s + 1 - RING)
                    nc.scalar.activation(phi[:, s % RING, :], p32[:, s % RING, :], ACT.Copy).then_inc(hi_act, 1)

            def position(r, s):
                for l in tiles_with(s, 0):
                    if has_tile(r, l):
                        copy_projection(r, l)
                masked = s - 1 == base(tile_of(s - 1))
                if has_block(r, s - 1) and not masked:
                    high_half(r, s - 1)
                if has_block(r, s):
                    exps(r, s)
                uses = shared_bank(r, s)
                for kind, l in uses:
                    if kind != "ctx":
                        copy_shared(r, kind, l)
                if has_block(r, s - 1) and masked:
                    high_half(r, s - 1)
                for l in tiles_with(s, NAT_HI):
                    if has_tile(r, l):
                        n = r * BT + l
                        act.wait_ge(rope_done, n + 1)
                        wait(act, stack_t, n - 1)
                        src, dst = rot[:, l % 2, :, :], nat[:, l % 2, :, :]
                        hi2 = dst[:, 0:GQ, :].rearrange("p h (x d) -> p h x d", x=3)[:, :, 0:3:2, :]
                        nc.scalar.activation(hi2, src[:, 0:GQ, None, :].broadcast_to([P, GQ, 2, DH]), ACT.Copy)
                        nc.scalar.activation(dst[:, GQ, 0:2 * DH].rearrange("p (x d) -> p x d", x=2),
                                             src[:, GQ, None, :].broadcast_to([P, 2, DH]), ACT.Copy)\
                            .then_inc(nat_hi, 1)
                l = last_of(s, HI_LAG)
                if l is not None and has_tile(r, l):
                    act.wait_ge(norm_done, r * BT + l + 1)
                    wait(act, ctx_t, r * BT + l - 1)
                    nc.scalar.activation(chl[:, l % 2, 0, :], c32[:, l % 2, :], ACT.Copy).then_inc(ctx_hi, 1)
                for kind, l in uses:
                    if kind == "ctx":
                        copy_shared(r, kind, l)
                q = weights_change(s)
                if q is not None and has_tile(r, q * BT):
                    split_w(r + q)

            positions(act, position)

        @block.vector
        def _(dve):
            def split_w(r):
                dve.wait_ge(w_hi, r + 1)
                for (a, b), m in zip(((0, P), (P, P + DH), (P + DH, WCOL)), (SQ, SK, SV)):
                    last = nc.vector.scalar_tensor_tensor(wcur[:, 1, :, a:b], wraw[:, :, a:b], K.sc[:, m:m + 1],
                                                          wcur[:, 0, :, a:b], ALU.mult, ALU.subtract)
                last.then_inc(w_ready, 1)

            def context_sums(r, l):
                dve.wait_ge(av_done, r * BB + base(l + 1))
                wait(dve, norm_done, r * BT + l)
                av = AV[:, 0:4 * 65].rearrange("p (h c) -> p h c", h=GQ)
                nc.vector.tensor_reduce(num[:], av[:, :, 0:64].rearrange("p h (x d) -> p h d x", x=2),
                                        AX.X, ALU.add).then_inc(norm_in, 1)
                nc.vector.reciprocal(rden[:], av[:, :, 64:65]).then_inc(norm_in, 1)

            def normalise(r, l):
                n = r * BT + l
                dve.wait_ge(norm_in, (n + 1) * 2)
                wait(dve, ctx_hi, n - 1)
                wait(dve, ctx_lo, n - 1)
                nc.vector.tensor_tensor(c32[:, l % 2, :].rearrange("p (h d) -> p h d", h=GQ), num[:],
                                        rden[:].broadcast_to([P, GQ, DH]), ALU.mult).then_inc(norm_done, 1)

            def block_max(r, m):
                l = tile_of(m)
                dve.wait_ge(m_mm, r * BB + m + 1)
                if m == base(l):
                    wait(dve, m_all, r * BT + l - 1)
                nc.vector.tensor_reduce(mpart[:, l % 2, :, key_tile(m)],
                                        M[m % 2][:].rearrange("p (h c) -> p h c", h=GQ),
                                        AX.X, ALU.max).then_inc(m_red, 1)

            def tile_max(r, l):
                dve.wait_ge(m_red, r * BB + base(l + 1))
                wait(dve, maug_ready, r * BT + l - 1)
                nc.vector.tensor_reduce(negm[:, l % 2, :], mpart[:, l % 2, :, 0:l % UT + 1],
                                        AX.X, ALU.max, negate=True).then_inc(m_all, 1)

            def max_hi(r, l):
                n = r * BT + l
                dve.wait_ge(m_all, n + 1)
                wait(dve, rows_t, n - 1)
                nc.vector.tensor_scalar(maug[:, l % 2, :, 0], negm[:, l % 2, :], 1.0 / MS, None, ALU.mult)\
                    .then_inc(maug_hi, 1)

            def max_lo(r, l):
                n = r * BT + l
                dve.wait_ge(maug_hi, n + 1)
                nc.vector.scalar_tensor_tensor(maug[:, l % 2, :, 1], negm[:, l % 2, :], 1.0 / MS,
                                               maug[:, l % 2, :, 0], ALU.mult, ALU.subtract)\
                    .then_inc(maug_ready, 1)

            def p_low(r, s):
                dve.wait_ge(hi_act, r * (BB // 2) + s // 2 + 1)
                wait(dve, av_done, r * BB + s + 1 - RING)
                nc.vector.tensor_tensor(plo[:, s % RING, :], p32[:, s % RING, :], phi[:, s % RING, :],
                                        ALU.subtract).then_inc(lo_dve, 1)

            def p_high(r, s):
                l = tile_of(s)
                dve.wait_ge(exp_done, r * BB + s + 1)
                if s == base(l):
                    dve.wait_ge(mask_done, r * BT + l + 1)
                wait(dve, av_done, r * BB + s + 1 - RING)
                nc.vector.tensor_copy(phi[:, s % RING, :], p32[:, s % RING, :]).then_inc(hi_dve, 1)

            def position(r, s):
                done = last_of(s, NORM_LAG)
                done = done if done is not None and has_tile(r, done) else None
                if done is not None:
                    context_sums(r, done)
                m = s - 1 + MAX_LEAD
                if has_block(r, m):
                    block_max(r, m)
                if done is not None:
                    normalise(r, done)
                maxed = last_of(m, 0) if has_block(r, m) else None
                if maxed is not None:
                    tile_max(r, maxed)
                if has_block(r, s - 2) and s % 2 == 0:
                    p_low(r, s - 2)
                if maxed is not None:
                    max_hi(r, maxed)
                if has_block(r, s - 1) and s % 2 == 0:
                    p_high(r, s - 1)
                for l in tiles_with(s, 0):
                    if has_tile(r, l):
                        n = r * BT + l
                        dve.wait_ge(p_evac, n + 1)
                        wait(dve, av_done, r * BB + 36 * (l // UT - 1))
                        v32, va = qkv[:, l % 2, WCOL - DH:WCOL], vaug[:, (l // UT) % 2, l % UT, :]
                        nc.vector.tensor_copy(va[:, 32:64], v32).then_inc(v_hi, 1)
                if maxed is not None:
                    max_lo(r, maxed)
                for l in tiles_with(s, 0):
                    if has_tile(r, l):
                        dve.wait_ge(v_hi, r * BT + l + 1)
                        nc.vector.tensor_tensor(va[:, 0:32], v32, va[:, 32:64], ALU.subtract).then_inc(v_ready, 1)
                q = weights_change(s - 1)
                if q is not None and has_tile(r, q * BT):
                    split_w(r + q)

            positions(dve, position)

        @block.gpsimd
        def _(pool):
            nc.gpsimd.memset(kst[96:98, :, :], MS).then_inc(const_ok, 1)
            pool.wait_ge(const_ok, 1)
            nc.gpsimd.memset(vaug[:, :, :, 64:65], 1.0).then_inc(const_ok, 1)
            pool.wait_ge(rope_in, 16)

            def rotate(r, l):
                n = r * BT + l
                k, j = l % 2, l % UT
                pool.wait_ge(p_evac, n + 1)
                wait(pool, rope_done, n)
                wait(pool, nat_ready, n - 1)
                x = qkv[:, k, 0:(GQ + 1) * DH].rearrange("p (h d) -> p h d", d=DH)
                bc = lambda t, w: t[:, None, :].broadcast_to([P, GQ + 1, w])
                H = DH // 2
                nc.gpsimd.tensor_tensor(t1[:], x, bc(rope[:, 0, j, :], DH), ALU.mult)
                nc.gpsimd.tensor_tensor(t2[:, :, 0:H], x[:, :, H:DH], bc(rope[:, 1, j, 0:H], H), ALU.mult)
                nc.gpsimd.tensor_tensor(t2[:, :, H:DH], x[:, :, 0:H], bc(rope[:, 1, j, H:DH], H), ALU.mult)\
                    .then_inc(rope_st, 1)
                pool.wait_ge(rope_st, n + 1)
                nc.gpsimd.tensor_tensor(rot[:, k, :, :], t1[:], t2[:], ALU.add).then_inc(rope_done, 1)

            def position(r, s):
                l = tile_of(s)
                if has_block(r, s) and s == base(l):
                    pool.wait_ge(exp_done, r * BB + s + 1)
                    apart(pool, apart_pool)
                    d = p32[:, s % RING, :].rearrange("p (h q) -> p h q", h=GQ)
                    nc.gpsimd.affine_select(out=d, in_=d, compare_op=ALU.is_ge, fill=0.0, base=0,
                                            pattern=[[0, GQ], [1, P]], channel_multiplier=-1)\
                        .then_inc(mask_done, 1)
                if has_block(r, s - 1) and (s - 1) % 2 == 1:
                    k = (s - 1) % RING
                    pool.wait_ge(hi_dve, r * (BB // 2) + (s - 1) // 2 + 1)
                    wait(pool, av_done, r * BB + s - RING)
                    nc.gpsimd.tensor_tensor(plo[:, k, :], p32[:, k, :], phi[:, k, :], ALU.subtract)\
                        .then_inc(lo_pool, 1)
                l = last_of(s, LO_LAG)
                if l is not None and has_tile(r, l):
                    pool.wait_ge(ctx_hi, r * BT + l + 1)
                    nc.gpsimd.tensor_tensor(chl[:, l % 2, 1, :], c32[:, l % 2, :], chl[:, l % 2, 0, :],
                                            ALU.subtract).then_inc(ctx_lo, 1)
                for l in tiles_with(s, NAT_LO):
                    if has_tile(r, l):
                        pool.wait_ge(nat_hi, r * BT + l + 1)
                        k = l % 2
                        nc.gpsimd.tensor_tensor(nat[:, k, 0:GQ, DH:2 * DH], rot[:, k, 0:GQ, :],
                                                nat[:, k, 0:GQ, 0:DH], ALU.subtract)
                        nc.gpsimd.tensor_tensor(nat[:, k, GQ, 2 * DH:3 * DH], rot[:, k, GQ, :],
                                                nat[:, k, GQ, 0:DH], ALU.subtract).then_inc(nat_ready, 1)
                for l in tiles_with(s, 0):
                    if has_tile(r, l):
                        rotate(r, l)

            positions(pool, position)


def phase_output(nc, K, x, wo, x1_dram):
    with ExitStack() as ctx:
        sb = lambda n, s, d: ctx.enter_context(nc.sbuf_tensor("c_" + n, s, d))
        ps = lambda n, s, d: ctx.enter_context(nc.psum_tensor("c_" + n, s, d))
        sem = lambda n: ctx.enter_context(nc.semaphore("c_" + n))
        wraw = sb("wraw", [P, 2, 2 * E], F32)
        wohl = sb("wohl", [P, 2, NC, E], F16)
        xin = sb("xin", [P, 2, E], F32)
        z = sb("z", [P, E], F32)
        x1 = sb("x1", [P, 2, E], F32)
        xhl = sb("xhl", [P, 2, 2, E], F16)
        st6 = sb("st6", [P, 2, 6], F32)
        mv = sb("mv", [P, 2], F32)
        ve = sb("ve", [P, 1], F32)
        sd = sb("sd", [P, 1], F32)
        rs = sb("rs", [P, 1], F32)
        Y = [ps(f"y{i}", [P, E], F32) for i in range(2)]
        PT = [[ps(f"pt{s}{h}", [P, NC, P], F16) for h in range(2)] for s in range(2)]
        w_in = [sem("w_in0"), sem("w_in1")]
        w_hi, w_lo = sem("w_hi"), sem("w_lo")
        x_in = [sem("x_in0"), sem("x_in1")]
        x1_out = [sem("x1_out0"), sem("x1_out1")]
        y_mm, chain = sem("y_mm"), sem("chain")
        var_ok, std_ok = sem("var"), sem("std")
        x1_ok, xn_ok, hi_ok, lo_ok = sem("x1_ok"), sem("xn"), sem("hi"), sem("lo")
        apart_dve = sem("apart")
        tr, ev_hi, ev_lo = sem("tr"), sem("ev_hi"), sem("ev_lo")
        xv = x.rearrange("(n p) e -> n p e", p=P)
        x1v = x1_dram.rearrange("(n p) e -> n p e", p=P)
        LINKS = 14
        block = ctx.enter_context(nc.Block())

        def pair(eng, tile):
            def body(r):
                tile(r * 2, 0, r)
                tile(r * 2 + 1, 1, r)
            loop(eng, 0, NT // 2 - 1, body)

        @block.sync
        def _(sp):
            for i in range(4):
                wait(sp, w_lo, i - 1)
                sp.dma_start(wraw[:, i % 2, :], wo[:, bass.ts(i, 2 * E)]).then_inc(w_in[i % 2], 16)

            def tile(n, k, r):
                wait(sp, x1_ok, n - 1)
                sp.dma_start(xin[:, k, :], xv[bass.ds(n, 1)].rearrange("a p e -> p (a e)")).then_inc(x_in[k], 16)
                if isinstance(n, int) and n == 0:
                    return
                store(n - 1, 1 - k)

            def store(n, k):
                sp.wait_ge(x1_ok, n + 1)
                sp.dma_start(x1v[bass.ds(n, 1)].rearrange("a p e -> p (a e)"), x1[:, k, :]).then_inc(x1_out[k], 16)

            pair(sp, tile)
            store(NT - 1, 1)
            for k in range(2):
                sp.wait_ge(x1_out[k], 16 * NT // 2)

        @block.scalar
        def _(act):
            for i in range(4):
                act.wait_ge(w_in[i % 2], 16 * (i // 2 + 1))
                nc.scalar.activation(wohl[:, 0, 2 * i:2 * i + 2, :].rearrange("p c n -> p (c n)"), wraw[:, i % 2, :],
                                     ACT.Copy, scale=K.sc[:, SO:SO + 1]).then_inc(w_hi, 1)

            def copy_out(n, k):
                act.wait_ge(tr, n * 2 + 1)
                nc.scalar.activation(K.xT[:, 0, :, bass.ds(n * P, P)], PT[k][0][:], ACT.Copy).then_inc(ev_hi, 1)

            def tile(n, k, r):
                act.wait_ge(var_ok, n * 2 + 1)
                nc.scalar.activation(sd[:], ve[:], ACT.Sqrt).then_inc(std_ok, 1)
                act.wait_ge(var_ok, n * 2 + 2)
                nc.scalar.activation(sd[:], ve[:], ACT.Sqrt, scale=XS ** -2).then_inc(std_ok, 1)
                act.wait_ge(xn_ok, n + 1)
                wait(act, tr, n * 2 - 2)
                nc.scalar.activation(xhl[:, k, 0, :], z[:], ACT.Copy).then_inc(hi_ok, 1)
                if not (isinstance(n, int) and n == 0):
                    copy_out(n - 1, 1 - k)

            pair(act, tile)
            copy_out(NT - 1, 1)

        @block.tensor
        def _(pe):
            pe.wait_ge(w_lo, 4)

            def transposes(n, k):
                for h, ready, out in ((0, hi_ok, ev_hi), (1, lo_ok, ev_lo)):
                    pe.wait_ge(ready, n + 1)
                    wait(pe, out, n - 1)
                    for c in range(NC):
                        j0 = c % 4 * 2 * P + c // 4
                        last = nc.tensor.transpose(PT[k][h][:, c, :], xhl[:, k, h, j0:j0 + 2 * P - 1:2], K.ident[:])
                    last.then_inc(tr, 1)

            def tile(n, k, r):
                wait(pe, chain, (n - 1) * LINKS - 7)
                for c in range(NC):
                    for a, b in ((0, 0), (0, 1), (1, 0)):
                        for h in range(2):
                            last = nc.tensor.matmul(Y[k][:, h * 512:(h + 1) * 512],
                                                    K.ctxT[:, a, c, bass.ds(n * P, P)],
                                                    wohl[:, b, c, h * 512:(h + 1) * 512],
                                                    start=(c == 0 and a == b), stop=(c == NC - 1 and a == 1))
                last.then_inc(y_mm, 1)
                if not (isinstance(n, int) and n == 0):
                    transposes(n - 1, 1 - k)

            pair(pe, tile)
            transposes(NT - 1, 1)

        @block.vector
        def _(dve):
            for i in range(4):
                dve.wait_ge(w_hi, i + 1)
                hi, lo = (wohl[:, h, 2 * i:2 * i + 2, :].rearrange("p c n -> p (c n)") for h in range(2))
                nc.vector.scalar_tensor_tensor(lo, wraw[:, i % 2, :], K.sc[:, SO:SO + 1], hi,
                                               ALU.mult, ALU.subtract).then_inc(w_lo, 1)

            def copy_out(n, k):
                dve.wait_ge(tr, n * 2 + 2)
                nc.vector.tensor_copy(K.xT[:, 1, :, bass.ds(n * P, P)], PT[k][1][:]).then_inc(ev_lo, 1)

            def tile(n, k, r):
                links = [0]

                def link(ins):
                    links[0] += 1
                    ins.then_inc(chain, 1)
                    dve.wait_ge(chain, n * LINKS + links[0])

                def stats(src):
                    for h in range(2):
                        last = nc.vector.bn_stats(st6[:, h, :], src[:, h * 512:(h + 1) * 512])
                    link(last)
                    apart(dve, apart_dve)
                    link(nc.vector.bn_aggr(mv[:], st6[:]))

                dve.wait_ge(y_mm, n + 1)
                stats(Y[k])
                link(nc.vector.tensor_scalar(ve[:], mv[:, 1:2], K.k_att[:], K.k_att[:], ALU.mult, ALU.mult))
                link(nc.vector.tensor_scalar(ve[:], ve[:], EPS, None, ALU.add))
                dve.sem_inc(var_ok, 1)
                dve.wait_ge(std_ok, n * 2 + 1)
                link(nc.vector.reciprocal(rs[:], sd[:]))
                link(nc.vector.tensor_scalar(rs[:], rs[:], K.k_att[:], None, ALU.mult))
                wait(dve, hi_ok, n)
                link(nc.vector.tensor_scalar(z[:], Y[k][:], mv[:, 0:1], rs[:], ALU.subtract, ALU.mult))
                dve.wait_ge(x_in[k], r * 16 + 16)
                wait(dve, x1_out[k], r * 16)
                link(nc.vector.tensor_tensor(x1[:, k, :], z[:], xin[:, k, :], ALU.add))
                dve.sem_inc(x1_ok, 1)
                stats(x1[:, k, :])
                link(nc.vector.tensor_scalar(ve[:], mv[:, 1:2], EPS, None, ALU.add))
                dve.sem_inc(var_ok, 1)
                dve.wait_ge(std_ok, n * 2 + 2)
                link(nc.vector.reciprocal(rs[:], sd[:]))
                link(nc.vector.tensor_scalar(z[:], x1[:, k, :], mv[:, 0:1], rs[:], ALU.subtract, ALU.mult))
                dve.sem_inc(xn_ok, 1)
                dve.wait_ge(hi_ok, n + 1)
                link(nc.vector.tensor_tensor(xhl[:, k, 1, :], z[:], xhl[:, k, 0, :], ALU.subtract))
                dve.sem_inc(lo_ok, 1)
                assert links[0] == LINKS
                if not (isinstance(n, int) and n == 0):
                    copy_out(n - 1, 1 - k)

            pair(dve, tile)
            copy_out(NT - 1, 1)


def phase_ffn(nc, K, gu_q, gu_sz, down_q, down_sz, x1_dram, out):
    with ExitStack() as ctx:
        sb = lambda n, s, d: ctx.enter_context(nc.sbuf_tensor("d_" + n, s, d))
        ps = lambda n, s, d: ctx.enter_context(nc.psum_tensor("d_" + n, s, d))
        sem = lambda n: ctx.enter_context(nc.semaphore("d_" + n))
        y = sb("y", [P, NT, E], F32)
        wgu = [sb(f"wgu{c}", [P, 2, NC, 2, P], F16) for c in range(2)]
        wd = sb("wd", [P, 2, 2, E], F16)
        gq = sb("gq", [P, 4, 2 * P], I32)
        gsz = sb("gsz", [P, 4, 4 * P], F32)
        dq = sb("dq", [P, E], I32)
        dsz = sb("dsz", [P, 2, E], F32)
        nib = sb("nib", [P, 512], I32)
        wf = sb("wf", [P, 512], F32)
        hT = sb("hT", [P, 2, 2, TOK], F16)
        sil = sb("sil", [P, 2, 512], F32)
        h32 = sb("h32", [P, 2, 512], F32)
        st6 = sb("st6", [P, 2, 2, 6], F32)
        mv = sb("mv", [P, 2, 2], F32)
        ve = sb("ve", [P, 2], F32)
        sd = sb("sd", [P, 2], F32)
        rs = sb("rs", [P, 2], F32)
        x1 = gsz[:].rearrange("p a b -> p (a b)").rearrange("p (k e) -> p k e", k=2)
        z = dsz
        GP = [ps(f"g{i}", [P, 512], F32) for i in range(2)]
        UP = [ps(f"u{i}", [P, 512], F32) for i in range(2)]
        D = [ps(f"d{i}", [P, E], F32) for i in range(2)]
        gq_in, gsz_in, dq_in, dsz_in = sem("gq_in"), sem("gsz_in"), sem("dq_in"), sem("dsz_in")
        g_unpacked, g_scaled, d_unpacked, d_scaled = sem("g_unp"), sem("g_scl"), sem("d_unp"), sem("d_scl")
        w_sub, w_step, w_hi, w_lo = sem("w_sub"), sem("w_step"), sem("w_hi"), sem("w_lo")
        gu_mm, silu_ok, h_ok, h_hi, h_lo = sem("gu_mm"), sem("silu"), sem("h_ok"), sem("h_hi"), sem("h_lo")
        d_mm, y_ok = sem("d_mm"), sem("y_ok")
        x1_in = [sem("x1_in0"), sem("x1_in1")]
        chain, var_ok, std_ok, z_ok, o_ok = sem("chain"), sem("var"), sem("std"), sem("z_ok"), sem("o_ok")
        o_out = [sem("o_out0"), sem("o_out1")]
        x1v = x1_dram.rearrange("(n p) e -> n p e", p=P)
        outv = out.rearrange("(n p) e -> n p e", p=P)
        LAST = GROUPS
        width = lambda g: LASTW if isinstance(g, int) and g == LAST else P
        block = ctx.enter_context(nc.Block())

        def groups(eng, body):
            body(0)
            with eng.Fori(1, LAST - 1) as g:
                body(g)
            body(LAST - 1)
            body(LAST)


        @block.sync
        def _(sp):
            def load_chunk(g, c):
                w = width(g)
                i = g * 2 + c
                o = g * (4 * P) + c * 2 * w
                wait(sp, g_unpacked, i * 4)
                sp.dma_start(gq[:, :, 0:2 * w], gu_q.rearrange("(j p) n -> p j n", p=P)[:, :, bass.ds(o, 2 * w)])\
                    .then_inc(gq_in, 16)
                wait(sp, g_scaled, i * 4)
                for q in range(4):
                    src = gu_sz.rearrange("(j q) n -> q j n", q=4)[q, :, bass.ds(g * (8 * P) + c * 4 * w, 4 * w)]
                    sp.dma_start(gsz[q * 32:(q + 1) * 32, :, 0:4 * w], src.partition_broadcast(32))\
                        .then_inc(gsz_in, 16)

            def load_down(g):
                w = width(g)
                wait(sp, d_unpacked, g * 4)
                sp.dma_start(dq[0:w, :], down_q[bass.ds(g * P, w), :]).then_inc(dq_in, 16)
                wait(sp, d_scaled, g * 4)
                for q in range(w // 32):
                    src = down_sz[bass.ds(g * 4 + q, 1)].rearrange("a x n -> (a x) n")
                    sp.dma_start(dsz[q * 32:(q + 1) * 32, :, :], src.partition_broadcast(32)).then_inc(dsz_in, 16)

            def body(g):
                load_chunk(g, 0)
                load_chunk(g, 1)
                load_down(g)
            groups(sp, body)
            sp.wait_ge(w_lo, 12 * (LAST + 1))
            for t in range(NT):
                wait(sp, o_ok, t - 1)
                sp.dma_start(x1[:, t % 2, :], x1v[t]).then_inc(x1_in[t % 2], 16)
                if t:
                    sp.wait_ge(o_ok, t)
                    sp.dma_start(outv[t - 1], z[:, (t - 1) % 2, :]).then_inc(o_out[(t - 1) % 2], 16)
            sp.wait_ge(o_ok, NT)
            sp.dma_start(outv[NT - 1], z[:, 1, :]).then_inc(o_out[1], 16)
            for k in range(2):
                sp.wait_ge(o_out[k], 16 * NT // 2)

        def split_target(g, kind, k):
            w = width(g)
            if kind == 2:
                dst = [wd[0:w, x, k // 2, k % 2 * 512:(k % 2 + 1) * 512] for x in range(2)]
                return dst, wf[0:w, :], K.sc[0:w, SD:SD + 1]
            n = k // 2 * 4
            m = SG + k % 2
            dst = [wgu[kind][:, x, n:n + 4, k % 2, 0:w] for x in range(2)]
            return dst, wf[:, 0:4 * w].rearrange("p (j i) -> p j i", j=4), K.sc[:, m:m + 1]

        @block.scalar
        def _(act):
            def item(g, kind, k):
                n = g * 12 + kind * 4 + k
                act.wait_ge(w_step, n + 1)
                (hi, _), src, scale = split_target(g, kind, k)
                nc.scalar.activation(hi, src, ACT.Copy, scale=scale).then_inc(w_hi, 1)

            def gate(g, c, b):
                w, e = width(g), g * 8 + c * 4 + b
                act.wait_ge(gu_mm, e + 1)
                wait(act, h_ok, e - 1)
                nc.scalar.activation(sil[0:w, b % 2, :], GP[b % 2][0:w, :], ACT.Silu, scale=K.k_gate[0:w, :])\
                    .then_inc(silu_ok, 1)
                act.wait_ge(h_ok, e + 1)
                wait(act, d_mm, g * NT)
                nc.scalar.activation(hT[0:w, 0, c, b * 512:(b + 1) * 512], h32[0:w, b % 2, :], ACT.Copy)\
                    .then_inc(h_hi, 1)

            for k in range(8):
                item(0, k // 4, k % 4)

            def body(g):
                last = isinstance(g, int) and g == LAST
                for b in range(4):
                    gate(g, 0, b)
                    item(g, 2, b)
                for b in range(4):
                    gate(g, 1, b)
                    if not last:
                        item(g + 1, 0, b)
                if not last:
                    for k in range(4):
                        item(g + 1, 1, k)
            groups(act, body)
            for t in range(NT):
                act.wait_ge(var_ok, t + 1)
                nc.scalar.activation(sd[:, t % 2:t % 2 + 1], ve[:, t % 2:t % 2 + 1], ACT.Sqrt).then_inc(std_ok, 1)

        @block.tensor
        def _(pe):
            def body(g):
                w = width(g)
                for c in range(2):
                    pe.wait_ge(w_lo, g * 12 + c * 4 + 4)
                    for b in range(4):
                        e = g * 8 + c * 4 + b
                        wait(pe, silu_ok, e - 1)
                        wait(pe, h_ok, e - 1)
                        for m, out_bank in enumerate((GP[b % 2], UP[b % 2])):
                            for kc in range(NC):
                                for a, x in ((0, 0), (0, 1), (1, 0)):
                                    last = nc.tensor.matmul(out_bank[0:w, :], wgu[c][:, a, kc, m, 0:w],
                                                            K.xT[:, x, kc, b * 512:(b + 1) * 512],
                                                            start=(kc == 0 and a == x), stop=(kc == NC - 1 and a == 1))
                        last.then_inc(gu_mm, 1)
                pe.wait_ge(w_lo, g * 12 + 12)
                for t in range(NT):
                    pe.wait_ge(h_lo, g * 8 + 4 + t // 4 + 1)
                    wait(pe, y_ok, g * NT + t - 1)
                    for c in range(2):
                        for a, b in ((0, 0), (0, 1), (1, 0)):
                            for h in range(2):
                                last = nc.tensor.matmul(D[t % 2][:, h * 512:(h + 1) * 512],
                                                        hT[0:w, a, c, t * P:(t + 1) * P],
                                                        wd[0:w, b, c, h * 512:(h + 1) * 512],
                                                        start=(c == 0 and a == b), stop=(c == 1 and a == 1))
                    last.then_inc(d_mm, 1)
            groups(pe, body)

        @block.vector
        def _(dve):
            links = [0]

            def link(ins):
                links[0] += 1
                ins.then_inc(chain, 1)
                dve.wait_ge(chain, links[0])

            def item(g, kind, k):
                w, n = width(g), g * 12 + kind * 4 + k
                (hi, lo), src, scale = split_target(g, kind, k)
                wait(dve, w_lo, n)
                if kind == 2:
                    dve.wait_ge(dq_in, g * 16 + 16)
                    raw, nb = dq[0:w, k % 2 * 512:(k % 2 + 1) * 512], nib[0:w, :]
                    s, zero = (dsz[0:w, x, k % 2 * 512:(k % 2 + 1) * 512] for x in range(2))
                    unpacked, scaled = d_unpacked, d_scaled
                else:
                    dve.wait_ge(gq_in, (g * 2 + kind + 1) * 16)
                    raw = gq[:, :, k % 2 * w:(k % 2 + 1) * w]
                    nb = nib[:, 0:4 * w].rearrange("p (j i) -> p j i", j=4)
                    s, zero = (gsz[:, :, (k % 2 * 2 + x) * w:(k % 2 * 2 + x + 1) * w] for x in range(2))
                    unpacked, scaled = g_unpacked, g_scaled
                if k // 2 == 0:
                    ins = nc.vector.tensor_scalar(nb, raw, 4, 15, ALU.logical_shift_right, ALU.bitwise_and)
                else:
                    ins = nc.vector.tensor_scalar(nb, raw, 15, None, ALU.bitwise_and)
                ins.then_inc(unpacked, 1)
                if kind == 2:
                    dve.wait_ge(d_unpacked, g * 4 + k + 1)
                    if width(g) == P:
                        dve.wait_ge(dsz_in, g * 64 + 64)
                    else:
                        dve.wait_ge(dsz_in, LAST * 64 + LASTW // 32 * 16)
                else:
                    dve.wait_ge(g_unpacked, (g * 2 + kind) * 4 + k + 1)
                    dve.wait_ge(gsz_in, (g * 2 + kind + 1) * 64)
                nc.vector.tensor_tensor(src, nb, zero, ALU.subtract).then_inc(w_sub, 1)
                dve.wait_ge(w_sub, n + 1)
                nc.vector.tensor_tensor(src, src, s, ALU.mult).then_inc(scaled, 1)
                if kind == 2:
                    dve.wait_ge(d_scaled, g * 4 + k + 1)
                    wait(dve, d_mm, g * NT)
                else:
                    dve.wait_ge(g_scaled, (g * 2 + kind) * 4 + k + 1)
                    wait(dve, gu_mm, g * 8 + kind * 4 - 4)
                dve.sem_inc(w_step, 1)
                dve.wait_ge(w_hi, n + 1)
                nc.vector.scalar_tensor_tensor(lo, src, scale, hi, ALU.mult, ALU.subtract).then_inc(w_lo, 1)

            def gated(g, c, b):
                w, e = width(g), g * 8 + c * 4 + b
                dve.wait_ge(silu_ok, e + 1)
                wait(dve, h_hi, e - 1)
                wait(dve, h_lo, e - 1)
                nc.vector.scalar_tensor_tensor(h32[0:w, b % 2, :], sil[0:w, b % 2, :], K.k_h[0:w, :],
                                               UP[b % 2][0:w, :], ALU.mult, ALU.mult).then_inc(h_ok, 1)

            def gated_low(g, c, b):
                w, e = width(g), g * 8 + c * 4 + b
                dve.wait_ge(h_hi, e + 1)
                cols = slice(b * 512, (b + 1) * 512)
                nc.vector.tensor_tensor(hT[0:w, 1, c, cols], h32[0:w, b % 2, :], hT[0:w, 0, c, cols],
                                        ALU.subtract).then_inc(h_lo, 1)

            def gather(g, t):
                dve.wait_ge(d_mm, g * NT + t + 1)
                if isinstance(g, int) and g == 0:
                    nc.vector.tensor_copy(y[:, t, :], D[t % 2][:]).then_inc(y_ok, 1)
                else:
                    wait(dve, y_ok, g * NT + t - (NT - 1))
                    nc.vector.tensor_tensor(y[:, t, :], y[:, t, :], D[t % 2][:], ALU.add).then_inc(y_ok, 1)

            for k in range(8):
                item(0, k // 4, k % 4)

            def body(g):
                last = isinstance(g, int) and g == LAST
                for b in range(4):
                    gated(g, 0, b)
                    item(g, 2, b)
                    gated_low(g, 0, b)
                for b in range(4):
                    gated(g, 1, b)
                    if not last:
                        item(g + 1, 0, b)
                    gated_low(g, 1, b)
                for t in range(NT):
                    gather(g, t)
                    if not last and t % 4 == 3:
                        item(g + 1, 1, t // 4)
                    if last:
                        last_norm(t)
                        if t:
                            last_norm_end(t - 1)

            def last_norm(t):
                k = t % 2
                dve.wait_ge(y_ok, LAST * NT + t + 1)
                for h in range(2):
                    last = nc.vector.bn_stats(st6[:, k, h, :], y[:, t, h * 512:(h + 1) * 512])
                link(last)
                link(nc.vector.bn_aggr(mv[:, k, :], st6[:, k, :, :]))
                wait(dve, std_ok, t - 1)
                link(nc.vector.tensor_scalar(ve[:, k:k + 1], mv[:, k, 1:2], K.k_y[:], K.k_y[:], ALU.mult, ALU.mult))
                nc.vector.tensor_scalar(ve[:, k:k + 1], ve[:, k:k + 1], EPS, None, ALU.add).then_inc(var_ok, 1)

            def last_norm_end(t):
                k = t % 2
                dve.wait_ge(std_ok, t + 1)
                link(nc.vector.reciprocal(rs[:, k:k + 1], sd[:, k:k + 1]))
                link(nc.vector.tensor_scalar(rs[:, k:k + 1], rs[:, k:k + 1], K.k_y[:], None, ALU.mult))
                wait(dve, o_out[k], t // 2 * 16)
                nc.vector.tensor_scalar(z[:, k, :], y[:, t, :], mv[:, k, 0:1], rs[:, k:k + 1],
                                        ALU.subtract, ALU.mult).then_inc(z_ok, 1)

            groups(dve, body)
            last_norm_end(NT - 1)

        @block.gpsimd
        def _(pool):
            for t in range(NT):
                k = t % 2
                pool.wait_ge(z_ok, t + 1)
                pool.wait_ge(x1_in[k], t // 2 * 16 + 16)
                nc.gpsimd.tensor_tensor(z[:, k, :], z[:, k, :], x1[:, k, :], ALU.add).then_inc(o_ok, 1)


class Shared:
    pass


def build(nc, x, wqkv, wo, szs, gu_q, gu_sz, down_q, down_sz, ropes, x1_dram, out):
    K = Shared()
    with ExitStack() as ctx:
        sb = lambda n, s, d: ctx.enter_context(nc.sbuf_tensor(n, s, d))
        K.ident = sb("ident", [P, P], F16)
        K.identb = sb("identb", [P, P], BF16)
        K.maskb = sb("maskb", [P, P], BF16)
        K.ln_ps = sb("ln_ps", [P, 1], F32)
        K.sc = sb("sc", [P, 8], F32)
        K.inv = sb("inv", [P, 8], F32)
        K.k_score, K.k_att, K.k_y, K.k_gate, K.k_h = (sb(n, [P, 1], F32) for n in
                                                      ("k_score", "k_att", "k_y", "k_gate", "k_h"))
        K.xT = sb("xT", [P, 2, NC, TOK], F16)
        phase_scales_and_norm(nc, K, x, wqkv, wo, szs)
        with nc.sbuf_tensor("ctxT", [P, 2, NC, TOK], F16) as ctxT:
            K.ctxT = ctxT
            phase_attention(nc, K, wqkv, ropes)
            phase_output(nc, K, x, wo, x1_dram)
        phase_ffn(nc, K, gu_q, gu_sz, down_q, down_sz, x1_dram, out)


def rope_tables():
    f = np.float32
    inv = (f(1.0) / np.power(f(500000.0), np.arange(0, DH, 2, dtype=f) / f(DH))).astype(f)
    wavelen = (f(2.0 * np.pi) / inv).astype(f)
    scaled = np.where(wavelen > f(2048), inv / f(32.0), inv).astype(f)
    smooth = ((f(2048) / wavelen - f(1.0)) / f(3.0)).astype(f)
    smoothed = ((f(1.0) - smooth) * scaled / f(32.0) + smooth * scaled).astype(f)
    scaled = np.where(~(wavelen < 2048) & ~(wavelen > 512), smoothed, scaled).astype(f)
    ang = (np.arange(T, dtype=f)[:, None] * scaled[None]).astype(f)
    cos, sin = np.cos(ang), np.sin(ang)
    full = np.stack([np.concatenate([cos, cos], 1), np.concatenate([-sin, sin], 1)])
    return np.ascontiguousarray(full.reshape(2, UT, P, DH).transpose(2, 0, 1, 3)).astype(f)


def chunked():
    starts = range(0, INTER, GROUP_I)
    return [np.arange(s + c, min(s + GROUP_I, INTER), 2) for s in starts for c in range(2)]


def kernel(**inputs):
    import concourse.bacc as _bacc
    from concourse.bass_utils import run_bass_kernel_spmd as _run

    a = {k[3:]: np.asarray(v) for k, v in inputs.items()}
    kv = lambda w, n: w.reshape(KVH, n * DH, E)
    w = np.concatenate([kv(a["attn_Wq"], GQ), kv(a["attn_Wk"], 1), kv(a["attn_Wv"], 1)], 1)
    wqkv = w.reshape(KVH, WCOL, NC, P).transpose(0, 3, 2, 1)
    wo = a["attn_Wo"].T.reshape(NC, P, E).transpose(1, 0, 2).reshape(P, NC * E)
    order = chunked()
    gu_q = np.concatenate([a["ffn_" + m + "_Wq"][i].T for i in order for m in ("gate", "up")], 1)
    gu_sz = np.concatenate([a["ffn_" + m][i].T for i in order
                            for m in ("gate_scale", "gate_zero", "up_scale", "up_zero")], 1)
    down_sz = np.stack([a["ffn_down_scale"].T, a["ffn_down_zero"].T], 1)
    arrays = {
        "x": a["attn_x"].reshape(TOK, E), "wqkv": wqkv, "wo": wo, "gu_q": gu_q, "gu_sz": gu_sz,
        "down_q": a["ffn_down_Wq"].T, "down_sz": down_sz, "ropes": rope_tables(),
    }
    for m in ("gate", "up", "down"):
        for s in ("scale", "zero"):
            arrays[f"{m}_{s}"] = a[f"ffn_{m}_{s}"].reshape(P, -1)
    arrays = {"in_" + k: np.ascontiguousarray(v) for k, v in arrays.items()}

    nc = _bacc.Bacc("TRN2", target_bir_lowering=False, num_devices=1)
    d = {k[3:]: nc.dram_tensor(k, v.shape, mybir.dt.from_np(v.dtype), kind="ExternalInput").ap()
         for k, v in arrays.items()}
    x1 = nc.dram_tensor("x1_rows", (TOK, E), F32, kind="Internal").ap()
    out = nc.dram_tensor("out_rows", (TOK, E), F32, kind="ExternalOutput").ap()
    szs = [d[f"{m}_{s}"] for m in ("gate", "up", "down") for s in ("scale", "zero")]
    build(nc, d["x"], d["wqkv"], d["wo"], szs, d["gu_q"], d["gu_sz"], d["down_q"], d["down_sz"], d["ropes"], x1, out)
    r = _run(nc, [arrays], core_ids=[0])
    return r.results[0]["out_rows"].reshape(BATCH, T, E)
```

```python
import numpy as np
import concourse.bass as bass
from concourse import mybir
from contextlib import ExitStack

F32 = mybir.dt.float32
F16 = mybir.dt.float16
BF16 = mybir.dt.bfloat16
I32 = mybir.dt.int32
ACT = mybir.ActivationFunctionType
ALU = mybir.AluOpType
AX = mybir.AxisListType

P = 128
BATCH, T, E = 2, 1024, 1024
TOK = BATCH * T
NT = TOK // P
NC = E // P
HEADS, KVH, DH = 32, 8, 32
GQ = HEADS // KVH
UT = T // P
QW = GQ * P
WCOL = (GQ + 2) * DH
INTER = 2752
GROUPS, GROUP_I = INTER // 256, 256
LASTW = (INTER - GROUPS * GROUP_I) // 2
EPS = 1e-5
XS = 1024.0
QS = 2.0 ** -24
MS = 2.0 ** 15
PS_LOG = 14 * float(np.log(2.0))
HS = 2.0 ** -45
SQ, SK, SV, SO, SG, SU, SD = range(7)
MASKED = -3.0e38


def wait(eng, sem, value):
    if isinstance(value, int) and value <= 0:
        return
    eng.wait_ge(sem, value)


def apart(eng, sem):
    eng.sem_inc(sem, 1)


def loop(eng, first, last, body):
    body(first)
    if last - first > 1:
        with eng.Fori(first + 1, last) as r:
            body(r)
    body(last)


WO_PIECE = NC * E // KVH


def phase_scales_and_norm(nc, K, x, wqkv, wo, szs):
    with ExitStack() as ctx:
        sb = lambda n, s, d: ctx.enter_context(nc.sbuf_tensor(n, s, d))
        sem = lambda n: ctx.enter_context(nc.semaphore(n))
        wtmp = sb("a_wtmp", [P, 2, NC * WCOL], F32)
        otmp = sb("a_otmp", [P, 2, WO_PIECE], F32)
        ztmp = sb("a_ztmp", [P, 6, 344], F32)
        zab = sb("a_zab", [P, 3, 344], F32)
        part = sb("a_part", [P, 4, 8], F32)
        own = sb("a_own", [P, 8], F32)
        allm = sb("a_allm", [P, 8], F32)
        ebits = sb("a_ebits", [P, 8], I32)
        tmp1 = sb("a_tmp1", [P, 3], F32)
        tmp2 = sb("a_tmp2", [P, 3], F32)
        xin = sb("a_xin", [P, 4, E], F32)
        xn = sb("a_xn", [P, 2, E], F32)
        xhl = sb("a_xhl", [P, 2, 2, E], F16)
        st6 = sb("a_st6", [P, 2, 2, 6], F32)
        mv = sb("a_mv", [P, 2, 2], F32)
        ve = sb("a_ve", [P, 2], F32)
        sd = sb("a_sd", [P, 2], F32)
        rs = sb("a_rs", [P, 2], F32)
        pt = [[ctx.enter_context(nc.psum_tensor(f"a_pt{s}{h}", [P, NC, P], F16)) for h in range(2)]
              for s in range(2)]
        w_in = [sem("a_w_in0"), sem("a_w_in1")]
        o_in = [sem("a_o_in0"), sem("a_o_in1")]
        w_used, o_used = sem("a_w_used"), sem("a_o_used")
        z_in = sem("a_z_in")
        x_in = [sem(f"a_x_in{k}") for k in range(4)]
        s_const = sem("a_const")
        first_w = sem("a_first_w")
        s_zero, s_zab = sem("a_zero"), sem("a_zab")
        s_bound = sem("a_bound")
        s_allmax = sem("a_allmax")
        s_chain = sem("a_chain")
        s_stats = sem("a_stats")
        s_apart = sem("a_apart")
        s_var = sem("a_var")
        s_std = sem("a_std")
        s_rstd = sem("a_rstd")
        s_xn = sem("a_xn_done")
        s_hi = sem("a_hi")
        s_lo = sem("a_lo")
        s_tr = sem("a_tr")
        s_ev_hi = sem("a_ev_hi")
        s_ev_lo = sem("a_ev_lo")
        xv = x.rearrange("(n p) e -> n p e", p=P)
        block = ctx.enter_context(nc.Block())


        @block.sync
        def _(sp):
            def body(r):
                for i in range(4):
                    n = r * 4 + i
                    wait(sp, s_xn, n - 3)
                    sp.dma_start(xin[:, i, :], xv[bass.ds(n, 1)].rearrange("a p e -> p (a e)"))\
                        .then_inc(x_in[i], 16)
                    g, k = r * 2 + i // 2, i // 2
                    if i % 2 == 0:
                        wait(sp, w_used, g - 1)
                        sp.dma_start(wtmp[:, k, :], wqkv[bass.ds(g, 1)].rearrange("a p c n -> p (a c n)"))\
                            .then_inc(w_in[k], 16)
                    else:
                        wait(sp, o_used, g - 1)
                        sp.dma_start(otmp[:, k, :], wo[:, bass.ds(g * WO_PIECE, WO_PIECE)]).then_inc(o_in[k], 16)
            body(0)
            for i, sz in enumerate(szs):
                sp.dma_start(ztmp[:, i, :], sz).then_inc(z_in, 16)
            with sp.Fori(1, NT // 4) as r:
                body(r)
            sp.dma_start(K.wraw[:], wqkv[0]).then_inc(first_w, 16)
            sp.wait_ge(first_w, 16)

        @block.gpsimd
        def _(pool):
            nc.gpsimd.memset(K.ident[:], 0.0).then_inc(s_const, 1)
            nc.gpsimd.memset(K.identb[:], 0.0).then_inc(s_const, 1)
            nc.gpsimd.memset(K.maskb[:], 0.0).then_inc(s_const, 1)
            pool.wait_ge(s_const, 3)
            for m in (K.ident, K.identb):
                nc.gpsimd.affine_select(out=m[:], in_=m[:], compare_op=ALU.not_equal, fill=1.0, base=0,
                                        pattern=[[-1, P]], channel_multiplier=1).then_inc(s_const, 1)
            nc.gpsimd.affine_select(out=K.maskb[:], in_=K.maskb[:], compare_op=ALU.is_ge, fill=MASKED, base=0,
                                    pattern=[[-1, P]], channel_multiplier=1).then_inc(s_const, 1)
            pool.wait_ge(s_bound, 4)
            nc.gpsimd.partition_all_reduce(allm[:, 0:7], own[:, 0:7], P, bass.bass_isa.ReduceOp.max)\
                .then_inc(s_allmax, 1)

        @block.vector
        def _(dve):
            links = [0]

            def link(ins):
                links[0] += 1
                ins.then_inc(s_chain, 1)
                dve.wait_ge(s_chain, links[0])

            def stats(n, i, r):
                k = i % 2
                dve.wait_ge(x_in[i], (r + 1) * 16)
                wait(dve, s_xn, n - 1)
                for h in range(2):
                    nc.vector.bn_stats(st6[:, k, h, :], xin[:, i, h * 512:(h + 1) * 512]).then_inc(s_stats, 1)
                dve.wait_ge(s_stats, n * 3 + 2)
                apart(dve, s_apart)
                nc.vector.bn_aggr(mv[:, k, :], st6[:, k, :, :]).then_inc(s_stats, 1)
                dve.wait_ge(s_stats, n * 3 + 3)
                nc.vector.tensor_scalar(ve[:, k:k + 1], mv[:, k, 1:2], EPS, None, ALU.add).then_inc(s_var, 1)

            def scale_rows(n, i):
                k = i % 2
                dve.wait_ge(s_std, n + 1)
                nc.vector.reciprocal(rs[:, k:k + 1], sd[:, k:k + 1]).then_inc(s_rstd, 1)
                dve.wait_ge(s_rstd, n + 1)
                wait(dve, s_hi, n - 1)
                wait(dve, s_lo, n - 1)
                nc.vector.tensor_scalar(xn[:, k, :], xin[:, i, :], mv[:, k, 0:1], rs[:, k:k + 1],
                                        ALU.subtract, ALU.mult).then_inc(s_xn, 1)

            def low(n, k):
                dve.wait_ge(s_hi, n + 1)
                wait(dve, s_tr, n * 2 - 2)
                nc.vector.tensor_tensor(xhl[:, k, 1, :], xn[:, k, :], xhl[:, k, 0, :], ALU.subtract)\
                    .then_inc(s_lo, 1)

            def bounds(g, k, r):
                dve.wait_ge(w_in[k], 16 * (r + 1))
                w = wtmp[:, k, :].rearrange("p (c n) -> p c n", c=NC)
                for m, (a, b) in enumerate(((0, P), (P, P + DH), (P + DH, WCOL))):
                    last = nc.vector.tensor_reduce(part[:, m, bass.ds(g, 1)], w[:, :, a:b], AX.XY, ALU.max,
                                                   apply_absolute_value=True)
                last.then_inc(w_used, 1)
                dve.wait_ge(o_in[k], 16 * (r + 1))
                nc.vector.tensor_reduce(part[:, 3, bass.ds(g, 1)], otmp[:, k, :], AX.X, ALU.max,
                                        apply_absolute_value=True).then_inc(o_used, 1)

            def body(r):
                for i in range(4):
                    n = r * 4 + i
                    stats(n, i, r)
                    if not isinstance(n, int) or n > 0:
                        low(n - 1, (i + 1) % 2)
                    if i % 2:
                        bounds(r * 2 + i // 2, i // 2, r)
                    scale_rows(n, i)

            def ffn_bounds():
                dve.wait_ge(z_in, 96)
                for m in range(3):
                    zero = ztmp[:, 2 * m + 1, :]
                    nc.vector.scalar_tensor_tensor(zab[:, m, :], zero, -1.0, zero, ALU.mult, ALU.max)\
                        .then_inc(s_zero, 1)
                for m in range(3):
                    dve.wait_ge(s_zero, m + 1)
                    nc.vector.scalar_tensor_tensor(zab[:, m, :], zab[:, m, :], 15.0, ztmp[:, 2 * m, :],
                                                   ALU.add, ALU.mult).then_inc(s_zab, 1)
                for m in range(3):
                    dve.wait_ge(s_zab, m + 1)
                    nc.vector.tensor_reduce(own[:, 4 + m:5 + m], zab[:, m, :], AX.X, ALU.max,
                                            apply_absolute_value=True).then_inc(s_bound, 1)

            body(0)
            with dve.Fori(1, NT // 4 - 1) as r:
                body(r)
            ffn_bounds()
            body(NT // 4 - 1)
            low(NT - 1, 1)
            dve.wait_ge(w_used, KVH)
            dve.wait_ge(o_used, KVH)
            nc.vector.tensor_reduce(own[:, 0:4], part[:], AX.X, ALU.max).then_inc(s_bound, 1)
            dve.wait_ge(s_allmax, 1)
            link(nc.vector.tensor_scalar(ebits[:, 0:7], allm[:, 0:7].bitcast(I32), 0x7F800000, None,
                                         ALU.bitwise_and))
            link(nc.vector.tensor_scalar(ebits[:, 0:7], ebits[:, 0:7], float(27 << 23), None, ALU.max))
            link(nc.vector.tensor_scalar(K.sc[:, 0:7].bitcast(I32), ebits[:, 0:7], -1.0, float(268 << 23),
                                         ALU.mult, ALU.add))
            link(nc.vector.tensor_scalar(K.inv[:, 0:7].bitcast(I32), ebits[:, 0:7], float(14 << 23), None,
                                         ALU.subtract))
            products = ((K.k_score, SQ, 2.0 ** 14 / float(np.sqrt(np.float32(DH))), SK, 2.0 ** 14),
                        (K.k_att, SV, 2.0 ** 14, SO, 1.0), (K.k_y, SG, 2.0 ** 17, SU, 2.0 ** 18))
            for i, (_, ma, ca, mb, cb) in enumerate(products):
                nc.vector.tensor_scalar(tmp1[:, i:i + 1], K.inv[:, ma:ma + 1], ca, None, ALU.mult)
                last = nc.vector.tensor_scalar(tmp2[:, i:i + 1], K.inv[:, mb:mb + 1], cb, None, ALU.mult)
            nc.vector.tensor_scalar(K.k_gate[:], K.inv[:, SG:SG + 1], 1.0 / XS, None, ALU.mult)
            nc.vector.tensor_scalar(K.k_h[:], K.sc[:, SG:SG + 1], HS, None, ALU.mult)
            link(last)
            for i, (out, _, _, _, _) in enumerate(products):
                last = nc.vector.tensor_tensor(out[:], tmp1[:, i:i + 1], tmp2[:, i:i + 1], ALU.mult)
            link(last)
            link(nc.vector.tensor_tensor(K.k_y[:], K.k_y[:], K.inv[:, SD:SD + 1], ALU.mult))

        @block.scalar
        def _(act):
            def copy_out(n, k, h):
                act.wait_ge(s_tr, n * 2 + h + 1)
                nc.scalar.activation(K.xT[:, h, :, bass.ds(n * P, P)], pt[k][h][:], ACT.Copy)\
                    .then_inc((s_ev_hi, s_ev_lo)[h], 1)

            def body(r):
                for i in range(4):
                    n, k = r * 4 + i, i % 2
                    act.wait_ge(s_var, n + 1)
                    wait(act, s_rstd, n - 1)
                    nc.scalar.activation(sd[:, k:k + 1], ve[:, k:k + 1], ACT.Sqrt, scale=XS ** -2).then_inc(s_std, 1)
                    before = not isinstance(n, int) or n > 0
                    if before:
                        copy_out(n - 1, 1 - k, 0)
                    act.wait_ge(s_xn, n + 1)
                    wait(act, s_tr, n * 2 - 3)
                    wait(act, s_lo, n - 1)
                    nc.scalar.activation(xhl[:, k, 0, :], xn[:, k, :], ACT.Copy).then_inc(s_hi, 1)
                    if before:
                        copy_out(n - 1, 1 - k, 1)

            loop(act, 0, NT // 4 - 1, body)
            copy_out(NT - 1, 1, 0)
            copy_out(NT - 1, 1, 1)

        @block.tensor
        def _(pe):
            pe.wait_ge(s_const, 6)

            def tile(n, k):
                for h in range(2):
                    pe.wait_ge((s_hi, s_lo)[h], n + 1)
                    wait(pe, (s_ev_hi, s_ev_lo)[h], n - 1)
                    for c in range(NC):
                        last = nc.tensor.transpose(pt[k][h][:, c, :], xhl[:, k, h, c * P:(c + 1) * P], K.ident[:])
                    last.then_inc(s_tr, 1)

            tile(0, 0)
            tile(1, 1)
            with pe.Fori(1, NT // 2) as r:
                tile(r * 2, 0)
                tile(r * 2 + 1, 1)


BT, BB = 2 * UT, 72
RING = 8
QSLOTS = 8
LEAD = 32
PROJ_SPAN = 69
NAT_HI, NAT_LO, STACK = 2, 2, 6
MAX_LEAD = 12
ROW_LAG = 3
AV_LAG, NORM_LAG, HI_LAG, LO_LAG, CTX_LAG = 5, 6, 7, 8, 10


def base(l):
    return 36 * (l // UT) + (l % UT) * (l % UT + 1) // 2


def tile_of(s):
    l = 8 * (s // 36)
    while base(l + 1) <= s:
        l += 1
    return l


def last_of(s, lag):
    l = tile_of(s - lag)
    return l if base(l + 1) - 1 == s - lag else None


def window(l):
    at = BB * (l // BT) - LEAD
    return at + l % BT * PROJ_SPAN // BT, at + (l % BT + 1) * PROJ_SPAN // BT


def tiles_with(s, after):
    return [l for l in range(-BT, 3 * BT) if window(l)[1] == s - after]


def chunks_at(s):
    for l in range(-BT, 3 * BT):
        a, b = window(l)
        if a <= s < b:
            return l, [c for c in range(NC) if a + c * (b - a) // NC == s]
    return None, []


def weights_change(s):
    q, j = divmod(s + LEAD - PROJ_SPAN, BB)
    return q + 1 if j == 0 else None


def has_tile(r, l):
    return not isinstance(r, int) or 0 <= BT * r + l < BT * KVH


def has_block(r, s):
    return not isinstance(r, int) or 0 <= BB * r + s < BB * KVH


def key_tile(s):
    l = tile_of(s)
    return l % UT if s == base(l) else s - base(l) - 1


def shared_bank(r, s):
    uses = [("stack", l) for l in tiles_with(s, STACK)]
    uses += [("rows", l) for l in [last_of(s + MAX_LEAD - ROW_LAG, 0)] if l is not None]
    uses += [("ctx", l) for l in [last_of(s, CTX_LAG)] if l is not None]
    return [(kind, l) for kind, l in uses if has_tile(r, l)]


def use_before(r, s, kind, l):
    uses = shared_bank(r, s)
    i = uses.index((kind, l))
    if i:
        return uses[i - 1]
    for p in range(s - 1, s - BB, -1):
        if shared_bank(r, p):
            return shared_bank(r, p)[-1]
    return None


def phase_attention(nc, K, wqkv, ropes, wo):
    with ExitStack() as ctx:
        sb = lambda n, s, d: ctx.enter_context(nc.sbuf_tensor(n, s, d))
        ps = lambda n, s, d: ctx.enter_context(nc.psum_tensor(n, s, d))
        sem = lambda n: ctx.enter_context(nc.semaphore("b_" + n))
        rope = sb("b_rope", [P, 2, UT, DH], F32)
        wcur = sb("b_wcur", [P, 2, NC, WCOL], F16)
        qkv = sb("b_qkv", [P, 2, WCOL], F32)
        t1 = sb("b_t1", [P, GQ + 1, DH], F32)
        t2 = sb("b_t2", [P, GQ + 1, DH], F32)
        rot = sb("b_rot", [P, 2, GQ + 1, DH], F32)
        nat = sb("b_nat", [P, 2, GQ + 1, 3 * DH], F16)
        qst = sb("b_qst", [P, QSLOTS, QW], F16)
        kst = sb("b_kst", [P, 2, T], F16)
        vaug = sb("b_vaug", [P, 2, UT, 66], F16)
        mpart = sb("b_mpart", [P, 2, GQ, UT], F32)
        negm = sb("b_negm", [P, 2, GQ], F32)
        maug = sb("b_maug", [P, 2, GQ, 2], F16)
        p32 = sb("b_p32", [P, RING, QW], F32)
        phi = sb("b_phi", [P, RING, QW], F16)
        plo = sb("b_plo", [P, RING, QW], F16)
        num = sb("b_num", [P, GQ, DH], F32)
        rden = sb("b_rden", [P, GQ, 1], F32)
        c32 = sb("b_c32", [P, 2, P], F32)
        chl = sb("b_chl", [P, 2, 2, P], F16)
        ST = [ps(f"b_st{i}", [P, QW], F32) for i in range(2)]
        M = [ps(f"b_m{i}", [P, QW], F32) for i in range(2)]
        AV = [ps(f"b_av{i}", [P, 512], F32) for i in range(2)]
        PR = ps("b_pr", [P, 512], F32)
        TB = ps("b_tb", [P, 1024], F16)
        apart_pool = sem("apart")
        rope_in, const_ok = sem("rope_in"), sem("const_ok")
        w_in, w_hi, w_ready, wo_in = sem("w_in"), sem("w_hi"), sem("w_ready"), sem("wo_in")
        p_done, p_evac = sem("p_done"), sem("p_evac")
        rope_st, rope_done = sem("rope_st"), sem("rope_done")
        v_hi, v_ready = sem("v_hi"), sem("v_ready")
        nat_hi, nat_ready = sem("nat_hi"), sem("nat_ready")
        stack_t, stack_evac = sem("stack_t"), sem("stack_evac")
        m_mm, m_red, m_all = sem("m_mm"), sem("m_red"), sem("m_all")
        maug_hi, maug_ready = sem("maug_hi"), sem("maug_ready")
        rows_t, rows_evac = sem("rows_t"), sem("rows_evac")
        st_done, exp_done, mask_done = sem("st_done"), sem("exp_done"), sem("mask_done")
        hi_act, hi_dve, lo_dve, lo_pool = sem("hi_act"), sem("hi_dve"), sem("lo_dve"), sem("lo_pool")
        av_done, norm_in, norm_done = sem("av_done"), sem("norm_in"), sem("norm_done")
        ctx_hi, ctx_lo, ctx_t, ctx_evac = sem("ctx_hi"), sem("ctx_lo"), sem("ctx_t"), sem("ctx_evac")
        block = ctx.enter_context(nc.Block())

        def lo_count(r, s):
            return lo_dve if s % 2 == 0 else lo_pool, r * (BB // 2) + s // 2 + 1

        def positions(eng, position):
            for s in range(PROJ_SPAN - LEAD - BB, 0):
                position(0, s)

            def body(r):
                for s in range(BB):
                    position(r, s)
            loop(eng, 0, KVH - 1, body)
            for s in range(BB, BB + CTX_LAG):
                position(KVH - 1, s)

        @block.sync
        def _(sp):
            sp.dma_start(rope[:], ropes).then_inc(rope_in, 16)

            def load(r):
                sp.wait_ge(w_ready, r)
                sp.dma_start(K.wraw[:], wqkv[bass.ds(r, 1)].rearrange("a p c n -> p (a c) n")).then_inc(w_in, 16)
            with sp.Fori(1, KVH) as r:
                load(r)
            sp.wait_ge(p_done, BT * KVH)
            sp.dma_start(K.wo_raw, wo.rearrange("p (c n) -> p c n", c=NC)).then_inc(wo_in, 16)
            sp.wait_ge(wo_in, 16)

        @block.tensor
        def _(pe):
            pe.wait_ge(const_ok, 2)

            def project(r, l, cs):
                if cs[0] == 0:
                    pe.wait_ge(w_ready, r + l // BT + 1)
                    wait(pe, p_evac, r * BT + l)
                t0 = (l // UT) % 2 * T + l % UT * P
                for c in cs:
                    for x, w in ((0, 0), (0, 1), (1, 0)):
                        last = nc.tensor.matmul(PR[:, 0:WCOL], K.xT[:, x, c, t0:t0 + P], wcur[:, w, c, :],
                                                start=(c == 0 and x == 0 and w == 0),
                                                stop=(c == NC - 1 and x == 1))
                if cs[-1] == NC - 1:
                    last.then_inc(p_done, 1)

            def scores_for_max(r, m):
                l, kt = tile_of(m), key_tile(m)
                diagonal = m == base(l)
                if diagonal:
                    pe.wait_ge(stack_evac, r * BT + l + 1)
                wait(pe, m_red, r * BB + m - 1)
                for h in range(GQ):
                    last = nc.tensor.matmul(M[m % 2][:, h * P:(h + 1) * P], qst[0:96, l % QSLOTS, h * P:(h + 1) * P],
                                            kst[0:96, (l // UT) % 2, kt * P:(kt + 1) * P],
                                            start=True, stop=not diagonal)
                    if diagonal:
                        last = nc.tensor.matmul(M[m % 2][:, h * P:(h + 1) * P], K.identb[:], K.maskb[:],
                                                start=False, stop=True)
                last.then_inc(m_mm, 1)

            def bank_free(r, s, kind, l):
                before = use_before(r, s, kind, l)
                if before is not None:
                    evac = {"stack": stack_evac, "rows": rows_evac, "ctx": ctx_evac}[before[0]]
                    pe.wait_ge(evac, r * BT + before[1] + 1)

            def max_rows(r, s, l):
                pe.wait_ge(maug_ready, r * BT + l + 1)
                bank_free(r, s, "rows", l)
                for h in range(GQ):
                    last = nc.tensor.transpose(TB[96:98, h * P:(h + 1) * P], maug[:, l % 2, h, :], K.ident[:])
                last.then_inc(rows_t, 1)

            def stack(r, s, l):
                pe.wait_ge(nat_ready, r * BT + l + 1)
                bank_free(r, s, "stack", l)
                for h in range(GQ + 1):
                    last = nc.tensor.transpose(TB[0:96, h * P:(h + 1) * P], nat[:, l % 2, h, :], K.ident[:])
                last.then_inc(stack_t, 1)

            def transpose_context(r, s, l):
                pe.wait_ge(ctx_lo, r * BT + l + 1)
                bank_free(r, s, "ctx", l)
                for x in range(2):
                    last = nc.tensor.transpose(TB[:, x * P:(x + 1) * P], chl[:, l % 2, x, :], K.ident[:])
                last.then_inc(ctx_t, 1)

            def scores(r, s):
                l = tile_of(s)
                if s == base(l):
                    pe.wait_ge(rows_evac, r * BT + l + 1)
                wait(pe, exp_done, r * BB + s - 1)
                kt = key_tile(s)
                nc.tensor.matmul(ST[s % 2][:], kst[0:98, (l // UT) % 2, kt * P:(kt + 1) * P],
                                 qst[0:98, l % QSLOTS, :], start=True, stop=True).then_inc(st_done, 1)

            def weigh(r, s):
                l = tile_of(s)
                first, final = s == base(l), s == base(l + 1) - 1
                if first:
                    pe.wait_ge(v_ready, r * BT + l + 1)
                    wait(pe, norm_in, (r * BT + l - 1) * 2)
                pe.wait_ge(*lo_count(r, s))
                v = vaug[:, (l // UT) % 2, key_tile(s), :]
                for h in range(GQ):
                    a = h * 65
                    nc.tensor.matmul(AV[l % 2][:, a:a + 65], phi[:, s % RING, h * P:(h + 1) * P], v[:, 0:65],
                                     start=(first and h == 0), stop=False, skip_group_check=True)
                    last = nc.tensor.matmul(AV[l % 2][:, a + 32:a + 65], plo[:, s % RING, h * P:(h + 1) * P], v[:, 32:65],
                                            start=False, stop=(final and h == GQ - 1), skip_group_check=True)
                last.then_inc(av_done, 1)

            def position(r, s):
                if has_block(r, s):
                    scores(r, s)
                if has_block(r, s - AV_LAG):
                    weigh(r, s - AV_LAG)
                uses = shared_bank(r, s)
                for kind, l in uses:
                    if kind == "stack":
                        stack(r, s, l)
                if has_block(r, s + MAX_LEAD):
                    scores_for_max(r, s + MAX_LEAD)
                for kind, l in uses:
                    if kind == "rows":
                        max_rows(r, s, l)
                l, cs = chunks_at(s)
                if cs and has_tile(r, l):
                    project(r, l, cs)
                for kind, l in uses:
                    if kind == "ctx":
                        transpose_context(r, s, l)

            positions(pe, position)

        @block.scalar
        def _(act):
            def split_w(r):
                wait(act, w_in, r * 16)
                wait(act, p_done, r * BT)
                for (a, b), m in zip(((0, P), (P, P + DH), (P + DH, WCOL)), (SQ, SK, SV)):
                    last = nc.scalar.activation(wcur[:, 0, :, a:b], K.wraw[:, :, a:b], ACT.Copy, scale=K.sc[:, m:m + 1])
                last.then_inc(w_hi, 1)

            def copy_projection(r, l):
                act.wait_ge(p_done, r * BT + l + 1)
                wait(act, rope_done, r * BT + l - 1)
                wait(act, v_ready, r * BT + l - 1)
                nc.scalar.activation(qkv[:, l % 2, :], PR[:, 0:WCOL], ACT.Copy, scale=QS).then_inc(p_evac, 1)

            def exps(r, s):
                act.wait_ge(st_done, r * BB + s + 1)
                wait(act, *lo_count(r, s - RING))
                nc.scalar.activation(p32[:, s % RING, :], ST[s % 2][:], ACT.Exp, bias=PS_LOG,
                                     scale=K.k_score[:]).then_inc(exp_done, 1)

            def copy_shared(r, kind, l):
                if kind == "stack":
                    act.wait_ge(stack_t, r * BT + l + 1)
                    wait(act, st_done, r * BB + max(base(l - QSLOTS + 1), 36 * (l // UT - 1)))
                    nc.scalar.activation(qst[0:96, l % QSLOTS, :], TB[0:96, 0:QW], ACT.Copy)
                    nc.scalar.activation(kst[0:96, (l // UT) % 2, l % UT * P:l % UT * P + P],
                                         TB[0:96, QW:QW + P], ACT.Copy).then_inc(stack_evac, 1)
                elif kind == "rows":
                    act.wait_ge(rows_t, r * BT + l + 1)
                    nc.scalar.activation(qst[96:98, l % QSLOTS, :], TB[96:98, 0:QW], ACT.Copy).then_inc(rows_evac, 1)
                else:
                    act.wait_ge(ctx_t, r * BT + l + 1)
                    t0 = (l // UT) % 2 * T + l % UT * P
                    dst = K.ctxT[:, :, bass.ds(r + l // BT, 1), t0:t0 + P].rearrange("p x a t -> p x (a t)")
                    nc.scalar.activation(dst, TB[:, 0:2 * P].rearrange("p (x t) -> p x t", x=2), ACT.Copy)\
                        .then_inc(ctx_evac, 1)

            def high_half(r, s):
                l = tile_of(s)
                if s % 2 == 0:
                    act.wait_ge(exp_done, r * BB + s + 1)
                    if s == base(l):
                        act.wait_ge(mask_done, r * BT + l + 1)
                    wait(act, av_done, r * BB + s + 1 - RING)
                    nc.scalar.activation(phi[:, s % RING, :], p32[:, s % RING, :], ACT.Copy).then_inc(hi_act, 1)

            def position(r, s):
                for l in tiles_with(s, 0):
                    if has_tile(r, l):
                        copy_projection(r, l)
                masked = s - 1 == base(tile_of(s - 1))
                if has_block(r, s - 1) and not masked:
                    high_half(r, s - 1)
                if has_block(r, s):
                    exps(r, s)
                uses = shared_bank(r, s)
                for kind, l in uses:
                    if kind != "ctx":
                        copy_shared(r, kind, l)
                if has_block(r, s - 1) and masked:
                    high_half(r, s - 1)
                for l in tiles_with(s, NAT_HI):
                    if has_tile(r, l):
                        n = r * BT + l
                        act.wait_ge(rope_done, n + 1)
                        wait(act, stack_t, n - 1)
                        src, dst = rot[:, l % 2, :, :], nat[:, l % 2, :, :]
                        hi2 = dst[:, 0:GQ, :].rearrange("p h (x d) -> p h x d", x=3)[:, :, 0:3:2, :]
                        nc.scalar.activation(hi2, src[:, 0:GQ, None, :].broadcast_to([P, GQ, 2, DH]), ACT.Copy)
                        nc.scalar.activation(dst[:, GQ, 0:2 * DH].rearrange("p (x d) -> p x d", x=2),
                                             src[:, GQ, None, :].broadcast_to([P, 2, DH]), ACT.Copy)\
                            .then_inc(nat_hi, 1)
                l = last_of(s, HI_LAG)
                if l is not None and has_tile(r, l):
                    act.wait_ge(norm_done, r * BT + l + 1)
                    wait(act, ctx_t, r * BT + l - 1)
                    nc.scalar.activation(chl[:, l % 2, 0, :], c32[:, l % 2, :], ACT.Copy).then_inc(ctx_hi, 1)
                for kind, l in uses:
                    if kind == "ctx":
                        copy_shared(r, kind, l)
                q = weights_change(s)
                if q is not None and has_tile(r, q * BT):
                    split_w(r + q)

            positions(act, position)

        @block.vector
        def _(dve):
            def split_w(r):
                dve.wait_ge(w_hi, r + 1)
                for (a, b), m in zip(((0, P), (P, P + DH), (P + DH, WCOL)), (SQ, SK, SV)):
                    last = nc.vector.scalar_tensor_tensor(wcur[:, 1, :, a:b], K.wraw[:, :, a:b], K.sc[:, m:m + 1],
                                                          wcur[:, 0, :, a:b], ALU.mult, ALU.subtract)
                last.then_inc(w_ready, 1)

            def context_sums(r, l):
                dve.wait_ge(av_done, r * BB + base(l + 1))
                wait(dve, norm_done, r * BT + l)
                av = AV[l % 2][:, 0:4 * 65].rearrange("p (h c) -> p h c", h=GQ)
                nc.vector.tensor_reduce(num[:], av[:, :, 0:64].rearrange("p h (x d) -> p h d x", x=2),
                                        AX.X, ALU.add).then_inc(norm_in, 1)
                nc.vector.reciprocal(rden[:], av[:, :, 64:65]).then_inc(norm_in, 1)

            def normalise(r, l):
                n = r * BT + l
                dve.wait_ge(norm_in, (n + 1) * 2)
                wait(dve, ctx_hi, n - 1)
                wait(dve, ctx_lo, n - 1)
                nc.vector.tensor_tensor(c32[:, l % 2, :].rearrange("p (h d) -> p h d", h=GQ), num[:],
                                        rden[:].broadcast_to([P, GQ, DH]), ALU.mult).then_inc(norm_done, 1)

            def block_max(r, m):
                l = tile_of(m)
                dve.wait_ge(m_mm, r * BB + m + 1)
                if m == base(l):
                    wait(dve, m_all, r * BT + l - 1)
                nc.vector.tensor_reduce(mpart[:, l % 2, :, key_tile(m)],
                                        M[m % 2][:].rearrange("p (h c) -> p h c", h=GQ),
                                        AX.X, ALU.max).then_inc(m_red, 1)

            def tile_max(r, l):
                dve.wait_ge(m_red, r * BB + base(l + 1))
                wait(dve, maug_ready, r * BT + l - 1)
                nc.vector.tensor_reduce(negm[:, l % 2, :], mpart[:, l % 2, :, 0:l % UT + 1],
                                        AX.X, ALU.max, negate=True).then_inc(m_all, 1)

            def max_hi(r, l):
                n = r * BT + l
                dve.wait_ge(m_all, n + 1)
                wait(dve, rows_t, n - 1)
                nc.vector.tensor_scalar(maug[:, l % 2, :, 0], negm[:, l % 2, :], 1.0 / MS, None, ALU.mult)\
                    .then_inc(maug_hi, 1)

            def max_lo(r, l):
                n = r * BT + l
                dve.wait_ge(maug_hi, n + 1)
                nc.vector.scalar_tensor_tensor(maug[:, l % 2, :, 1], negm[:, l % 2, :], 1.0 / MS,
                                               maug[:, l % 2, :, 0], ALU.mult, ALU.subtract)\
                    .then_inc(maug_ready, 1)

            def p_low(r, s):
                dve.wait_ge(hi_act, r * (BB // 2) + s // 2 + 1)
                wait(dve, av_done, r * BB + s + 1 - RING)
                nc.vector.tensor_tensor(plo[:, s % RING, :], p32[:, s % RING, :], phi[:, s % RING, :],
                                        ALU.subtract).then_inc(lo_dve, 1)

            def p_high(r, s):
                l = tile_of(s)
                dve.wait_ge(exp_done, r * BB + s + 1)
                if s == base(l):
                    dve.wait_ge(mask_done, r * BT + l + 1)
                wait(dve, av_done, r * BB + s + 1 - RING)
                nc.vector.tensor_copy(phi[:, s % RING, :], p32[:, s % RING, :]).then_inc(hi_dve, 1)

            def position(r, s):
                done = last_of(s, NORM_LAG)
                done = done if done is not None and has_tile(r, done) else None
                if done is not None:
                    context_sums(r, done)
                m = s - 1 + MAX_LEAD
                if has_block(r, m):
                    block_max(r, m)
                if done is not None:
                    normalise(r, done)
                maxed = last_of(m, 0) if has_block(r, m) else None
                if maxed is not None:
                    tile_max(r, maxed)
                if has_block(r, s - 2) and s % 2 == 0:
                    p_low(r, s - 2)
                if maxed is not None:
                    max_hi(r, maxed)
                if has_block(r, s - 1) and s % 2 == 0:
                    p_high(r, s - 1)
                for l in tiles_with(s, 0):
                    if has_tile(r, l):
                        n = r * BT + l
                        dve.wait_ge(p_evac, n + 1)
                        wait(dve, av_done, r * BB + 36 * (l // UT - 1))
                        v32, va = qkv[:, l % 2, WCOL - DH:WCOL], vaug[:, (l // UT) % 2, l % UT, :]
                        nc.vector.tensor_copy(va[:, 32:64], v32).then_inc(v_hi, 1)
                if maxed is not None:
                    max_lo(r, maxed)
                for l in tiles_with(s, 0):
                    if has_tile(r, l):
                        dve.wait_ge(v_hi, r * BT + l + 1)
                        nc.vector.tensor_tensor(va[:, 0:32], v32, va[:, 32:64], ALU.subtract).then_inc(v_ready, 1)
                q = weights_change(s - 1)
                if q is not None and has_tile(r, q * BT):
                    split_w(r + q)

            positions(dve, position)

        @block.gpsimd
        def _(pool):
            nc.gpsimd.memset(kst[96:98, :, :], MS).then_inc(const_ok, 1)
            pool.wait_ge(const_ok, 1)
            nc.gpsimd.memset(vaug[:, :, :, 64:65], 1.0).then_inc(const_ok, 1)
            pool.wait_ge(rope_in, 16)

            def rotate(r, l):
                n = r * BT + l
                k, j = l % 2, l % UT
                pool.wait_ge(p_evac, n + 1)
                wait(pool, rope_done, n)
                wait(pool, nat_ready, n - 1)
                x = qkv[:, k, 0:(GQ + 1) * DH].rearrange("p (h d) -> p h d", d=DH)
                bc = lambda t, w: t[:, None, :].broadcast_to([P, GQ + 1, w])
                H = DH // 2
                nc.gpsimd.tensor_tensor(t1[:], x, bc(rope[:, 0, j, :], DH), ALU.mult)
                nc.gpsimd.tensor_tensor(t2[:, :, 0:H], x[:, :, H:DH], bc(rope[:, 1, j, 0:H], H), ALU.mult)
                nc.gpsimd.tensor_tensor(t2[:, :, H:DH], x[:, :, 0:H], bc(rope[:, 1, j, H:DH], H), ALU.mult)\
                    .then_inc(rope_st, 1)
                pool.wait_ge(rope_st, n + 1)
                nc.gpsimd.tensor_tensor(rot[:, k, :, :], t1[:], t2[:], ALU.add).then_inc(rope_done, 1)

            def position(r, s):
                l = tile_of(s)
                if has_block(r, s) and s == base(l):
                    pool.wait_ge(exp_done, r * BB + s + 1)
                    apart(pool, apart_pool)
                    d = p32[:, s % RING, :].rearrange("p (h q) -> p h q", h=GQ)
                    nc.gpsimd.affine_select(out=d, in_=d, compare_op=ALU.is_ge, fill=0.0, base=0,
                                            pattern=[[0, GQ], [1, P]], channel_multiplier=-1)\
                        .then_inc(mask_done, 1)
                for l in tiles_with(s, 0):
                    if has_tile(r, l):
                        rotate(r, l)
                if has_block(r, s - 1) and (s - 1) % 2 == 1:
                    k = (s - 1) % RING
                    pool.wait_ge(hi_dve, r * (BB // 2) + (s - 1) // 2 + 1)
                    wait(pool, av_done, r * BB + s - RING)
                    nc.gpsimd.tensor_tensor(plo[:, k, :], p32[:, k, :], phi[:, k, :], ALU.subtract)\
                        .then_inc(lo_pool, 1)
                l = last_of(s, LO_LAG)
                if l is not None and has_tile(r, l):
                    pool.wait_ge(ctx_hi, r * BT + l + 1)
                    nc.gpsimd.tensor_tensor(chl[:, l % 2, 1, :], c32[:, l % 2, :], chl[:, l % 2, 0, :],
                                            ALU.subtract).then_inc(ctx_lo, 1)
                for l in tiles_with(s, NAT_LO):
                    if has_tile(r, l):
                        pool.wait_ge(nat_hi, r * BT + l + 1)
                        k = l % 2
                        nc.gpsimd.tensor_tensor(nat[:, k, 0:GQ, DH:2 * DH], rot[:, k, 0:GQ, :],
                                                nat[:, k, 0:GQ, 0:DH], ALU.subtract)
                        nc.gpsimd.tensor_tensor(nat[:, k, GQ, 2 * DH:3 * DH], rot[:, k, GQ, :],
                                                nat[:, k, GQ, 0:DH], ALU.subtract).then_inc(nat_ready, 1)

            positions(pool, position)


def phase_output(nc, K, x, x1_dram):
    with ExitStack() as ctx:
        sb = lambda n, s, d: ctx.enter_context(nc.sbuf_tensor("c_" + n, s, d))
        ps = lambda n, s, d: ctx.enter_context(nc.psum_tensor("c_" + n, s, d))
        sem = lambda n: ctx.enter_context(nc.semaphore("c_" + n))
        wohl = sb("wohl", [P, 2, NC, E], F16)
        xin = sb("xin", [P, 2, E], F32)
        z = sb("z", [P, E], F32)
        x1 = sb("x1", [P, 2, E], F32)
        xhl = sb("xhl", [P, 2, 2, E], F16)
        st6 = sb("st6", [P, 2, 6], F32)
        mv = sb("mv", [P, 2], F32)
        ve = sb("ve", [P, 1], F32)
        sd = sb("sd", [P, 1], F32)
        rs = sb("rs", [P, 1], F32)
        Y = [ps(f"y{i}", [P, E], F32) for i in range(2)]
        PT = [[ps(f"pt{s}{h}", [P, NC, P], F16) for h in range(2)] for s in range(2)]
        w_hi, w_lo = sem("w_hi"), sem("w_lo")
        x_in = [sem("x_in0"), sem("x_in1")]
        x1_out = [sem("x1_out0"), sem("x1_out1")]
        y_mm, chain = sem("y_mm"), sem("chain")
        var_ok, std_ok = sem("var"), sem("std")
        x1_ok, xn_ok, hi_ok, lo_ok = sem("x1_ok"), sem("xn"), sem("hi"), sem("lo")
        apart_dve = sem("apart")
        tr, ev_hi, ev_lo = sem("tr"), sem("ev_hi"), sem("ev_lo")
        xv = x.rearrange("(n p) e -> n p e", p=P)
        x1v = x1_dram.rearrange("(n p) e -> n p e", p=P)
        LINKS = 14
        block = ctx.enter_context(nc.Block())

        def pair(eng, tile):
            def body(r):
                tile(r * 2, 0, r)
                tile(r * 2 + 1, 1, r)
            loop(eng, 0, NT // 2 - 1, body)

        @block.sync
        def _(sp):
            def tile(n, k, r):
                wait(sp, x1_ok, n - 1)
                sp.dma_start(xin[:, k, :], xv[bass.ds(n, 1)].rearrange("a p e -> p (a e)")).then_inc(x_in[k], 16)
                if isinstance(n, int) and n == 0:
                    return
                store(n - 1, 1 - k)

            def store(n, k):
                sp.wait_ge(x1_ok, n + 1)
                sp.dma_start(x1v[bass.ds(n, 1)].rearrange("a p e -> p (a e)"), x1[:, k, :]).then_inc(x1_out[k], 16)

            pair(sp, tile)
            store(NT - 1, 1)
            for k in range(2):
                sp.wait_ge(x1_out[k], 16 * NT // 2)

        @block.scalar
        def _(act):
            for c in range(NC):
                nc.scalar.activation(wohl[:, 0, c, :], K.wo_raw[:, c, :], ACT.Copy, scale=K.sc[:, SO:SO + 1])\
                    .then_inc(w_hi, 1)

            def copy_out(n, k):
                act.wait_ge(tr, n * 2 + 1)
                nc.scalar.activation(K.xT[:, 0, :, bass.ds(n * P, P)], PT[k][0][:], ACT.Copy).then_inc(ev_hi, 1)

            def tile(n, k, r):
                act.wait_ge(var_ok, n * 2 + 1)
                nc.scalar.activation(sd[:], ve[:], ACT.Sqrt).then_inc(std_ok, 1)
                act.wait_ge(var_ok, n * 2 + 2)
                nc.scalar.activation(sd[:], ve[:], ACT.Sqrt, scale=XS ** -2).then_inc(std_ok, 1)
                act.wait_ge(xn_ok, n + 1)
                wait(act, tr, n * 2 - 2)
                nc.scalar.activation(xhl[:, k, 0, :], z[:], ACT.Copy).then_inc(hi_ok, 1)
                if not (isinstance(n, int) and n == 0):
                    copy_out(n - 1, 1 - k)

            pair(act, tile)
            copy_out(NT - 1, 1)

        @block.tensor
        def _(pe):
            def transposes(n, k):
                for h, ready, out in ((0, hi_ok, ev_hi), (1, lo_ok, ev_lo)):
                    pe.wait_ge(ready, n + 1)
                    wait(pe, out, n - 1)
                    for c in range(NC):
                        j0 = c % 4 * 2 * P + c // 4
                        last = nc.tensor.transpose(PT[k][h][:, c, :], xhl[:, k, h, j0:j0 + 2 * P - 1:2], K.ident[:])
                    last.then_inc(tr, 1)

            def tile(n, k, r):
                wait(pe, chain, (n - 1) * LINKS - 7)
                for c in range(NC):
                    if isinstance(n, int) and n == 0:
                        pe.wait_ge(w_lo, c + 1)
                    for a, b in ((0, 0), (0, 1), (1, 0)):
                        for h in range(2):
                            last = nc.tensor.matmul(Y[k][:, h * 512:(h + 1) * 512],
                                                    K.ctxT[:, a, c, bass.ds(n * P, P)],
                                                    wohl[:, b, c, h * 512:(h + 1) * 512],
                                                    start=(c == 0 and a == b), stop=(c == NC - 1 and a == 1))
                last.then_inc(y_mm, 1)
                if not (isinstance(n, int) and n == 0):
                    transposes(n - 1, 1 - k)

            pair(pe, tile)
            transposes(NT - 1, 1)

        @block.vector
        def _(dve):
            for c in range(NC):
                dve.wait_ge(w_hi, c + 1)
                nc.vector.scalar_tensor_tensor(wohl[:, 1, c, :], K.wo_raw[:, c, :], K.sc[:, SO:SO + 1],
                                               wohl[:, 0, c, :], ALU.mult, ALU.subtract).then_inc(w_lo, 1)

            def copy_out(n, k):
                dve.wait_ge(tr, n * 2 + 2)
                nc.vector.tensor_copy(K.xT[:, 1, :, bass.ds(n * P, P)], PT[k][1][:]).then_inc(ev_lo, 1)

            def tile(n, k, r):
                links = [0]

                def link(ins):
                    links[0] += 1
                    ins.then_inc(chain, 1)
                    dve.wait_ge(chain, n * LINKS + links[0])

                def stats(src):
                    for h in range(2):
                        last = nc.vector.bn_stats(st6[:, h, :], src[:, h * 512:(h + 1) * 512])
                    link(last)
                    apart(dve, apart_dve)
                    link(nc.vector.bn_aggr(mv[:], st6[:]))

                dve.wait_ge(y_mm, n + 1)
                stats(Y[k])
                link(nc.vector.tensor_scalar(ve[:], mv[:, 1:2], K.k_att[:], K.k_att[:], ALU.mult, ALU.mult))
                link(nc.vector.tensor_scalar(ve[:], ve[:], EPS, None, ALU.add))
                dve.sem_inc(var_ok, 1)
                dve.wait_ge(std_ok, n * 2 + 1)
                link(nc.vector.reciprocal(rs[:], sd[:]))
                link(nc.vector.tensor_scalar(rs[:], rs[:], K.k_att[:], None, ALU.mult))
                wait(dve, hi_ok, n)
                link(nc.vector.tensor_scalar(z[:], Y[k][:], mv[:, 0:1], rs[:], ALU.subtract, ALU.mult))
                dve.wait_ge(x_in[k], r * 16 + 16)
                wait(dve, x1_out[k], r * 16)
                link(nc.vector.tensor_tensor(x1[:, k, :], z[:], xin[:, k, :], ALU.add))
                dve.sem_inc(x1_ok, 1)
                stats(x1[:, k, :])
                link(nc.vector.tensor_scalar(ve[:], mv[:, 1:2], EPS, None, ALU.add))
                dve.sem_inc(var_ok, 1)
                dve.wait_ge(std_ok, n * 2 + 2)
                link(nc.vector.reciprocal(rs[:], sd[:]))
                link(nc.vector.tensor_scalar(z[:], x1[:, k, :], mv[:, 0:1], rs[:], ALU.subtract, ALU.mult))
                dve.sem_inc(xn_ok, 1)
                if not (isinstance(n, int) and n == 0):
                    copy_out(n - 1, 1 - k)
                dve.wait_ge(hi_ok, n + 1)
                link(nc.vector.tensor_tensor(xhl[:, k, 1, :], z[:], xhl[:, k, 0, :], ALU.subtract))
                dve.sem_inc(lo_ok, 1)
                assert links[0] == LINKS

            pair(dve, tile)
            copy_out(NT - 1, 1)


def phase_ffn(nc, K, gu_q, gu_sz, down_q, down_sz, x1_dram, out):
    with ExitStack() as ctx:
        sb = lambda n, s, d: ctx.enter_context(nc.sbuf_tensor("d_" + n, s, d))
        ps = lambda n, s, d: ctx.enter_context(nc.psum_tensor("d_" + n, s, d))
        sem = lambda n: ctx.enter_context(nc.semaphore("d_" + n))
        y = sb("y", [P, NT, E], F32)
        wgu = [sb(f"wgu{c}", [P, 2, NC, 2, P], F16) for c in range(2)]
        wd = sb("wd", [P, 2, 2, E], F16)
        gq = sb("gq", [P, 4, 2 * P], I32)
        gsz = sb("gsz", [P, 4, 4 * P], F32)
        dq = sb("dq", [P, E], I32)
        dsz = sb("dsz", [P, 2, E], F32)
        nib = sb("nib", [P, 512], I32)
        wf = sb("wf", [P, 512], F32)
        hT = sb("hT", [P, 2, 2, TOK], F16)
        sil = sb("sil", [P, 2, 512], F32)
        h32 = sb("h32", [P, 2, 512], F32)
        st6 = sb("st6", [P, 2, 2, 6], F32)
        mv = sb("mv", [P, 2, 2], F32)
        ve = sb("ve", [P, 2], F32)
        sd = sb("sd", [P, 2], F32)
        rs = sb("rs", [P, 2], F32)
        nb = sb("nb", [P, 2], F32)
        x1 = gsz[:].rearrange("p a b -> p (a b)").rearrange("p (k e) -> p k e", k=2)
        z = dsz
        GP = [ps(f"g{i}", [P, 512], F32) for i in range(2)]
        UP = [ps(f"u{i}", [P, 512], F32) for i in range(2)]
        D = [ps(f"d{i}", [P, E], F32) for i in range(2)]
        gq_in, gsz_in, dq_in, dsz_in = sem("gq_in"), sem("gsz_in"), sem("dq_in"), sem("dsz_in")
        g_unpacked, g_scaled, d_unpacked, d_scaled = sem("g_unp"), sem("g_scl"), sem("d_unp"), sem("d_scl")
        w_sub, w_step, w_hi, w_lo = sem("w_sub"), sem("w_step"), sem("w_hi"), sem("w_lo")
        gu_mm, silu_ok, h_ok, h_hi, h_lo = sem("gu_mm"), sem("silu"), sem("h_ok"), sem("h_hi"), sem("h_lo")
        d_mm, y_ok = sem("d_mm"), sem("y_ok")
        x1_in = [sem("x1_in0"), sem("x1_in1")]
        st_ok, mv_ok, rs_ok = sem("st_ok"), sem("mv_ok"), sem("rs_ok")
        var_ok, std_ok, z_ok, o_ok = sem("var"), sem("std"), sem("z_ok"), sem("o_ok")
        nb_ok = sem("nb_ok")
        o_out = [sem("o_out0"), sem("o_out1")]
        x1v = x1_dram.rearrange("(n p) e -> n p e", p=P)
        outv = out.rearrange("(n p) e -> n p e", p=P)
        LAST = GROUPS
        width = lambda g: LASTW if isinstance(g, int) and g == LAST else P
        block = ctx.enter_context(nc.Block())

        def groups(eng, body):
            body(0)
            with eng.Fori(1, LAST - 1) as g:
                body(g)
            body(LAST - 1)
            body(LAST)


        @block.sync
        def _(sp):
            def load_chunk(g, c):
                w = width(g)
                i = g * 2 + c
                o = g * (4 * P) + c * 2 * w
                wait(sp, g_unpacked, i * 4)
                sp.dma_start(gq[:, :, 0:2 * w], gu_q.rearrange("(j p) n -> p j n", p=P)[:, :, bass.ds(o, 2 * w)])\
                    .then_inc(gq_in, 16)
                wait(sp, g_scaled, i * 4)
                for q in range(4):
                    src = gu_sz.rearrange("(j q) n -> q j n", q=4)[q, :, bass.ds(g * (8 * P) + c * 4 * w, 4 * w)]
                    sp.dma_start(gsz[q * 32:(q + 1) * 32, :, 0:4 * w], src.partition_broadcast(32))\
                        .then_inc(gsz_in, 16)

            def load_down(g):
                w = width(g)
                wait(sp, d_unpacked, g * 4)
                sp.dma_start(dq[0:w, :], down_q[bass.ds(g * P, w), :]).then_inc(dq_in, 16)
                wait(sp, d_scaled, g * 4)
                for q in range(w // 32):
                    src = down_sz[bass.ds(g * 4 + q, 1)].rearrange("a x n -> (a x) n")
                    sp.dma_start(dsz[q * 32:(q + 1) * 32, :, :], src.partition_broadcast(32)).then_inc(dsz_in, 16)

            def body(g):
                load_chunk(g, 0)
                load_chunk(g, 1)
                load_down(g)
            groups(sp, body)
            sp.wait_ge(w_lo, 12 * (LAST + 1))
            for t in range(NT):
                wait(sp, o_ok, t - 1)
                sp.dma_start(x1[:, t % 2, :], x1v[t]).then_inc(x1_in[t % 2], 16)
                if t:
                    sp.wait_ge(o_ok, t)
                    sp.dma_start(outv[t - 1], z[:, (t - 1) % 2, :]).then_inc(o_out[(t - 1) % 2], 16)
            sp.wait_ge(o_ok, NT)
            sp.dma_start(outv[NT - 1], z[:, 1, :]).then_inc(o_out[1], 16)
            for k in range(2):
                sp.wait_ge(o_out[k], 16 * NT // 2)

        def split_target(g, kind, k):
            w = width(g)
            if kind == 2:
                dst = [wd[0:w, x, k // 2, k % 2 * 512:(k % 2 + 1) * 512] for x in range(2)]
                return dst, wf[0:w, :], K.sc[0:w, SD:SD + 1]
            n = k // 2 * 4
            m = SG + k % 2
            dst = [wgu[kind][:, x, n:n + 4, k % 2, 0:w] for x in range(2)]
            return dst, wf[:, 0:4 * w].rearrange("p (j i) -> p j i", j=4), K.sc[:, m:m + 1]

        @block.scalar
        def _(act):
            def item(g, kind, k):
                n = g * 12 + kind * 4 + k
                act.wait_ge(w_step, n + 1)
                (hi, _), src, scale = split_target(g, kind, k)
                nc.scalar.activation(hi, src, ACT.Copy, scale=scale).then_inc(w_hi, 1)

            def items_beside(g, b):
                if isinstance(g, int) and g == 0:
                    for k in (2 * b, 2 * b + 1):
                        item(0, 1 + k // 4, k % 4)
                else:
                    item(g, 2, b)

            def gate(g, c, b):
                w, e = width(g), g * 8 + c * 4 + b
                act.wait_ge(gu_mm, e + 1)
                wait(act, h_ok, e - 1)
                nc.scalar.activation(sil[0:w, b % 2, :], GP[b % 2][0:w, :], ACT.Silu, scale=K.k_gate[0:w, :])\
                    .then_inc(silu_ok, 1)
                act.wait_ge(h_ok, e + 1)
                wait(act, d_mm, g * NT)
                nc.scalar.activation(hT[0:w, 0, c, b * 512:(b + 1) * 512], h32[0:w, b % 2, :], ACT.Copy)\
                    .then_inc(h_hi, 1)

            for k in range(4):
                item(0, 0, k)

            def body(g):
                last = isinstance(g, int) and g == LAST
                for b in range(4):
                    gate(g, 0, b)
                    items_beside(g, b)
                for b in range(4):
                    gate(g, 1, b)
                    if not last:
                        item(g + 1, 0, b)
                if not last:
                    for k in range(4):
                        item(g + 1, 1, k)
            def scale_rows(t):
                k = t % 2
                act.wait_ge(nb_ok, t + 1)
                wait(act, o_out[k], t // 2 * 16)
                nc.scalar.activation(z[:, k, :], y[:, t, :], ACT.Identity, bias=nb[:, k:k + 1],
                                     scale=rs[:, k:k + 1]).then_inc(z_ok, 1)

            groups(act, body)
            for t in range(NT):
                act.wait_ge(var_ok, t + 1)
                nc.scalar.activation(sd[:, t % 2:t % 2 + 1], ve[:, t % 2:t % 2 + 1], ACT.Sqrt, bias=EPS).then_inc(std_ok, 1)
                if t:
                    scale_rows(t - 1)
            scale_rows(NT - 1)

        @block.tensor
        def _(pe):
            def body(g):
                w = width(g)
                for c in range(2):
                    for b in range(4):
                        e = g * 8 + c * 4 + b
                        wait(pe, silu_ok, e - 1)
                        wait(pe, h_ok, e - 1)
                        for k in range(4):
                            m, out_bank = k % 2, (GP, UP)[k % 2][b % 2]
                            if b == 0:
                                pe.wait_ge(w_lo, g * 12 + c * 4 + k + 1)
                            for kc in range(k // 2 * 4, k // 2 * 4 + 4):
                                for a, x in ((0, 0), (0, 1), (1, 0)):
                                    last = nc.tensor.matmul(out_bank[0:w, :], wgu[c][:, a, kc, m, 0:w],
                                                            K.xT[:, x, kc, b * 512:(b + 1) * 512],
                                                            start=(kc == 0 and a == x), stop=(kc == NC - 1 and a == 1))
                        last.then_inc(gu_mm, 1)
                pe.wait_ge(w_lo, g * 12 + 12)
                for t in range(NT):
                    pe.wait_ge(h_lo, g * 8 + 4 + t // 4 + 1)
                    wait(pe, y_ok, g * NT + t - 1)
                    for c in range(2):
                        for a, b in ((0, 0), (0, 1), (1, 0)):
                            for h in range(2):
                                last = nc.tensor.matmul(D[t % 2][:, h * 512:(h + 1) * 512],
                                                        hT[0:w, a, c, t * P:(t + 1) * P],
                                                        wd[0:w, b, c, h * 512:(h + 1) * 512],
                                                        start=(c == 0 and a == b), stop=(c == 1 and a == 1))
                    last.then_inc(d_mm, 1)
            groups(pe, body)

        @block.vector
        def _(dve):
            def item(g, kind, k, parts=range(4)):
                w, n = width(g), g * 12 + kind * 4 + k
                (hi, lo), src, scale = split_target(g, kind, k)
                if kind == 2:
                    raw, nb = dq[0:w, k % 2 * 512:(k % 2 + 1) * 512], nib[0:w, :]
                    s, zero = (dsz[0:w, x, k % 2 * 512:(k % 2 + 1) * 512] for x in range(2))
                    unpacked, scaled, count = d_unpacked, d_scaled, g * 4 + k + 1
                else:
                    raw = gq[:, :, k % 2 * w:(k % 2 + 1) * w]
                    nb = nib[:, 0:4 * w].rearrange("p (j i) -> p j i", j=4)
                    s, zero = (gsz[:, :, (k % 2 * 2 + x) * w:(k % 2 * 2 + x + 1) * w] for x in range(2))
                    unpacked, scaled, count = g_unpacked, g_scaled, (g * 2 + kind) * 4 + k + 1
                if 0 in parts:
                    wait(dve, w_lo, n)
                    if kind == 2:
                        dve.wait_ge(dq_in, g * 16 + 16)
                    else:
                        dve.wait_ge(gq_in, (g * 2 + kind + 1) * 16)
                    if k // 2 == 0:
                        ins = nc.vector.tensor_scalar(nb, raw, 4, 15, ALU.logical_shift_right, ALU.bitwise_and)
                    else:
                        ins = nc.vector.tensor_scalar(nb, raw, 15, None, ALU.bitwise_and)
                    ins.then_inc(unpacked, 1)
                if 1 in parts:
                    dve.wait_ge(unpacked, count)
                    if kind != 2:
                        dve.wait_ge(gsz_in, (g * 2 + kind + 1) * 64)
                    elif width(g) == P:
                        dve.wait_ge(dsz_in, g * 64 + 64)
                    else:
                        dve.wait_ge(dsz_in, LAST * 64 + LASTW // 32 * 16)
                    nc.vector.tensor_tensor(src, nb, zero, ALU.subtract).then_inc(w_sub, 1)
                if 2 in parts:
                    dve.wait_ge(w_sub, n + 1)
                    nc.vector.tensor_tensor(src, src, s, ALU.mult).then_inc(scaled, 1)
                    dve.wait_ge(scaled, count)
                    if kind == 2:
                        wait(dve, d_mm, g * NT)
                    else:
                        wait(dve, gu_mm, g * 8 + kind * 4 - 4)
                    dve.sem_inc(w_step, 1)
                if 3 in parts:
                    dve.wait_ge(w_hi, n + 1)
                    nc.vector.scalar_tensor_tensor(lo, src, scale, hi, ALU.mult, ALU.subtract).then_inc(w_lo, 1)

            def items_beside(g, b):
                if isinstance(g, int) and g == 0:
                    for k in (2 * b, 2 * b + 1):
                        item(0, 1 + k // 4, k % 4)
                else:
                    item(g, 2, b)

            def gated(g, c, b):
                w, e = width(g), g * 8 + c * 4 + b
                dve.wait_ge(silu_ok, e + 1)
                wait(dve, h_hi, e - 1)
                wait(dve, h_lo, e - 1)
                nc.vector.scalar_tensor_tensor(h32[0:w, b % 2, :], sil[0:w, b % 2, :], K.k_h[0:w, :],
                                               UP[b % 2][0:w, :], ALU.mult, ALU.mult).then_inc(h_ok, 1)

            def gated_low(g, c, b):
                w, e = width(g), g * 8 + c * 4 + b
                dve.wait_ge(h_hi, e + 1)
                cols = slice(b * 512, (b + 1) * 512)
                nc.vector.tensor_tensor(hT[0:w, 1, c, cols], h32[0:w, b % 2, :], hT[0:w, 0, c, cols],
                                        ALU.subtract).then_inc(h_lo, 1)

            def gather(g, t):
                dve.wait_ge(d_mm, g * NT + t + 1)
                if isinstance(g, int) and g == 0:
                    nc.vector.tensor_copy(y[:, t, :], D[t % 2][:]).then_inc(y_ok, 1)
                else:
                    wait(dve, y_ok, g * NT + t - (NT - 1))
                    nc.vector.tensor_tensor(y[:, t, :], y[:, t, :], D[t % 2][:], ALU.add).then_inc(y_ok, 1)

            for k in range(4):
                item(0, 0, k)

            def body(g):
                last = isinstance(g, int) and g == LAST
                for b in range(4):
                    gated(g, 0, b)
                    items_beside(g, b)
                    gated_low(g, 0, b)
                for b in range(4):
                    gated(g, 1, b)
                    if not last:
                        item(g + 1, 0, b)
                    gated_low(g, 1, b)
                for t in range(NT):
                    gather(g, t)
                    if not last:
                        item(g + 1, 1, t // 4, parts=(t % 4,))
                    if last:
                        last_norm(t)

            def last_norm(t):
                k, j = t % 2, (t - 1) % 2
                if t:
                    dve.wait_ge(std_ok, t)
                    wait(dve, z_ok, t - 2)
                    nc.vector.reciprocal(rs[:, j:j + 1], sd[:, j:j + 1]).then_inc(rs_ok, 1)
                if t < NT:
                    dve.wait_ge(y_ok, LAST * NT + t + 1)
                    nc.vector.bn_stats(st6[:, k, 0, :], y[:, t, 0:512]).then_inc(st_ok, 1)
                if t:
                    dve.wait_ge(rs_ok, 2 * t - 1)
                    nc.vector.tensor_scalar(rs[:, j:j + 1], rs[:, j:j + 1], K.k_y[:], None, ALU.mult)\
                        .then_inc(rs_ok, 1)
                if t < NT:
                    nc.vector.bn_stats(st6[:, k, 1, :], y[:, t, 512:1024]).then_inc(st_ok, 1)
                if t:
                    dve.wait_ge(rs_ok, 2 * t)
                    nc.vector.scalar_tensor_tensor(nb[:, j:j + 1], mv[:, j, 0:1], -1.0, rs[:, j:j + 1],
                                                   ALU.mult, ALU.mult).then_inc(nb_ok, 1)
                if t < NT:
                    dve.wait_ge(st_ok, 2 * t + 2)
                    nc.vector.bn_aggr(mv[:, k, :], st6[:, k, :, :]).then_inc(mv_ok, 1)
                    dve.wait_ge(mv_ok, t + 1)
                    wait(dve, std_ok, t - 1)
                    nc.vector.tensor_scalar(ve[:, k:k + 1], mv[:, k, 1:2], K.k_y[:], K.k_y[:],
                                            ALU.mult, ALU.mult).then_inc(var_ok, 1)

            groups(dve, body)
            last_norm(NT)

        @block.gpsimd
        def _(pool):
            for t in range(NT):
                k = t % 2
                pool.wait_ge(z_ok, t + 1)
                pool.wait_ge(x1_in[k], t // 2 * 16 + 16)
                nc.gpsimd.tensor_tensor(z[:, k, :], z[:, k, :], x1[:, k, :], ALU.add).then_inc(o_ok, 1)


class Shared:
    pass


def build(nc, x, wqkv, wo, szs, gu_q, gu_sz, down_q, down_sz, ropes, x1_dram, out):
    K = Shared()
    with ExitStack() as ctx:
        sb = lambda n, s, d: ctx.enter_context(nc.sbuf_tensor(n, s, d))
        K.ident = sb("ident", [P, P], F16)
        K.identb = sb("identb", [P, P], BF16)
        K.maskb = sb("maskb", [P, P], BF16)
        K.sc = sb("sc", [P, 8], F32)
        K.inv = sb("inv", [P, 8], F32)
        K.k_score, K.k_att, K.k_y, K.k_gate, K.k_h = (sb(n, [P, 1], F32) for n in
                                                      ("k_score", "k_att", "k_y", "k_gate", "k_h"))
        K.xT = sb("xT", [P, 2, NC, TOK], F16)
        K.wo_raw = K.xT[:, 0, :, :].bitcast(F32)
        with nc.sbuf_tensor("wraw", [P, NC, WCOL], F32) as wraw:
            K.wraw = wraw
            phase_scales_and_norm(nc, K, x, wqkv, wo, szs)
            with nc.sbuf_tensor("ctxT", [P, 2, NC, TOK], F16) as ctxT:
                K.ctxT = ctxT
                phase_attention(nc, K, wqkv, ropes, wo)
                phase_output(nc, K, x, x1_dram)
        phase_ffn(nc, K, gu_q, gu_sz, down_q, down_sz, x1_dram, out)


def rope_tables():
    f = np.float32
    inv = (f(1.0) / np.power(f(500000.0), np.arange(0, DH, 2, dtype=f) / f(DH))).astype(f)
    wavelen = (f(2.0 * np.pi) / inv).astype(f)
    scaled = np.where(wavelen > f(2048), inv / f(32.0), inv).astype(f)
    smooth = ((f(2048) / wavelen - f(1.0)) / f(3.0)).astype(f)
    smoothed = ((f(1.0) - smooth) * scaled / f(32.0) + smooth * scaled).astype(f)
    scaled = np.where(~(wavelen < 2048) & ~(wavelen > 512), smoothed, scaled).astype(f)
    ang = (np.arange(T, dtype=f)[:, None] * scaled[None]).astype(f)
    cos, sin = np.cos(ang), np.sin(ang)
    full = np.stack([np.concatenate([cos, cos], 1), np.concatenate([-sin, sin], 1)])
    return np.ascontiguousarray(full.reshape(2, UT, P, DH).transpose(2, 0, 1, 3)).astype(f)


def chunked():
    starts = range(0, INTER, GROUP_I)
    return [np.arange(s + c, min(s + GROUP_I, INTER), 2) for s in starts for c in range(2)]


def kernel(**inputs):
    import concourse.bacc as _bacc
    from concourse.bass_utils import run_bass_kernel_spmd as _run

    a = {k[3:]: np.asarray(v) for k, v in inputs.items()}
    kv = lambda w, n: w.reshape(KVH, n * DH, E)
    w = np.concatenate([kv(a["attn_Wq"], GQ), kv(a["attn_Wk"], 1), kv(a["attn_Wv"], 1)], 1)
    wqkv = w.reshape(KVH, WCOL, NC, P).transpose(0, 3, 2, 1)
    wo = a["attn_Wo"].T.reshape(NC, P, E).transpose(1, 0, 2).reshape(P, NC * E)
    order = chunked()
    gu_q = np.concatenate([a["ffn_" + m + "_Wq"][i].T for i in order for m in ("gate", "up")], 1)
    gu_sz = np.concatenate([a["ffn_" + m][i].T for i in order
                            for m in ("gate_scale", "gate_zero", "up_scale", "up_zero")], 1)
    down_sz = np.stack([a["ffn_down_scale"].T, a["ffn_down_zero"].T], 1)
    arrays = {
        "x": a["attn_x"].reshape(TOK, E), "wqkv": wqkv, "wo": wo, "gu_q": gu_q, "gu_sz": gu_sz,
        "down_q": a["ffn_down_Wq"].T, "down_sz": down_sz, "ropes": rope_tables(),
    }
    for m in ("gate", "up", "down"):
        for s in ("scale", "zero"):
            arrays[f"{m}_{s}"] = a[f"ffn_{m}_{s}"].reshape(P, -1)
    arrays = {"in_" + k: np.ascontiguousarray(v) for k, v in arrays.items()}

    nc = _bacc.Bacc("TRN2", target_bir_lowering=False, num_devices=1)
    d = {k[3:]: nc.dram_tensor(k, v.shape, mybir.dt.from_np(v.dtype), kind="ExternalInput").ap()
         for k, v in arrays.items()}
    x1 = nc.dram_tensor("x1_rows", (TOK, E), F32, kind="Internal").ap()
    out = nc.dram_tensor("out_rows", (TOK, E), F32, kind="ExternalOutput").ap()
    szs = [d[f"{m}_{s}"] for m in ("gate", "up", "down") for s in ("scale", "zero")]
    build(nc, d["x"], d["wqkv"], d["wo"], szs, d["gu_q"], d["gu_sz"], d["down_q"], d["down_sz"], d["ropes"], x1, out)
    r = _run(nc, [arrays], core_ids=[0])
    return r.results[0]["out_rows"].reshape(BATCH, T, E)
```
